# Optimizing a Trainium2 kernel written in Bass

```python
import numpy as np
import jax
import jax.numpy as jnp

def _softmax(x, axis=-1):
    return jax.nn.softmax(x, axis=axis)

def _gelu(x):
    return jax.nn.gelu(x, approximate=True)

def _silu(x):
    return jax.nn.silu(x)

def _sigmoid(x):
    return jax.nn.sigmoid(x)

def _layernorm(x, axis=-1, eps=1e-05):
    m = jnp.mean(x, axis=axis, keepdims=True)
    v = jnp.var(x, axis=axis, keepdims=True)
    return (x - m) / jnp.sqrt(v + eps)

def _scatter_add(tgt, idx, src, axis=0):
    return tgt.at[idx].add(src)

def _segment_sum(src, seg, n):
    return jax.ops.segment_sum(src, seg, n)
kernel_name = 'mk_recurrent_d2_jaxref_r8_bce96d'

def setup_inputs(seed: int=0):
    np.random.seed(seed)
    _w = jnp.asarray

    def _L0_attn_setup():
        import jax, jax.numpy as jnp
        import numpy as np
        D_MODEL = 128
        N_HEADS = 16
        D_HEAD = D_MODEL // N_HEADS
        RPE_HIDDEN = 32

        def _rpe_bias(T, w1, b1, w2, b2):
            pos = jnp.arange(T, dtype=jnp.float32)
            rel = pos[:, None] - pos[None, :]
            rel = jnp.sign(rel) * jnp.log1p(jnp.abs(rel))
            h = jax.nn.relu(rel[..., None] * w1[0] + b1)
            bias = h @ w2 + b2
            return jnp.transpose(bias, (2, 0, 1))
        key = jax.random.key(seed)
        ks = jax.random.split(key, 8)
        B, T = (2, 256)
        s = lambda fan_in: 1.0 / np.sqrt(fan_in)
        return {'x': jax.random.normal(ks[0], (B, T, D_MODEL), dtype=jnp.float32), 'w_qkv': jax.random.uniform(ks[1], (D_MODEL, 3 * D_MODEL), jnp.float32, -s(D_MODEL), s(D_MODEL)), 'b_qkv': jnp.zeros((3 * D_MODEL,), jnp.float32), 'w_out': jax.random.uniform(ks[2], (D_MODEL, D_MODEL), jnp.float32, -s(D_MODEL), s(D_MODEL)), 'b_out': jnp.zeros((D_MODEL,), jnp.float32), 'w1_rpe': jax.random.uniform(ks[3], (1, RPE_HIDDEN), jnp.float32, -1.0, 1.0), 'b1_rpe': jax.random.uniform(ks[4], (RPE_HIDDEN,), jnp.float32, -1.0, 1.0), 'w2_rpe': jax.random.uniform(ks[5], (RPE_HIDDEN, N_HEADS), jnp.float32, -s(RPE_HIDDEN), s(RPE_HIDDEN)), 'b2_rpe': jnp.zeros((N_HEADS,), jnp.float32)}
    _L0_attn_in = _L0_attn_setup()

    def _L0_ffn_setup():
        import jax, jax.numpy as jnp
        import numpy as np
        ALPHA = 1.702
        LIMIT = 7.0
        TOP_K = 2
        key = jax.random.key(seed)
        ks = jax.random.split(key, 4)
        B, S, H, E, I = (2, 128, 128, 8, 256)
        return {'hidden_states': jax.random.normal(ks[0], (B, S, H), jnp.float32), 'router_weight': jax.random.normal(ks[1], (E, H), jnp.float32), 'router_bias': jnp.zeros((E,), jnp.float32), 'gate_up_proj': jax.random.normal(ks[2], (E, H, 2 * I), jnp.float32) * 0.02, 'gate_up_bias': jnp.zeros((E, 2 * I), jnp.float32), 'down_proj': jax.random.normal(ks[3], (E, I, H), jnp.float32) * 0.02, 'down_bias': jnp.zeros((E, H), jnp.float32)}
    _L0_ffn_in = _L0_ffn_setup()

    def _L1_attn_setup():
        import jax, jax.numpy as jnp
        import numpy as np
        B, S, D, H = (2, 256, 128, 16)
        HD = D // H
        key = jax.random.key(seed)
        ks = jax.random.split(key, 5)
        x = jax.random.normal(ks[0], (B, S, D), dtype=jnp.float32)
        qk_w = jax.random.normal(ks[1], (D, 2 * D), dtype=jnp.float32) * 0.02
        qk_b = jnp.zeros((2 * D,), dtype=jnp.float32)
        v_w = jax.random.normal(ks[2], (D, D), dtype=jnp.float32) * 0.02
        cproj_w = jax.random.normal(ks[3], (D, D), dtype=jnp.float32) * 0.02
        resid_gain = jnp.ones((1, H, 1, 1), dtype=jnp.float32)
        skip_gain = jnp.ones((1, H, 1, 1), dtype=jnp.float32)
        centre_gain = jnp.ones((1, H, 1, 1), dtype=jnp.float32)
        return {'x': x, 'qk_w': qk_w, 'qk_b': qk_b, 'v_w': v_w, 'cproj_w': cproj_w, 'resid_gain': resid_gain, 'skip_gain': skip_gain, 'centre_gain': centre_gain}
    _L1_attn_in = _L1_attn_setup()

    def _L1_ffn_setup():
        import jax, jax.numpy as jnp
        import numpy as np
        key = jax.random.key(seed)
        k1, k2, k3, k4, k5 = jax.random.split(key, 5)
        d_in, d_out, r = (128, 128, 32)
        x = jax.random.normal(k1, (8, 1024, d_in), dtype=jnp.float32)
        W = jax.random.normal(k2, (d_out, d_in), dtype=jnp.float32) * (1.0 / np.sqrt(d_in))
        b = jax.random.normal(k3, (d_out,), dtype=jnp.float32) * 0.01
        V_r = jax.random.normal(k4, (d_in, r), dtype=jnp.float32) * (1.0 / np.sqrt(d_in))
        C = jax.random.normal(k5, (d_out, r), dtype=jnp.float32) * (1.0 / np.sqrt(r))
        return {'x': x, 'W': W, 'b': b, 'V_r': V_r, 'C': C}
    _L1_ffn_in = _L1_ffn_setup()
    _d = {'L0_attn_x': _L0_attn_in['x'], 'L0_attn_w_qkv': _L0_attn_in['w_qkv'], 'L0_attn_b_qkv': _L0_attn_in['b_qkv'], 'L0_attn_w_out': _L0_attn_in['w_out'], 'L0_attn_b_out': _L0_attn_in['b_out'], 'L0_attn_w1_rpe': _L0_attn_in['w1_rpe'], 'L0_attn_b1_rpe': _L0_attn_in['b1_rpe'], 'L0_attn_w2_rpe': _L0_attn_in['w2_rpe'], 'L0_attn_b2_rpe': _L0_attn_in['b2_rpe'], 'L0_ffn_router_weight': _L0_ffn_in['router_weight'], 'L0_ffn_router_bias': _L0_ffn_in['router_bias'], 'L0_ffn_gate_up_proj': _L0_ffn_in['gate_up_proj'], 'L0_ffn_gate_up_bias': _L0_ffn_in['gate_up_bias'], 'L0_ffn_down_proj': _L0_ffn_in['down_proj'], 'L0_ffn_down_bias': _L0_ffn_in['down_bias'], 'L1_attn_qk_w': _L1_attn_in['qk_w'], 'L1_attn_qk_b': _L1_attn_in['qk_b'], 'L1_attn_v_w': _L1_attn_in['v_w'], 'L1_attn_cproj_w': _L1_attn_in['cproj_w'], 'L1_attn_resid_gain': _L1_attn_in['resid_gain'], 'L1_attn_skip_gain': _L1_attn_in['skip_gain'], 'L1_attn_centre_gain': _L1_attn_in['centre_gain'], 'L1_ffn_W': _L1_ffn_in['W'], 'L1_ffn_b': _L1_ffn_in['b'], 'L1_ffn_V_r': _L1_ffn_in['V_r'], 'L1_ffn_C': _L1_ffn_in['C']}
    _x0 = _d['L0_attn_x']
    _d['L0_attn_x'] = jax.random.normal(jax.random.fold_in(jax.random.key(seed), 1), (16, 256, 128), dtype=_x0.dtype)
    del _x0
    return _d

def reference(L0_attn_x, L0_attn_w_qkv, L0_attn_b_qkv, L0_attn_w_out, L0_attn_b_out, L0_attn_w1_rpe, L0_attn_b1_rpe, L0_attn_w2_rpe, L0_attn_b2_rpe, L0_ffn_router_weight, L0_ffn_router_bias, L0_ffn_gate_up_proj, L0_ffn_gate_up_bias, L0_ffn_down_proj, L0_ffn_down_bias, L1_attn_qk_w, L1_attn_qk_b, L1_attn_v_w, L1_attn_cproj_w, L1_attn_resid_gain, L1_attn_skip_gain, L1_attn_centre_gain, L1_ffn_W, L1_ffn_b, L1_ffn_V_r, L1_ffn_C):

    def _L0_attn_ref(x, w_qkv, b_qkv, w_out, b_out, w1_rpe, b1_rpe, w2_rpe, b2_rpe):
        import jax, jax.numpy as jnp
        import numpy as np
        D_MODEL = 128
        N_HEADS = 16
        D_HEAD = D_MODEL // N_HEADS
        RPE_HIDDEN = 32

        def _rpe_bias(T, w1, b1, w2, b2):
            pos = jnp.arange(T, dtype=jnp.float32)
            rel = pos[:, None] - pos[None, :]
            rel = jnp.sign(rel) * jnp.log1p(jnp.abs(rel))
            h = jax.nn.relu(rel[..., None] * w1[0] + b1)
            bias = h @ w2 + b2
            return jnp.transpose(bias, (2, 0, 1))
        B, T, C = x.shape
        qkv = x @ w_qkv + b_qkv
        q, k, v = jnp.split(qkv, 3, axis=-1)

        def heads(t):
            return jnp.transpose(t.reshape(B, T, N_HEADS, D_HEAD), (0, 2, 1, 3))
        q, k, v = (heads(q), heads(k), heads(v))
        scores = jnp.einsum('bhtd,bhsd->bhts', q, k) / np.sqrt(D_HEAD)
        scores = scores + _rpe_bias(T, w1_rpe, b1_rpe, w2_rpe, b2_rpe)[None]
        attn = jax.nn.softmax(scores, axis=-1)
        out = jnp.einsum('bhts,bhsd->bhtd', attn, v)
        out = jnp.transpose(out, (0, 2, 1, 3)).reshape(B, T, C)
        return out @ w_out + b_out

    def _L0_ffn_ref(hidden_states, router_weight, router_bias, gate_up_proj, gate_up_bias, down_proj, down_bias):
        import jax, jax.numpy as jnp
        import numpy as np
        ALPHA = 1.702
        LIMIT = 7.0
        TOP_K = 2
        B, S, H = hidden_states.shape
        E, _, two_I = gate_up_proj.shape
        I = two_I // 2
        flat = hidden_states.reshape(B * S, H)
        logits = flat @ router_weight.T + router_bias
        scores = jax.nn.softmax(logits, axis=-1)
        topk_w, topk_idx = jax.lax.top_k(scores, TOP_K)
        gu = jnp.einsum('th,ehn->ten', flat, gate_up_proj) + gate_up_bias
        gate = jnp.minimum(gu[..., :I], LIMIT)
        up = jnp.clip(gu[..., I:], -LIMIT, LIMIT)
        glu = gate * jax.nn.sigmoid(gate * ALPHA)
        act = (up + 1.0) * glu
        down = jnp.einsum('tei,eih->teh', act, down_proj) + down_bias
        gathered = jnp.take_along_axis(down, topk_idx[:, :, None], axis=1)
        out = (gathered * topk_w[:, :, None]).sum(axis=1)
        return out.reshape(B, S, H)

    def _L1_attn_ref(x, qk_w, qk_b, v_w, cproj_w, resid_gain, skip_gain, centre_gain):
        import jax, jax.numpy as jnp
        import numpy as np
        B, S, D, H = (2, 256, 128, 16)
        HD = D // H
        b, s, d = x.shape
        h, hd = (H, d // H)
        qk = x @ qk_w + qk_b
        q, k = jnp.split(qk, 2, axis=-1)
        v = x @ v_w
        q = q.reshape(b, s, h, hd).transpose(0, 2, 1, 3)
        k = k.reshape(b, s, h, hd).transpose(0, 2, 1, 3)
        v = v.reshape(b, s, h, hd).transpose(0, 2, 1, 3)
        scores = jnp.einsum('bhqd,bhkd->bhqk', q, k) / jnp.sqrt(jnp.float32(hd))
        causal = jnp.tril(jnp.ones((s, s), dtype=bool))
        neg = jnp.finfo(scores.dtype).min
        scores = jnp.where(causal, scores, neg)
        attn = jax.nn.softmax(scores, axis=-1)
        row = jnp.arange(1, s + 1, dtype=jnp.float32)
        uniform = jnp.tril(jnp.ones((s, s), dtype=jnp.float32) / row[:, None])
        eye = jnp.eye(s, dtype=jnp.float32)
        new_attn = resid_gain * attn + skip_gain * eye[None, None] - centre_gain * uniform[None, None]
        out = jnp.einsum('bhqk,bhkd->bhqd', new_attn, v)
        out = out.transpose(0, 2, 1, 3).reshape(b, s, d)
        out = out @ cproj_w
        return out

    def _L1_ffn_ref(x, W, b, V_r, C):
        import jax, jax.numpy as jnp
        import numpy as np
        base = jnp.einsum('bsd,od->bso', x, W) + b
        correction = jnp.einsum('bsr,or->bso', jnp.einsum('bsd,dr->bsr', x, V_r), C)
        return base + correction
    x = L0_attn_x
    xn = _layernorm(x, axis=-1)
    s = _L0_attn_ref(xn, L0_attn_w_qkv, L0_attn_b_qkv, L0_attn_w_out, L0_attn_b_out, L0_attn_w1_rpe, L0_attn_b1_rpe, L0_attn_w2_rpe, L0_attn_b2_rpe)
    g = _silu(_L0_ffn_ref(xn, L0_ffn_router_weight, L0_ffn_router_bias, L0_ffn_gate_up_proj, L0_ffn_gate_up_bias, L0_ffn_down_proj, L0_ffn_down_bias))
    x = x + s * g
    xn = _layernorm(x, axis=-1)
    s = _L1_attn_ref(xn, L1_attn_qk_w, L1_attn_qk_b, L1_attn_v_w, L1_attn_cproj_w, L1_attn_resid_gain, L1_attn_skip_gain, L1_attn_centre_gain)
    g = _silu(_L1_ffn_ref(xn, L1_ffn_W, L1_ffn_b, L1_ffn_V_r, L1_ffn_C))
    x = x + s * g
    return x

_drawn_inputs = setup_inputs


def setup_inputs(seed=0):
    import zlib

    import numpy as np

    out = dict(_drawn_inputs(seed))
    spreads = {'L0_attn_b_qkv': (0.0, 0.8),
     'L0_attn_b_out': (0.0, 0.8),
     'L0_attn_b2_rpe': (0.0, 2.0),
     'L0_ffn_router_bias': (0.0, 0.8),
     'L0_ffn_gate_up_bias': (0.0, 0.8),
     'L0_ffn_down_bias': (0.0, 0.8),
     'L1_attn_qk_b': (0.0, 2.0),
     'L1_attn_resid_gain': (1.0, 0.6),
     'L1_attn_skip_gain': (1.0, 0.6),
     'L1_attn_centre_gain': (1.0, 0.6)}
    factors = {'L0_attn_w_qkv': 8.0,
     'L0_attn_w_out': 8.0,
     'L0_attn_w1_rpe': 8.0,
     'L0_attn_b1_rpe': 8.0,
     'L0_attn_w2_rpe': 8.0,
     'L0_ffn_router_weight': 8.0,
     'L0_ffn_gate_up_proj': 8.0,
     'L0_ffn_down_proj': 8.0,
     'L1_attn_qk_w': 64.0,
     'L1_ffn_b': 200.0,
     'L1_attn_v_w': 8.0,
     'L1_attn_cproj_w': 8.0,
     'L1_ffn_W': 8.0,
     'L1_ffn_V_r': 8.0,
     'L1_ffn_C': 8.0}
    for name, (base, spread) in spreads.items():
        noise = np.random.default_rng([zlib.crc32(name.encode()), seed]).standard_normal(out[name].shape)
        drawn = base * np.exp(spread * noise) if base else spread * noise
        out[name] = jnp.asarray(drawn.astype(out[name].dtype))
    for name, factor in factors.items():
        out[name] = (out[name] * factor).astype(out[name].dtype)
    return out
```

```python
from contextlib import ExitStack

import concourse.bass as bass
from concourse import mybir

ALU = mybir.AluOpType
ACT = mybir.ActivationFunctionType
F32 = mybir.dt.float32
BF16 = mybir.dt.bfloat16
AX = mybir.AxisListType

P = 128
B, T, D = 16, 256, 128
H, HD = 16, 8
Q4 = 4
NT = B * T // P
E, I = 8, 256
G = 8
RPE = 32
RANK = 32
ALPHA, LIMIT = 1.702, 7.0
EPS = 1e-5
QSCALE = float(HD) ** -0.5
NEG = -1.0e30
PARTS = 3
PAIRS = 6
QROWS = PAIRS * HD
REL = 512
TAB = 384
C_EYE, C_MA, C_MB, C_UT, C_RANK = 0, 128, 384, 640, 1152
C_FLIP = 1160
C_ALL = C_FLIP + 128


class Step:

    def __init__(self, k, J=0):
        self.k, self.J = k, J

    def n(self, d=0):
        return self.k + d + 3 * self.J

    def third(self, d=0):
        return (self.k + d) // 3 + self.J

    def has(self, d=0):
        return 0 <= self.k + d < B

    def buf(self, d=0):
        return (self.k + d) % 3


class Shared:
    pass


def build(nc, x_in, w_qkv, b_qkv, w_out, b_out, w1_rpe, b1_rpe, w2_rpe, b2_rpe, router_w, router_b,
          gu_w, gu_b, down_w, down_b, qk_w, qk_b, v_w, cproj_w, resid, skip, centre, f_w, f_b, f_v, f_c,
          consts, rel, out):
    with ExitStack() as ctx:
        def sb(name, shape, dt=F32):
            return ctx.enter_context(nc.sbuf_tensor(name, shape, dt))

        def sem(name):
            return ctx.enter_context(nc.semaphore(name))

        v = Shared()
        v.sem = sem
        v.x_in, v.w_qkv, v.b_qkv, v.w_out, v.b_out, v.w1_rpe = x_in, w_qkv, b_qkv, w_out, b_out, w1_rpe
        v.b1_rpe, v.w2_rpe, v.b2_rpe, v.router_w, v.router_b, v.gu_w = b1_rpe, w2_rpe, b2_rpe, router_w, router_b, gu_w
        v.gu_b, v.down_w, v.down_b, v.qk_w, v.qk_b, v.v_w = gu_b, down_w, down_b, qk_w, qk_b, v_w
        v.cproj_w, v.resid, v.skip, v.centre, v.f_w, v.f_b = cproj_w, resid, skip, centre, f_w, f_b
        v.f_v, v.f_c, v.consts, v.rel, v.out = f_v, f_c, consts, rel, out

        v.ps = ctx.enter_context(nc.psum_tensor("ps", [P, 8, 512], F32))

        v.x = sb("x", [P, NT, D])
        v.gate = sb("gate", [P, NT, D])
        v.xnT = sb("xnT", [P, NT * P])
        v.probs = sb("probs", [P, 8, 1024])
        v.qs = sb("qs", [P, 3, H, T], BF16)
        v.ks = sb("ks", [P, 3, H, T], BF16)
        v.tabB = sb("tabB", [P, H, TAB])
        v.tabA = sb("tabA", [P, H, TAB], BF16)
        v.vpad = sb("vpad", [P, 3, 8, 160])
        v.onespad = sb("onespad", [P, 4, 32])
        v.cst = sb("cst", [P, C_ALL])
        v.eyeb = sb("eyeb", [P, P], BF16)
        v.maskA = sb("maskA", [P, P], BF16)
        v.maskB = sb("maskB", [P, P], BF16)
        v.wqk0 = sb("wqk0", [P, 2, P])
        v.wqk1 = sb("wqk1", [P, 2, P])
        v.wv0 = sb("wv0", [P, P])
        v.wv1 = sb("wv1", [P, 2, P])
        v.wvs = sb("wvs", [P, P])
        v.wo0 = sb("wo0", [P, D])
        v.wo1 = sb("wo1", [P, D])
        v.bo = sb("bo", [P, D])
        v.cols = sb("cols", [P, 8])
        v.rwT = sb("rwT", [P, E])
        v.rb = sb("rb", [1, 4 * E])
        v.ones = sb("ones", [1, P])
        v.feff = sb("feff", [P, D])
        v.fb = sb("fb", [1, D])
        v.gub = sb("gub", [P, 32])
        v.wts = sb("wts", [P, NT, E])
        v.xb = sb("xb", [P, T])
        v.qkf = sb("qkf", [P, 2, T])
        v.qkr = sb("qkr", [P, 2, T])
        v.qk3 = sb("qk3", [P, 2, PARTS, T], BF16)
        v.mx = sb("mx", [P, 3, 2, H])
        v.mres = sb("mres", [P, 2, H])
        v.m3 = sb("m3", [P, PARTS, 2, H], BF16)
        v.mT = sb("mT", [PARTS * 2 * H, P], BF16)
        v.rden = sb("rden", [P, T])
        v.on = sb("on", [P, T])
        v.yt = sb("yt", [P, T])
        v.stat = sb("stat", [P, 4, NT])
        v.zrow = sb("zrow", [PARTS, T], BF16)
        v.eps = sb("eps", [P, 1])

        v.wgu = v.probs[:, 0:4, :].rearrange("p a b -> p (a b)").rearrange("p (e n) -> p e n", e=E)
        v.wdn = v.probs[:, 4:6, :].rearrange("p a b -> p (a b)").rearrange("p (e n) -> p e n", e=2 * E)
        v.squares = v.probs[:, 6:8, :].rearrange("p a b -> p (a b)").rearrange("p (t d) -> p t d", d=D)
        v.spare = v.probs[:, 6, :]
        v.acts = v.probs[:, 6:8, 0:512]
        v.vcen = v.tabA[:, 0:6, 0:256].bitcast(F32).rearrange("p (b c) n -> p b c n", c=2)
        v.scratch = v.tabB[:, :, :].rearrange("p h u -> p (h u)")
        v.rt = v.scratch[:, 0:8 * NT * E].rearrange("p (k t e) -> p k t e", k=8, e=E)

        v.bias_f = nc.dram_tensor("bias_f", (H, REL), F32, kind="Internal")
        v.bias_r = nc.dram_tensor("bias_r", (H, REL), BF16, kind="Internal")
        v.parts_d = nc.dram_tensor("parts_d", (3, 2, PARTS, P, T), BF16, kind="Internal")
        v.max_d = nc.dram_tensor("max_d", (3, PARTS, 2, H, P), BF16, kind="Internal")

        setup(nc, v)
        experts(nc, v)
        tables(nc, v)
        attention(nc, v, 0)
        middle(nc, v)
        attention(nc, v, 1)


def setup(nc, v):
    sem = v.sem
    ps, cst, x, gate, xnT, stat = v.ps, v.cst, v.x, v.gate, v.xnT, v.stat
    scr = v.scratch
    hid = scr[0:RPE + 1, 0:2 * REL]
    relb = scr[0:RPE, 2 * REL:4 * REL]
    base = 4 * REL
    w2 = scr[0:RPE + 1, base:base + H]
    w2p = scr[0:RPE + 1, base + H:base + 2 * H]
    bfw = scr[0:H, base + 32:base + 32 + REL]
    brv = scr[0:H, base + 544:base + 544 + REL // 2].bitcast(BF16)
    base += 800
    wqkv = scr[:, base:base + 3 * P]
    base += 3 * P
    wqk = scr[:, base:base + 2 * P]
    base += 2 * P
    rows = scr[0:1, base:base + 6 * P].rearrange("p (a b) -> p a b", b=P)
    base += 6 * P
    rowsp = scr[0:1, base:base + 6 * P].rearrange("p (a b) -> p a b", b=P)
    base += 6 * P
    gains = v.spare[:, 0:3 * H].rearrange("p (a h) -> p a h", h=H)
    bor = v.spare[0:1, 64:64 + P]
    bvb = v.spare[:, 192:192 + P]
    fw = v.spare[:, 320:320 + P]
    fv = v.spare[:, 448:448 + RANK]
    fc = v.spare[:, 480:480 + RANK]
    fvT = v.spare[0:RANK, 512:512 + P]
    fcT = v.spare[0:RANK, 640:640 + P]
    rw = v.spare[0:E, 768:768 + P]
    gubr = v.spare[0:32, 896:896 + P]
    rpc = v.xb[0:RPE, 0:2]
    eye = cst[:, C_EYE:C_EYE + P]

    c_load = sem("su_consts")
    x_load = sem("su_x")
    w_load = sem("su_weights")
    e_load = sem("su_expert_weights")
    copied = sem("su_copied")
    hidden = sem("su_hidden")
    bias_mm = sem("su_bias_mm")
    bias_cp = sem("su_bias_cp")
    bias_st = sem("su_bias_stored")
    small_mm = sem("su_small_mm")
    small_cp = sem("su_small_cp")
    zeroed = sem("su_zeroed")
    ln = sem("su_ln")
    sq = sem("su_sq")
    rs = sem("su_rs")
    tr = sem("su_tr")
    trc = sem("su_trc")
    lg = sem("su_lg")
    lgc = sem("su_lgc")
    ro = sem("su_ro")
    ex = sem("su_ex")
    NW = 26

    with nc.Block() as block:
        @block.sync
        def _(sp):
            sp.dma_start(cst[:, :], v.consts[:, :]).then_inc(c_load, 16)
            for half in range(2):
                sp.dma_start(x[:, 16 * half:16 * half + 16, :],
                             v.x_in[8 * half:8 * half + 8].rearrange("b (c p) d -> p (b c) d", p=P)).then_inc(x_load, 16)
            loads = [
                (relb, v.rel[0, :].partition_broadcast(RPE)),
                (w2[0:RPE, :], v.w2_rpe[:, :]),
                (w2[RPE:RPE + 1, :], v.b2_rpe.rearrange("(a n) -> a n", a=1)),
                (rpc[:, 0:1], v.w1_rpe.rearrange("a k -> k a")),
                (rpc[:, 1:2], v.b1_rpe.rearrange("(k a) -> k a", a=1)),
                (wqkv, v.w_qkv[:, :]),
                (wqk, v.qk_w[:, :]),
                (v.wv1[:, 0, :], v.v_w[:, :]),
                (v.wo0[:, :], v.w_out[:, :]),
                (v.wo1[:, :], v.cproj_w[:, :]),
                (rows[:, 0:3, :], v.b_qkv.rearrange("(o a n) -> o a n", o=1, a=3)),
                (rows[:, 3:5, :], v.qk_b.rearrange("(o a n) -> o a n", o=1, a=2)),
                (gains[:, 0, :], v.resid[0, :, 0, 0].partition_broadcast(P)),
                (gains[:, 1, :], v.skip[0, :, 0, 0].partition_broadcast(P)),
                (gains[:, 2, :], v.centre[0, :, 0, 0].partition_broadcast(P)),
                (bor, v.b_out.rearrange("(a n) -> a n", a=1)),
                (fw, v.f_w[:, :]),
                (fv, v.f_v[:, :]),
                (fc, v.f_c[:, :]),
                (v.fb[:, :], v.f_b.rearrange("(a n) -> a n", a=1)),
                (rw, v.router_w[:, :]),
                (gubr, v.gu_b.rearrange("e (j n) -> (e j) n", n=P)),
            ] + [(v.rb[:, E * c:E * c + E], v.router_b.rearrange("(a n) -> a n", a=1)) for c in range(4)]
            for dst, src in loads:
                sp.dma_start(dst, src).then_inc(w_load, 16)
            assert len(loads) == NW
            sp.dma_start(v.wgu, v.gu_w.rearrange("e h n -> h e n")).then_inc(e_load, 16)
            sp.dma_start(v.wdn, v.down_w.rearrange("e (c i) h -> i (e c) h", c=2)).then_inc(e_load, 16)
            sp.wait_ge(bias_cp, 2)
            sp.dma_start(v.bias_f[:, :], bfw).then_inc(bias_st, 16)
            sp.dma_start(v.bias_r[:, :], brv).then_inc(bias_st, 16)
            sp.wait_ge(bias_st, 32)
            sp.wait_ge(e_load, 32)

        @block.gpsimd
        def _(pool):
            nc.gpsimd.memset(v.vpad[:], 0.0).then_inc(zeroed, 1)
            nc.gpsimd.memset(v.onespad[:], 0.0).then_inc(zeroed, 1)
            pool.wait_ge(zeroed, 2)
            for i in range(4):
                nc.gpsimd.memset(v.onespad[:, i, 8 * i:8 * i + 8], 1.0).then_inc(zeroed, 1)
            nc.gpsimd.memset(v.zrow[:], 0.0).then_inc(zeroed, 1)
            for buf in range(3):
                nc.gpsimd.memset(v.qs[:, buf].bitcast(F32), 0.0).then_inc(zeroed, 1)
                nc.gpsimd.memset(v.ks[:, buf].bitcast(F32), 0.0).then_inc(zeroed, 1)

        @block.vector
        def _(dve):
            nc.vector.memset(v.eps[:], EPS).then_inc(ln, 1)
            nc.vector.memset(v.ones[:], 1.0).then_inc(copied, 1)
            nc.vector.memset(hid[RPE:RPE + 1, :], 1.0).then_inc(copied, 1)
            dve.wait_ge(c_load, 16)
            nc.vector.tensor_copy(v.eyeb[:], eye).then_inc(copied, 1)
            nc.vector.tensor_copy(v.maskA[:], cst[:, C_MA + P:C_MA + 2 * P]).then_inc(copied, 1)
            nc.vector.tensor_copy(v.maskB[:], cst[:, C_MB:C_MB + P]).then_inc(copied, 1)
            dve.wait_ge(w_load, 16 * NW)
            dve.wait_ge(copied, 5)
            nc.vector.tensor_scalar(hid[0:RPE, :], relb, rpc[:, 0:1], rpc[:, 1:2], ALU.mult, ALU.add).then_inc(hidden, 1)
            dve.wait_ge(hidden, 1)
            nc.vector.tensor_scalar(hid[0:RPE, :], hid[0:RPE, :], 0.0, None, ALU.max).then_inc(hidden, 1)
            for i in range(4):
                nc.vector.tensor_copy(w2p[:, 4 * i:4 * i + 4], w2[:, i:H:4]).then_inc(hidden, 1)
            for src, dst in ((wqkv, v.wqk0), (wqk, v.wqk1)):
                for a in range(2):
                    nc.vector.tensor_copy(dst[:, a, :].rearrange("p (d i q) -> p d i q", d=HD, i=4),
                                          src[:, P * a:P * a + P].rearrange("p (q i d) -> p d i q", q=4, i=4)
                                          ).then_inc(copied, 1)
            for a in (0, 1, 3, 4):
                nc.vector.tensor_copy(rowsp[:, a, :].rearrange("p (d i q) -> p d i q", d=HD, i=4),
                                      rows[:, a, :].rearrange("p (q i d) -> p d i q", q=4, i=4)).then_inc(copied, 1)
            nc.vector.tensor_copy(rowsp[:, 2, :], rows[:, 2, :]).then_inc(copied, 1)
            nc.vector.tensor_copy(rowsp[:, 5, :].rearrange("p (h d) -> p h d", d=HD),
                                  gains[0:1, 0, :].unsqueeze(2).broadcast_to([1, H, HD])).then_inc(copied, 1)
            nc.vector.tensor_copy(v.wv0[:], wqkv[:, 2 * P:3 * P]).then_inc(copied, 1)
            vw = v.wv1[:, 0, :].rearrange("p (h d) -> p h d", d=HD)
            nc.vector.tensor_tensor(v.wvs[:].rearrange("p (h d) -> p h d", d=HD), vw,
                                    gains[:, 1, :].unsqueeze(2).broadcast_to([P, H, HD]), ALU.mult).then_inc(copied, 1)
            nc.vector.scalar_tensor_tensor(v.wv1[:, 1, :].rearrange("p (h d) -> p h d", d=HD), vw, -1.0,
                                           gains[:, 2, :].unsqueeze(2).broadcast_to([P, H, HD]),
                                           ALU.mult, ALU.mult).then_inc(copied, 1)
            dve.wait_ge(bias_mm, 2)
            nc.vector.tensor_copy(bfw, ps[0:H, 0, :]).then_inc(bias_cp, 1)
            nc.vector.tensor_copy(brv, ps[0:H, 1, :]).then_inc(bias_cp, 1)
            dve.wait_ge(small_mm, 1)
            nc.vector.tensor_scalar(v.cols[:, 0:1], ps[:, 2, 0:1], QSCALE, None, ALU.mult).then_inc(small_cp, 1)
            nc.vector.tensor_copy(v.cols[:, 1:3], ps[:, 2, 1:3]).then_inc(small_cp, 1)
            nc.vector.tensor_scalar(v.cols[:, 3:4], ps[:, 2, 3:4], QSCALE, None, ALU.mult).then_inc(small_cp, 1)
            nc.vector.tensor_copy(v.cols[:, 4:6], ps[:, 2, 4:6]).then_inc(small_cp, 1)
            nc.vector.tensor_copy(v.rwT[:], ps[:, 2, 8:8 + E]).then_inc(small_cp, 1)
            nc.vector.tensor_copy(v.gub[:], ps[:, 2, 32:64]).then_inc(small_cp, 1)
            nc.vector.tensor_copy(fvT, ps[0:RANK, 2, 128:256]).then_inc(small_cp, 1)
            nc.vector.tensor_copy(fcT, ps[0:RANK, 2, 256:384]).then_inc(small_cp, 1)
            dve.wait_ge(small_cp, 8)
            nc.vector.tensor_copy(bvb, v.cols[:, 2:3].broadcast_to([P, P])).then_inc(small_cp, 1)
            up = v.gub[:].rearrange("p (e j) -> p e j", j=4)[:, :, 2:4]
            nc.vector.tensor_scalar(up, up, 1.0, None, ALU.add).then_inc(small_cp, 1)
            dve.wait_ge(small_mm, 2)
            nc.vector.tensor_copy(v.bo[:], ps[:, 3, 0:P]).then_inc(small_cp, 1)
            nc.vector.tensor_copy(v.feff[:], ps[:, 3, P:2 * P]).then_inc(small_cp, 1)
            dve.wait_ge(zeroed, 13)
            nc.vector.memset(v.ks[32:64, :, :, :], 1.0).then_inc(small_cp, 1)
            dve.wait_ge(small_cp, 13)
            layernorm_vector(nc, dve, v, ln, sq, rs, x_load)
            r = v.rt
            dve.wait_ge(lg, G)
            L, cand, one1, L2, one2, tmp, ew = (r[:, k] for k in range(7))
            nc.vector.tensor_copy(L, ps[:, 7, 0:NT * E].rearrange("p (t e) -> p t e", e=E)).then_inc(ro, 1)
            rank = cst[:, C_RANK:C_RANK + E].unsqueeze(1).broadcast_to([P, NT, E])

            def wide(a):
                return a.unsqueeze(2).broadcast_to([P, NT, E])

            m1, m2, rk = stat[:, 0, :], stat[:, 1, :], stat[:, 2, :]
            n = 1

            def pick(src, m, hot, n):
                dve.wait_ge(ro, n)
                nc.vector.tensor_reduce(m, src, AX.X, ALU.max).then_inc(ro, 1)
                dve.wait_ge(ro, n + 1)
                nc.vector.tensor_tensor(cand, src, wide(m), ALU.is_equal).then_inc(ro, 1)
                dve.wait_ge(ro, n + 2)
                nc.vector.tensor_tensor(cand, cand, rank, ALU.mult).then_inc(ro, 1)
                dve.wait_ge(ro, n + 3)
                nc.vector.tensor_reduce(rk, cand, AX.X, ALU.max).then_inc(ro, 1)
                dve.wait_ge(ro, n + 4)
                nc.vector.tensor_tensor(hot, cand, wide(rk), ALU.is_equal).then_inc(ro, 1)
                return n + 5

            n = pick(L, m1, one1, n)
            dve.wait_ge(ro, n)
            nc.vector.scalar_tensor_tensor(L2, one1, -3.0e38, L, ALU.mult, ALU.add).then_inc(ro, 1)
            n = pick(L2, m2, one2, n + 1)
            dve.wait_ge(ro, n)
            nc.vector.tensor_tensor(one1, one1, one2, ALU.add).then_inc(ro, 1)
            nc.vector.tensor_tensor(tmp, L, wide(m1), ALU.subtract).then_inc(lgc, 1)
            dve.wait_ge(ex, 1)
            nc.vector.tensor_reduce(m2, ew, AX.X, ALU.add).then_inc(ro, 1)
            dve.wait_ge(ro, n + 2)
            nc.vector.reciprocal(m2, m2).then_inc(ro, 1)
            nc.vector.tensor_tensor(ew, ew, one1, ALU.mult).then_inc(ro, 1)
            dve.wait_ge(ro, n + 4)
            nc.vector.tensor_tensor(v.wts[:], ew, wide(m2), ALU.mult).then_inc(ro, 1)

        @block.scalar
        def _(act):
            layernorm_scalar(nc, act, v, ln, sq, rs)
            for g in range(G):
                act.wait_ge(tr, g + 1)
                nc.scalar.activation(xnT[:, 512 * g:512 * g + 512], ps[:, 4 + g % 2, :], ACT.Copy).then_inc(trc, 1)
            act.wait_ge(lgc, 1)
            nc.scalar.activation(v.rt[:, 6], v.rt[:, 5], ACT.Exp).then_inc(ex, 1)

        @block.tensor
        def _(pe):
            pe.wait_ge(w_load, 16 * NW)
            pe.wait_ge(hidden, 6)
            for k in range(2):
                nc.tensor.matmul(ps[0:H, k, :], w2p, hid[:, REL * k:REL * k + REL], start=True, stop=True).then_inc(bias_mm, 1)
            pe.wait_ge(copied, 18)
            one = v.ones[0:1, 0:1]
            for k in range(6):
                nc.tensor.matmul(ps[:, 2, k:k + 1], rowsp[:, k, :], one, start=True, stop=True)
            nc.tensor.transpose(ps[:, 2, 8:8 + E], rw, eye[0:E, 0:E])
            nc.tensor.transpose(ps[:, 2, 32:64], gubr, eye[0:32, 0:32])
            nc.tensor.matmul(ps[0:RANK, 2, 128:256], fv, eye, start=True, stop=True)
            nc.tensor.matmul(ps[0:RANK, 2, 256:384], fc, eye, start=True, stop=True).then_inc(small_mm, 1)
            pe.wait_ge(small_cp, 10)
            nc.tensor.matmul(ps[:, 3, 0:P], bvb, v.wo0[:], start=True, stop=False)
            nc.tensor.matmul(ps[:, 3, 0:P], v.ones[0:1, 0:P], bor, start=False, stop=True)
            nc.tensor.matmul(ps[:, 3, P:2 * P], fw, eye, start=True, stop=False)
            nc.tensor.matmul(ps[:, 3, P:2 * P], fvT, fcT, start=False, stop=True).then_inc(small_mm, 1)
            def logits(g, pe):
                pe.wait_ge(trc, g + 1)
                o = ps[:, 7, 32 * g:32 * g + 32]
                nc.tensor.matmul(o, v.ones[0:1, 0:P], v.rb[:], start=(g == 0), stop=False, skip_group_check=True)
                for c in range(4):
                    t = 4 * g + c
                    mm = nc.tensor.matmul(ps[:, 7, E * t:E * t + E], xnT[:, P * t:P * t + P], v.rwT[:],
                                          start=False, stop=True, skip_group_check=True)
                mm.then_inc(lg, 1)

            for g in range(G):
                if g >= 2:
                    pe.wait_ge(trc, g - 1)
                pe.wait_ge(ln, layernorm_ready(g))
                for c in range(4):
                    mm = nc.tensor.transpose(ps[:, 4 + g % 2, P * c:P * c + P], gate[:, 4 * g + c, :], eye)
                mm.then_inc(tr, 1)
                if g >= 1:
                    logits(g - 1, pe)
            logits(G - 1, pe)



def layernorm_ready(g):
    return 7 if g < G // 2 else 13


def layernorm_vector(nc, dve, v, ln, sq, rs, x_load=None):
    for half in range(2):
        a = slice(16 * half, 16 * half + 16)
        xh, gh = v.x[:, a, :], v.gate[:, a, :]
        s, var, r, m = (v.stat[:, k, a] for k in range(4))
        n = 6 * half + 1
        if x_load is not None:
            dve.wait_ge(x_load, 16 * (half + 1))
        nc.vector.tensor_reduce(s, xh, AX.X, ALU.add).then_inc(ln, 1)
        dve.wait_ge(ln, n + 1)
        nc.vector.tensor_scalar(m, s, 1.0 / D, None, ALU.mult).then_inc(ln, 1)
        dve.wait_ge(ln, n + 2)
        nc.vector.tensor_tensor(gh, xh, m.unsqueeze(2).broadcast_to([P, 16, D]), ALU.subtract).then_inc(ln, 1)
        dve.wait_ge(sq, half + 1)
        nc.vector.tensor_reduce(var, v.squares, AX.X, ALU.add).then_inc(ln, 1)
        dve.wait_ge(rs, half + 1)
        nc.vector.reciprocal(r, r).then_inc(ln, 1)
        dve.wait_ge(ln, n + 5)
        nc.vector.tensor_tensor(gh, gh, r.unsqueeze(2).broadcast_to([P, 16, D]), ALU.mult).then_inc(ln, 1)


def layernorm_scalar(nc, act, v, ln, sq, rs):
    for half in range(2):
        a = slice(16 * half, 16 * half + 16)
        act.wait_ge(ln, 6 * half + 4)
        nc.scalar.activation(v.squares, v.gate[:, a, :], ACT.Square).then_inc(sq, 1)
        act.wait_ge(ln, 6 * half + 5)
        nc.scalar.activation(v.stat[:, 2, a], v.stat[:, 1, a], ACT.Sqrt, bias=v.eps[:, 0:1], scale=1.0 / D).then_inc(rs, 1)


def experts(nc, v):
    sem = v.sem
    ps, xnT, cst, wgu, wdn, gub, wts, gate = v.ps, v.xnT, v.cst, v.wgu, v.wdn, v.gub, v.wts, v.gate
    eye = cst[:, C_EYE:C_EYE + P]
    scr = v.scratch
    U = 2 * E

    def buf(k):
        return scr[:, 1024 * k:1024 * k + 1024].rearrange("p (b n) -> p b n", b=2)

    gt, sg, ut, gl = buf(0), buf(1), buf(2), buf(3)
    tmp2 = scr[:, 4096:5120].rearrange("p (b n) -> p b n", b=2)
    sgo = scr[:, 5120:5632]
    wg = scr[:, 5632:5664]
    acc = v.probs[:, 6, 512:1024]
    bd = v.qkr[0:32, :, :].rearrange("p a t -> p (a t)")
    wT = v.qkf[0:32, 0, 0:P]
    acts = (v.acts[:, 0, :], v.acts[:, 1, :])

    bd_ready = sem("ex_bd")
    gu_full = sem("ex_gu_full")
    g_done = sem("ex_g_done")
    u_done = sem("ex_u_done")
    s_done = sem("ex_s_done")
    glu_done = sem("ex_glu_done")
    clip_done = sem("ex_clip_done")
    a_done = sem("ex_a_done")
    dn_full = sem("ex_dn_full")
    t_done = sem("ex_t_done")
    acc0_done = sem("ex_acc0_done")
    acc_done = sem("ex_acc_done")
    wg_done = sem("ex_wg")
    wt_mm = sem("ex_wt_mm")
    wt_done = sem("ex_wt")
    bias_mm = sem("ex_bias_mm")
    so_done = sem("ex_so")
    out_done = sem("ex_out")
    bd_zero = sem("ex_bd_zero")

    def tokens(g):
        return xnT[:, bass.ds(g * 512, 512)]

    def group(a, g):
        return a[:, bass.ds(g * 4, 4), :]

    with nc.Block() as block:
        @block.sync
        def _(sp):
            sp.wait_ge(bd_zero, 1)
            for c in range(4):
                sp.dma_start(bd[E * c:E * c + E, D * c:D * c + D], v.down_b[:, :]).then_inc(bd_ready, 16)
            sp.wait_ge(bd_ready, 64)

        @block.tensor
        def _(pe):
            def step(g, first):
                for u in range(U):
                    if u >= 2 or not first:
                        pe.wait_ge(g_done, g * U + u - 1)
                        pe.wait_ge(u_done, g * U + u - 1)
                    e, half = u // 2, u % 2
                    for k in range(2):
                        mm = nc.tensor.matmul(ps[:, 2 * (u % 2) + k, :], wgu[:, e, I * k + P * half:I * k + P * half + P],
                                              tokens(g), start=True, stop=True)
                    mm.then_inc(gu_full, 1)
                    if u == 2:
                        pe.wait_ge(wg_done, g + 1)
                        if not first:
                            pe.wait_ge(wt_done, g)
                        nc.tensor.transpose(ps[0:32, 6, 0:P], wg, eye).then_inc(wt_mm, 1)
                    if u == 3:
                        pe.wait_ge(wt_done, g + 1)
                        if first:
                            pe.wait_ge(bd_ready, 64)
                        else:
                            pe.wait_ge(acc0_done, g)
                        nc.tensor.matmul(ps[:, 7, :], wT, bd, start=True, stop=True).then_inc(bias_mm, 1)
                    if u >= 2:
                        down(g * U + u - 2, u - 2, first, g * E + u // 2 - 1)
                    elif not first:
                        down(g * U + u - 2, U + u - 2, False, g * E)

            def down(n, u, first, experts_begun):
                e, half = u // 2, u % 2
                pe.wait_ge(a_done, n + 1)
                if half == 0 and not (first and e < 2):
                    pe.wait_ge(t_done, experts_begun - 2)
                for c in range(4):
                    mm = nc.tensor.matmul(ps[:, 4 + e % 2, D * c:D * c + D], acts[u % 2][:, P * c:P * c + P], wdn[:, u, :],
                                          start=(half == 0 and c == 0), stop=(half == 1), skip_group_check=True)
                mm.then_inc(dn_full, 1)

            step(0, True)
            with pe.Fori(1, G) as g:
                step(g, False)
            down(G * U - 2, U - 2, False, G * E)
            down(G * U - 1, U - 1, False, G * E)

        @block.scalar
        def _(act):
            def step(g, first):
                for u in range(U):
                    n = g * U + u
                    e, half = u // 2, u % 2
                    act.wait_ge(gu_full, n + 1)
                    if u >= 2 or not first:
                        act.wait_ge(a_done, n - 1)
                    nc.scalar.activation(ut[:, u % 2, :], ps[:, 2 * (u % 2) + 1, :], ACT.Identity,
                                         bias=gub[:, 4 * e + 2 + half:4 * e + 3 + half]).then_inc(u_done, 1)
                    act.wait_ge(g_done, n + 1)
                    if u >= 2 or not first:
                        act.wait_ge(glu_done, n - 1)
                    nc.scalar.activation(sg[:, u % 2, :], gt[:, u % 2, :], ACT.Sigmoid, scale=ALPHA).then_inc(s_done, 1)
                    if u == 0:
                        if not first:
                            act.wait_ge(wt_mm, g)
                        nc.scalar.activation(wg.rearrange("p (t e) -> p t e", e=E), group(wts, g), ACT.Copy).then_inc(wg_done, 1)
                    if u == 2:
                        act.wait_ge(wt_mm, g + 1)
                        if not first:
                            act.wait_ge(bias_mm, g)
                        nc.scalar.activation(wT, ps[0:32, 6, 0:P], ACT.Copy).then_inc(wt_done, 1)
                    if u == 3 and not first:
                        finish(g - 1)

            def finish(g):
                act.wait_ge(acc_done, (g + 1) * (E - 1))
                nc.scalar.activation(sgo, acc, ACT.Sigmoid).then_inc(so_done, 1)

            step(0, True)
            with act.Fori(1, G) as g:
                step(g, False)
            finish(G - 1)

        @block.vector
        def _(dve):
            nc.vector.memset(bd, 0.0).then_inc(bd_zero, 1)

            def activation(n, u):
                dve.wait_ge(u_done, n + 1)
                nc.vector.tensor_scalar(ut[:, u % 2, :], ut[:, u % 2, :], 1.0 - LIMIT, 1.0 + LIMIT,
                                        ALU.max, ALU.min).then_inc(clip_done, 1)
                dve.wait_ge(glu_done, n + 1)
                dve.wait_ge(clip_done, n + 1)
                nc.vector.tensor_tensor(acts[u % 2], ut[:, u % 2, :], gl[:, u % 2, :], ALU.mult).then_inc(a_done, 1)

            def weigh(g, e, first):
                n = g * E + e
                dve.wait_ge(dn_full, 2 * n + 2)
                if e >= 3:
                    dve.wait_ge(acc_done, g * (E - 1) + e - 2)
                elif e < 2 and not first:
                    dve.wait_ge(acc_done, g * (E - 1) + e - 1)
                t = tmp2[:, e % 2, :].rearrange("p (t d) -> p t d", d=D)
                w = group(wts, g)[:, :, e:e + 1].broadcast_to([P, 4, D])
                nc.vector.tensor_tensor(t, ps[:, 4 + e % 2, :].rearrange("p (t d) -> p t d", d=D), w,
                                        ALU.mult).then_inc(t_done, 1)
                if e == 0:
                    dve.wait_ge(t_done, n + 1)
                    dve.wait_ge(bias_mm, g + 1)
                    nc.vector.tensor_tensor(acc, tmp2[:, 0, :], ps[:, 7, :], ALU.add).then_inc(acc0_done, 1)

            def finish(g):
                dve.wait_ge(so_done, g + 1)
                nc.vector.tensor_tensor(group(gate, g), acc.rearrange("p (t d) -> p t d", d=D),
                                        sgo.rearrange("p (t d) -> p t d", d=D), ALU.mult).then_inc(out_done, 1)

            def step(g, first):
                for u in range(U):
                    n = g * U + u
                    e, half = u // 2, u % 2
                    if u >= 1 or not first:
                        if u >= 3 or not first:
                            dve.wait_ge(dn_full, n - 2)
                        activation(n - 1, (u - 1) % U)
                    if u == 4 and not first:
                        finish(g - 1)
                    if u % 2 == 0 and u >= 4:
                        weigh(g, e - 2, first)
                    elif u % 2 == 0 and not first:
                        weigh(g - 1, E + e - 2, False)
                    dve.wait_ge(gu_full, n + 1)
                    if u >= 2 or not first:
                        dve.wait_ge(glu_done, n - 1)
                    nc.vector.tensor_scalar(gt[:, u % 2, :], ps[:, 2 * (u % 2), :], gub[:, 4 * e + half:4 * e + half + 1],
                                            LIMIT, ALU.add, ALU.min).then_inc(g_done, 1)

            step(0, True)
            with dve.Fori(1, G) as g:
                step(g, False)
            dve.wait_ge(dn_full, G * U - 2)
            activation(G * U - 1, U - 1)
            weigh(G - 1, E - 2, False)
            weigh(G - 1, E - 1, False)
            finish(G - 1)

        @block.gpsimd
        def _(pool):
            def add(g, e):
                pool.wait_ge(t_done, g * E + e + 1)
                if e == 1:
                    pool.wait_ge(acc0_done, g + 1)
                else:
                    pool.wait_ge(acc_done, g * (E - 1) + e - 1)
                nc.gpsimd.tensor_tensor(acc, acc, tmp2[:, e % 2, :], ALU.add).then_inc(acc_done, 1)

            def step(g, first):
                for u in range(U):
                    n = g * U + u
                    pool.wait_ge(s_done, n + 1)
                    if u >= 2 or not first:
                        pool.wait_ge(a_done, n - 1)
                    nc.gpsimd.tensor_tensor(gl[:, u % 2, :], gt[:, u % 2, :], sg[:, u % 2, :], ALU.mult).then_inc(glu_done, 1)
                    if u % 2 == 0:
                        if u >= 6:
                            add(g, u // 2 - 2)
                        elif u < 4 and not first:
                            add(g - 1, E + u // 2 - 2)

            step(0, True)
            with pool.Fori(1, G) as g:
                step(g, False)
            add(G - 1, E - 2)
            add(G - 1, E - 1)


def tables(nc, v):
    ps, cst = v.ps, v.cst
    flip = cst[:, C_FLIP:C_FLIP + P]
    flipb = v.acts[:, 0, 0:P // 2].bitcast(BF16)
    tabs = (v.tabA[:].rearrange("p h u -> p (h u)"), v.tabB[:].rearrange("p h u -> p (h u)"))
    N = H * TAB // 512
    ld, fl, mm, cp = [v.sem(f"ta_ld{i}") for i in range(2)], v.sem("ta_flip"), v.sem("ta_mm"), v.sem("ta_cp")
    with nc.Block() as block:
        @block.sync
        def _(sp):
            for i, src in enumerate((v.bias_r, v.bias_f)):
                sp.dma_start((v.tabA, v.tabB)[i][:], bass.AP(src, 1, [[1, P], [REL, H], [1, TAB]])).then_inc(ld[i], 16)
                sp.wait_ge(ld[i], 16)

        @block.vector
        def _(dve):
            nc.vector.tensor_copy(flipb, flip).then_inc(fl, 1)

        @block.tensor
        def _(pe):
            pe.wait_ge(fl, 1)
            for i in range(2):
                pe.wait_ge(ld[i], 16)
                for n in range(N):
                    k = N * i + n
                    if k >= 8:
                        pe.wait_ge(cp, k - 7)
                    nc.tensor.matmul(ps[:, k % 8, :], flip if i else flipb, tabs[i][:, 512 * n:512 * n + 512],
                                     start=True, stop=True).then_inc(mm, 1)

        @block.scalar
        def _(act):
            for k in range(2 * N):
                act.wait_ge(mm, k + 1)
                n = k % N
                nc.scalar.activation(tabs[k // N][:, 512 * n:512 * n + 512], ps[:, k % 8, :], ACT.Copy).then_inc(cp, 1)


def middle(nc, v):
    sem = v.sem
    ps, gate, xnT, cst = v.ps, v.gate, v.xnT, v.cst
    eye = cst[:, C_EYE:C_EYE + P]
    ln, sq, rs = sem("mi_ln"), sem("mi_sq"), sem("mi_rs")
    tr, trc = sem("mi_tr"), sem("mi_trc")
    fm, sg, gd = sem("mi_ffn"), sem("mi_sigmoid"), sem("mi_gate")
    with nc.Block() as block:
        @block.vector
        def _(dve):
            nc.vector.memset(v.eps[:], EPS).then_inc(ln, 1)
            layernorm_vector(nc, dve, v, ln, sq, rs)
            for g in range(G):
                dve.wait_ge(sg, g + 1)
                a = gate[:, 4 * g:4 * g + 4, :]
                nc.vector.tensor_tensor(a, ps[:, 4 + g % 4, :].rearrange("p (t d) -> p t d", d=D), a,
                                        ALU.mult).then_inc(gd, 1)

        @block.scalar
        def _(act):
            layernorm_scalar(nc, act, v, ln, sq, rs)

            def sigmoid(g):
                act.wait_ge(fm, g + 1)
                nc.scalar.activation(gate[:, 4 * g:4 * g + 4, :].rearrange("p t d -> p (t d)"), ps[:, 4 + g % 4, :],
                                     ACT.Sigmoid).then_inc(sg, 1)

            for g in range(G):
                act.wait_ge(tr, g + 1)
                nc.scalar.activation(xnT[:, 512 * g:512 * g + 512], ps[:, g % 4, :], ACT.Copy).then_inc(trc, 1)
                if g >= 1:
                    sigmoid(g - 1)
            sigmoid(G - 1)

        @block.tensor
        def _(pe):
            def ffn(g):
                pe.wait_ge(trc, g + 1)
                if g >= 4:
                    pe.wait_ge(gd, g - 3)
                for c in range(4):
                    t = 4 * g + c
                    o = ps[:, 4 + g % 4, D * c:D * c + D]
                    nc.tensor.matmul(o, v.ones[0:1, 0:P], v.fb[:], start=(c == 0), stop=False, skip_group_check=True)
                    mm = nc.tensor.matmul(o, xnT[:, P * t:P * t + P], v.feff[:], start=False, stop=True,
                                          skip_group_check=True)
                mm.then_inc(fm, 1)

            for g in range(G):
                pe.wait_ge(ln, layernorm_ready(g))
                if g >= 4:
                    pe.wait_ge(trc, g - 3)
                for c in range(4):
                    mm = nc.tensor.transpose(ps[:, g % 4, P * c:P * c + P], gate[:, 4 * g + c, :], eye)
                mm.then_inc(tr, 1)
                if g >= 1:
                    ffn(g - 1)
            ffn(G - 1)


class Units:

    def __init__(self, count):
        self.count = count
        self.order = [("A", 0), ("A", 1), ("A", 2)]
        for j in range(count - 3):
            self.order += [("B", j), ("A", j + 3)]
        self.order += [("B", j) for j in range(count - 3, count)]

    def exists(self, k, kind):
        return 0 <= (k if kind == "A" else k - 1) < B

    def slot(self, k, pos):
        return (len(self.order) * k + pos) % 3

    def before(self, k, pos):
        n = len(self.order) * k + pos - 3
        while n >= 0:
            kk, p = divmod(n, len(self.order))
            kind, j = self.order[p]
            if self.exists(kk, kind):
                return kind, j, kk - k
            n -= 3
        return None


def attention(nc, v, layer):
    U = Units(8 if layer == 0 else 6)
    NU = U.count
    ps, x, gate, xnT, probs, qs, ks = v.ps, v.x, v.gate, v.xnT, v.probs, v.qs, v.ks
    cst, vpad, onespad, cols, xb, vcen = v.cst, v.vpad, v.onespad, v.cols, v.xb, v.vcen
    qkf, qkr, qk3, mx, mres, m3, mT = v.qkf, v.qkr, v.qk3, v.mx, v.mres, v.m3, v.mT
    rden, on, yt, eyeb, maskA, maskB = v.rden, v.on, v.yt, v.eyeb, v.maskA, v.maskB
    wqk, wo = (v.wqk0, v.wo0) if layer == 0 else (v.wqk1, v.wo1)
    bq, bk = (0, 1) if layer == 0 else (3, 4)
    ring = ps[:, 0:6, :].rearrange("p (s b) n -> p s (b n)", s=3)
    od = ps[:, 6, :]
    misc = ps[:, 7, :]

    def sem(name):
        return v.sem(f"l{layer}_{name}")

    full = {"A": sem("a_full"), "B": sem("b_full")}
    used = {"A": sem("a_used"), "B": sem("b_used")}
    exp_done = sem("exp_done") if layer == 0 else used["B"]
    pv_done = sem("pv_done")
    qk_full, v_full, e_full = sem("qk_full"), sem("v_full"), sem("e_full")
    y_full, mt_full = sem("y_full"), sem("mt_full")
    qk_evac, v_evac, e_evac = sem("qk_evac"), sem("v_evac"), sem("e_evac")
    y_evac, mt_evac = sem("y_evac"), sem("mt_evac")
    s1_done, r1_done, s2_done, s3_done = sem("s1"), sem("r1"), sem("s2"), sem("s3")
    xb_done = sem("xb")
    max_parts = sem("max_parts")
    rd_done, on_done = sem("rd"), sem("on")
    y_done, fin_done = sem("y"), sem("fin")
    part_st = [sem(f"part_st{i}") for i in range(3)]
    stack_ld = [sem(f"stack_ld{i}") for i in range(3)]
    max_st = [sem(f"max_st{i}") for i in range(3)]
    max_ld = [sem(f"max_ld{i}") for i in range(3)]
    out_st = [sem(f"out_st{i}") for i in range(3)]
    STACK_DMAS = 10

    MISC = ["QK", "V", "E", "Y", "M"] if layer else ["QK", "V", "Y", "M"]
    LAG = {"QK": 1, "V": 0, "E": -2, "Y": -2, "M": 0}
    EVAC = {"QK": qk_evac, "V": v_evac, "E": e_evac, "Y": y_evac, "M": mt_evac}

    COUNT = {"QK": 2, "V": 3 if layer else 2, "E": 1, "Y": 1, "M": 1}

    def misc_free(eng, s, use):
        at = MISC.index(use)
        for back in range(0, -3, -1):
            for m in reversed(MISC[:at] if back == 0 else MISC):
                if s.has(back + LAG[m]):
                    eng.wait_ge(EVAC[m], COUNT[m] * (s.n(back + LAG[m]) + 1))
                    return

    def heads_of(kind, j):
        if layer == 0:
            return range(4 * (j // 2), 4 * (j // 2) + 4), j % 2, T
        if j < 4:
            return range(4 * j, 4 * j + 4), (1 if kind == "A" else 0), T
        return range(8 * (j - 4), 8 * (j - 4) + 8), (0 if kind == "A" else 1), P

    def emit(eng, body):
        body(Step(-1))
        body(Step(0))
        body(Step(1))
        body(Step(2))
        with eng.Fori(0, 4) as J:
            for r in range(3):
                body(Step(3 + r, J))
        for k in range(15, 18):
            body(Step(k))

    with nc.Block() as block:
        @block.sync
        def _(sp):
            def ahead(*counts):
                return [c if isinstance(c, int) else sp.snap(sp.to_reg(c)) for c in counts]

            def stacks(s):
                b = s.buf(1)
                made, stored, scored = ahead(s.n(1) + 1, 16 * (s.third(1) + 1), NU * (s.n(-2) + 1))
                sp.wait_ge(s3_done, made)
                sp.dma_start(v.parts_d[b].rearrange("a c p t -> p a c t"), qk3[:]).then_inc(part_st[b], 16)
                sp.wait_ge(part_st[b], stored)
                if s.has(-2):
                    sp.wait_ge(full["B"], scored)
                part = v.parts_d[b].rearrange("a c (d h) t -> a (c d) h t", d=HD)
                for row, n in ((0, 3), (3, 2), (5, 1)):
                    sp.dma_start(qs[8 * row:8 * (row + n), b], part[0, 0:8 * n]).then_inc(stack_ld[b], 16)
                for row, c in enumerate((0, 0, 0, 1, 1, 2)):
                    sp.dma_start(ks[8 * row:8 * row + 8, b], part[1, 8 * c:8 * c + 8]).then_inc(stack_ld[b], 16)
                sp.dma_start(qs[QROWS:QROWS + PARTS, b], v.zrow[:].unsqueeze(1).broadcast_to([PARTS, H, T])
                             ).then_inc(stack_ld[b], 16)

            def maxima(s):
                b = s.buf()
                turned, stored, scored = ahead(s.n() + 1, 16 * (s.third() + 1), NU * (s.n() + 1))
                sp.wait_ge(mt_evac, turned)
                sp.dma_start(v.max_d[b].rearrange("c t h p -> (c t h) p"), mT[:]).then_inc(max_st[b], 16)
                sp.wait_ge(max_st[b], stored)
                sp.wait_ge(full["A"], scored)
                for t in range(2):
                    sp.dma_start(qs[QROWS:QROWS + PARTS, b, :, P * t:P * t + P], v.max_d[b, :, t]
                                 ).then_inc(max_ld[b], 16)

            def body(s):
                if s.has(1):
                    stacks(s)
                if s.has():
                    maxima(s)

            emit(sp, body)
            for b in range(3):
                uses = len(range(b, B, 3))
                sp.wait_ge(max_ld[b], 32 * uses)
                if layer:
                    sp.wait_ge(out_st[b], 16 * uses)

        @block.gpsimd
        def _(pool):
            def body(s):
                if s.has(1):
                    b = s.buf(1)
                    pool.wait_ge(s1_done, s.n(1) + 1)
                    nc.gpsimd.tensor_tensor(qkr[:], qkf[:], qk3[:, :, 0, :], ALU.subtract).then_inc(r1_done, 1)
                    pool.wait_ge(s2_done, s.n(1) + 1)
                    nc.gpsimd.tensor_tensor(qk3[:, :, 2, :], qkr[:], qk3[:, :, 1, :],
                                            ALU.subtract).then_inc(s3_done, 1)

            emit(pool, body)

        @block.vector
        def _(dve):
            def maximum(s, j, slot):
                heads, t, w = heads_of("A", j)
                dve.wait_ge(full["A"], NU * s.n() + j + 1)
                nc.vector.tensor_reduce(mx[:, s.buf(), t, heads[0]:heads[-1] + 1],
                                        ring[:, slot].rearrange("p (h n) -> p h n", n=w), AX.X, ALU.max
                                        ).then_inc(used["A"], 1)

            def add_bias(s, j, slot):
                heads, c, _ = heads_of("B", j)
                off = P * (1 - c)
                dve.wait_ge(full["B"], NU * s.n(-1) + j + 1)
                if s.has(-2):
                    dve.wait_ge(pv_done, NU * s.n(-2) + j + 1)
                nc.vector.tensor_tensor(probs[:, j, :].rearrange("p (h n) -> p h n", n=T),
                                        ring[:, slot].rearrange("p (h n) -> p h n", n=T),
                                        v.tabB[:, heads[0]:heads[0] + 4, off:off + T], ALU.add).then_inc(used["B"], 1)

            def divide(s):
                b = s.buf(-2)
                dve.wait_ge(pv_done, NU * (s.n(-2) + 1))
                nc.vector.reciprocal(rden[:], od[:, T:2 * T]).then_inc(rd_done, 1)
                dve.wait_ge(rd_done, s.n(-2) + 1)
                if s.has(-3):
                    dve.wait_ge(y_full, s.n(-3) + 1)
                if layer == 0:
                    nc.vector.tensor_tensor(on[:], od[:, 0:T], rden[:], ALU.mult).then_inc(on_done, 1)
                else:
                    nc.vector.scalar_tensor_tensor(on[:], od[:, 0:T], cols[:, 5:6], rden[:], ALU.mult, ALU.mult
                                                   ).then_inc(on_done, 1)

            def add_shape(s):
                b = s.buf(-2)
                dve.wait_ge(e_full, s.n(-2) + 1)
                dve.wait_ge(on_done, s.n(-2) + 1)
                nc.vector.tensor_tensor(on[:], misc[:, 0:T], on[:], ALU.add).then_inc(e_evac, 1)

            def maximum_parts(s):
                m = mx[:, s.buf()]
                n = 4 * s.n()
                dve.wait_ge(used["A"], NU * (s.n() + 1))
                if s.has(-1):
                    dve.wait_ge(mt_full, s.n(-1) + 1)
                nc.vector.tensor_scalar(m3[:, 0], m, -1.0, None, ALU.mult).then_inc(max_parts, 1)
                dve.wait_ge(max_parts, n + 1)
                nc.vector.scalar_tensor_tensor(mres[:], m, -1.0, m3[:, 0], ALU.mult, ALU.subtract).then_inc(max_parts, 1)
                dve.wait_ge(max_parts, n + 2)
                nc.vector.tensor_copy(m3[:, 1], mres[:]).then_inc(max_parts, 1)
                dve.wait_ge(max_parts, n + 3)
                nc.vector.tensor_tensor(m3[:, 2], mres[:], m3[:, 1], ALU.subtract).then_inc(max_parts, 1)

            def project(s):
                y = yt[:].rearrange("p (c d) -> p c d", c=2)
                o = misc[:, 0:T].rearrange("p (c d) -> p c d", c=2)
                dve.wait_ge(y_full, s.n(-2) + 1)
                g = gate[:, bass.ds(s.n(-2) * 2, 2), :]
                xt = x[:, bass.ds(s.n(-2) * 2, 2), :]
                if layer == 0:
                    nc.vector.tensor_tensor(y, o, v.bo[:].unsqueeze(1).broadcast_to([P, 2, D]), ALU.add).then_inc(y_evac, 1)
                    dve.wait_ge(y_evac, s.n(-2) + 1)
                    nc.vector.tensor_tensor(y, y, g, ALU.mult).then_inc(y_done, 1)
                    dve.wait_ge(y_done, s.n(-2) + 1)
                    nc.vector.tensor_tensor(xt, xt, y, ALU.add).then_inc(fin_done, 1)
                else:
                    if s.has(-3):
                        dve.wait_ge(out_st[s.buf(-3)], 16 * (s.third(-3) + 1))
                    nc.vector.tensor_tensor(y, o, g, ALU.mult).then_inc(y_evac, 1)
                    dve.wait_ge(y_evac, s.n(-2) + 1)
                    nc.vector.tensor_tensor(y, xt, y, ALU.add).then_inc(fin_done, 1)

            def body(s):
                if s.has(-2):
                    divide(s)
                for pos, (kind, j) in enumerate(U.order):
                    if U.exists(s.k, kind):
                        (maximum if kind == "A" else add_bias if layer == 0 else lambda *a: None)(s, j, U.slot(s.k, pos))
                    if kind == "A" and j == NU - 1 and s.has():
                        maximum_parts(s)
                    if layer and pos == 4 and s.has(-2):
                        add_shape(s)
                    if pos == 7 and s.has(-2):
                        project(s)

            emit(dve, body)

        @block.scalar
        def _(act):
            def parts_one(s):
                b = s.buf(1)
                act.wait_ge(qk_full, s.n(1) + 1)
                if s.has():
                    act.wait_ge(s3_done, s.n() + 1)
                nc.scalar.activation(qkf[:, 0], misc[:, 0:T], ACT.Identity, bias=cols[:, bq:bq + 1], scale=QSCALE
                                     ).then_inc(qk_evac, 1)
                nc.scalar.activation(qkf[:, 1], misc[:, T:2 * T], ACT.Identity, bias=cols[:, bk:bk + 1]
                                     ).then_inc(qk_evac, 1)
                act.wait_ge(qk_evac, 2 * (s.n(1) + 1))
                if s.has():
                    act.wait_ge(part_st[s.buf()], 16 * (s.third() + 1))
                nc.scalar.activation(qk3[:, :, 0, :], qkf[:], ACT.Copy).then_inc(s1_done, 1)

            def parts_two(s):
                act.wait_ge(r1_done, s.n(1) + 1)
                nc.scalar.activation(qk3[:, :, 1, :], qkr[:], ACT.Copy).then_inc(s2_done, 1)

            def values(s):
                b = s.buf()
                act.wait_ge(v_full, s.n() + 1)
                if s.has(-3):
                    act.wait_ge(pv_done, NU * (s.n(-3) + 1))
                w = P if layer == 0 else 2 * P
                pv = misc[:, 0:2 * w].rearrange("p (c a n) -> p c a n", c=2, n=P)
                dst = vpad[:, b].rearrange("p c (i w) -> p c i w", w=40)
                for c in range(2):
                    nc.scalar.activation(dst[:, 4 * c:4 * c + 4, :, 0:HD],
                                               pv[:, c, 0, :].rearrange("p (q i d) -> p q i d", q=4, i=4), ACT.Copy
                                         ).then_inc(v_evac, 1)
                if layer:
                    if s.has(-3):
                        act.wait_ge(e_full, s.n(-3) + 1)
                    nc.scalar.activation(vcen[:, b], pv[:, :, 1, :], ACT.Copy).then_inc(v_evac, 1)

            def max_rows(s):
                b = s.buf()
                act.wait_ge(mt_full, s.n() + 1)
                if s.has(-1):
                    act.wait_ge(max_st[s.buf(-1)], 16 * (s.third(-1) + 1))
                nc.scalar.activation(mT[:], misc[0:PARTS * 2 * H, 0:P // 2].bitcast(BF16), ACT.Copy).then_inc(mt_evac, 1)

            def exponential(s, j, slot):
                if layer == 0:
                    act.wait_ge(used["B"], NU * s.n(-1) + j + 1)
                    nc.scalar.activation(probs[:, j, :], probs[:, j, :], ACT.Exp).then_inc(exp_done, 1)
                else:
                    act.wait_ge(full["B"], NU * s.n(-1) + j + 1)
                    if s.has(-2):
                        act.wait_ge(pv_done, NU * s.n(-2) + j + 1)
                    nc.scalar.activation(probs[:, j, :], ring[:, slot], ACT.Exp).then_inc(exp_done, 1)

            def store(s):
                b = s.buf(-2)
                act.wait_ge(fin_done, s.n(-2) + 1)
                act.dma_start(v.out[bass.ds(s.n(-2), 1)].rearrange("b (c p) d -> p (b c) d", p=P),
                             yt[:].rearrange("p (c d) -> p c d", c=2)).then_inc(out_st[b], 16)

            def body(s):
                if s.has():
                    if s.has(-1):
                        act.wait_ge(v_full, s.n(-1) + 1)
                    nc.scalar.activation(xb[:], xnT[:, bass.ds(s.n() * T, T)], ACT.Copy).then_inc(xb_done, 1)
                for pos, (kind, j) in enumerate(U.order):
                    if kind == "B" and U.exists(s.k, kind):
                        exponential(s, j, U.slot(s.k, pos))
                    if pos == 1 and s.has(1):
                        parts_one(s)
                    if pos == 4 and s.has(1):
                        parts_two(s)
                    if pos == 4 and s.has():
                        values(s)
                if layer and s.has(-2):
                    store(s)
                if s.has():
                    max_rows(s)

            emit(act, body)

        @block.tensor
        def _(pe):
            def batch_tokens(s, d):
                return xnT[:, bass.ds(s.n(d) * T, T)]

            def slot_free(s, pos):
                former = U.before(s.k, pos)
                if former:
                    kind, j, back = former
                    pe.wait_ge(used[kind], NU * s.n(back - (kind == "B")) + j + 1)

            def first_pass(s, pos, j):
                b, o = s.buf(), ring[:, U.slot(s.k, pos)]
                heads, t, w = heads_of("A", j)
                if j == 0:
                    pe.wait_ge(stack_ld[b], 16 * STACK_DMAS * (s.third() + 1))
                slot_free(s, pos)
                for n, h in enumerate(heads):
                    last = n == len(heads) - 1
                    q = qs[:, b, h, P * t:P * t + P]
                    at = o[:, w * n:w * n + w]
                    if layer == 0:
                        if n % 2 == 0:
                            off = P * (1 - t)
                            nc.tensor.matmul(o[:, T * n:T * n + 2 * T], eyeb[:], v.tabA[:, h:h + 2, off:off + T],
                                             start=True, stop=False, skip_group_check=True)
                        mm = nc.tensor.matmul(at, q, ks[:, b, h, :], start=False, stop=True, skip_group_check=True)
                    elif w == T:
                        nc.tensor.matmul(at, q, ks[:, b, h, :], start=(n % 2 == 0), stop=False, skip_group_check=True)
                        mm = nc.tensor.matmul(at[:, P:T], eyeb[:], maskA[:], start=False, stop=True, skip_group_check=True)
                    else:
                        if n % 4 == 0:
                            nc.tensor.matmul(o[:, P * n:P * n + 4 * P], eyeb[:], maskA[:].unsqueeze(1).broadcast_to([P, 4, P]),
                                             start=True, stop=False, skip_group_check=True)
                        mm = nc.tensor.matmul(at, q, ks[:, b, h, 0:P], start=False, stop=True, skip_group_check=True)
                    if last:
                        mm.then_inc(full["A"], 1)

            def second_pass(s, pos, j):
                b, o = s.buf(-1), ring[:, U.slot(s.k, pos)]
                heads, c, w = heads_of("B", j)
                if j == 0:
                    pe.wait_ge(max_ld[b], 32 * (s.third(-1) + 1))
                slot_free(s, pos)
                for n, h in enumerate(heads):
                    k = ks[:, b, h, P * c:P * c + P]
                    at = o[:, w * n:w * n + w]
                    if layer == 0:
                        mm = nc.tensor.matmul(at, k, qs[:, b, h, :], start=(n % 2 == 0), stop=True, skip_group_check=True)
                    elif w == T:
                        nc.tensor.matmul(at, k, qs[:, b, h, :], start=(n % 2 == 0), stop=False, skip_group_check=True)
                        mm = nc.tensor.matmul(at[:, 0:P], eyeb[:], maskB[:], start=False, stop=True, skip_group_check=True)
                    else:
                        if n % 4 == 0:
                            nc.tensor.matmul(o[:, P * n:P * n + 4 * P], eyeb[:], maskB[:].unsqueeze(1).broadcast_to([P, 4, P]),
                                             start=True, stop=False, skip_group_check=True)
                        mm = nc.tensor.matmul(at, k, qs[:, b, h, P:T], start=False, stop=True, skip_group_check=True)
                    if n == len(heads) - 1:
                        mm.then_inc(full["B"], 1)

            def values(s, d, j):
                b = s.buf(d)
                heads, c, w = heads_of("B", j)
                if j == 0:
                    pe.wait_ge(v_evac, COUNT["V"] * (s.n(d) + 1))
                    if s.has(d - 1):
                        pe.wait_ge(on_done, s.n(d - 1) + 1)
                pe.wait_ge(exp_done, NU * s.n(d) + j + 1)
                t0 = 0 if w == T else P
                for what in range(2):
                    for n, h in enumerate(heads):
                        i, q = h // 4, h % 4
                        lhs = vpad[:, b, 4 * c + q, 32 * i:32 * i + 32] if what == 0 else onespad[:, i, :]
                        mm = nc.tensor.matmul(od[32 * q:32 * q + 32, T * what + t0:T * what + T], lhs,
                                              probs[:, j, w * n:w * n + w], start=(j == 0 and what == 0 and i == 0),
                                              stop=(j == NU - 1), skip_group_check=True)
                mm.then_inc(pv_done, 1)

            def body(s):
                if s.has(-2):
                    values(s, -2, NU - 2)
                    values(s, -2, NU - 1)
                for pos, (kind, j) in enumerate(U.order):
                    if pos == 1 and s.has(1):
                        misc_free(pe, s, "QK")
                        for a in range(2):
                            mm = nc.tensor.matmul(misc[:, T * a:T * a + T], wqk[:, a, :], batch_tokens(s, 1),
                                                  start=True, stop=True)
                        mm.then_inc(qk_full, 1)
                    if pos == 4 and s.has():
                        misc_free(pe, s, "V")
                        pe.wait_ge(xb_done, s.n() + 1)
                        n = P if layer == 0 else 2 * P
                        w = v.wv0[:] if layer == 0 else v.wv1[:].rearrange("p a n -> p (a n)")
                        for c in range(2):
                            mm = nc.tensor.matmul(misc[:, n * c:n * c + n], xb[:, P * c:P * c + P], w,
                                                  start=True, stop=True)
                        mm.then_inc(v_full, 1)
                    if layer and pos == 5 and s.has(-2):
                        misc_free(pe, s, "E")
                        nc.tensor.matmul(misc[:, 0:T], v.wvs[:], batch_tokens(s, -2), start=True, stop=False,
                                         skip_group_check=True)
                        vc = vcen[:, s.buf(-2)]
                        nc.tensor.matmul(misc[:, 0:T], vc[:, 0], cst[:, C_UT:C_UT + T], start=False, stop=False,
                                         skip_group_check=True)
                        nc.tensor.matmul(misc[:, P:T], vc[:, 1], cst[:, C_UT + T + P:C_UT + 2 * T], start=False, stop=True,
                                         skip_group_check=True).then_inc(e_full, 1)
                    if pos == 7 and s.has(-2):
                        misc_free(pe, s, "Y")
                        pe.wait_ge(on_done, s.n(-2) + 1)
                        for c in range(2):
                            mm = nc.tensor.matmul(misc[:, D * c:D * c + D], on[:, P * c:P * c + P], wo[:],
                                                  start=True, stop=True)
                        mm.then_inc(y_full, 1)
                    if U.exists(s.k, kind):
                        (first_pass if kind == "A" else second_pass)(s, pos, j)
                    if kind == "B" and j >= 2 and s.has(-1):
                        values(s, -1, j - 2)
                if s.has():
                    misc_free(pe, s, "M")
                    pe.wait_ge(max_parts, 4 * (s.n() + 1))
                    nc.tensor.transpose(misc[0:PARTS * 2 * H, 0:P // 2].bitcast(BF16),
                                        m3[:].rearrange("p c t h -> p (c t h)"), eyeb[:]).then_inc(mt_full, 1)

            emit(pe, body)


_INS = ['L0_attn_x', 'L0_attn_w_qkv', 'L0_attn_b_qkv', 'L0_attn_w_out', 'L0_attn_b_out', 'L0_attn_w1_rpe',
        'L0_attn_b1_rpe', 'L0_attn_w2_rpe', 'L0_attn_b2_rpe', 'L0_ffn_router_weight', 'L0_ffn_router_bias',
        'L0_ffn_gate_up_proj', 'L0_ffn_gate_up_bias', 'L0_ffn_down_proj', 'L0_ffn_down_bias', 'L1_attn_qk_w',
        'L1_attn_qk_b', 'L1_attn_v_w', 'L1_attn_cproj_w', 'L1_attn_resid_gain', 'L1_attn_skip_gain',
        'L1_attn_centre_gain', 'L1_ffn_W', 'L1_ffn_b', 'L1_ffn_V_r', 'L1_ffn_C']


def _constants():
    import numpy as np
    c = np.zeros((P, C_ALL), np.float32)
    p = np.arange(P)[:, None]
    n = np.arange(P)[None, :]
    t = np.arange(T)[None, :]
    c[:, C_EYE:C_EYE + P] = p == n
    c[:, C_MA + P:C_MA + 2 * P] = np.where(n <= p, 0.0, NEG)
    c[:, C_MB:C_MB + P] = np.where(n >= p, 0.0, NEG)
    for h in range(2):
        c[:, C_UT + T * h:C_UT + T * h + T] = np.where(P * h + p <= t, np.float32(1.0) / (t + 1).astype(np.float32), 0.0)
    c[:, C_FLIP:C_FLIP + P] = p == P - 1 - n
    c[:, C_RANK:C_RANK + E] = E - np.arange(E)[None, :]
    r = np.arange(-T, T).astype(np.float32)
    f = (np.sign(r) * np.log1p(np.abs(r))).astype(np.float32)
    return c, np.concatenate([f, -f])[None, :].astype(np.float32)


def kernel(**inputs):
    import numpy as _np
    import concourse.bacc as _bacc
    from concourse import mybir as _mybir
    from concourse.bass_utils import run_bass_kernel_spmd as _run

    nc = _bacc.Bacc("TRN2", target_bir_lowering=False, num_devices=1)
    arrays, args = {}, []
    given = {name: inputs[name] for name in _INS}
    given["consts"], given["rel"] = _constants()
    for name, a in given.items():
        a = _np.ascontiguousarray(a)
        arrays[f"in_{name}_dram"] = a
        args.append(nc.dram_tensor(f"in_{name}_dram", a.shape, _mybir.dt.from_np(a.dtype), kind="ExternalInput").ap())
    shape = inputs["L0_attn_x"].shape
    args.append(nc.dram_tensor("out_0_dram", shape, _mybir.dt.float32, kind="ExternalOutput").ap())
    build(nc, *args)
    r = _run(nc, [arrays], core_ids=[0])
    return r.results[0]["out_0_dram"]
```

```python
from contextlib import ExitStack

import concourse.bass as bass
from concourse import mybir

ALU = mybir.AluOpType
ACT = mybir.ActivationFunctionType
F32 = mybir.dt.float32
BF16 = mybir.dt.bfloat16
U32 = mybir.dt.uint32
I32 = mybir.dt.int32
AX = mybir.AxisListType

P = 128
B, T, D = 16, 256, 128
H, HD = 16, 8
Q4 = 4
NT = B * T // P
E, I = 8, 256
TOPK = 2
G = 8
SLOT_TILES = NT * TOPK + E
RPE = 32
RANK = 32
ALPHA, LIMIT = 1.702, 7.0
EPS = 1e-5
QSCALE = float(HD) ** -0.5
NEG = -1.0e30
PARTS = 3
PAIRS = 6
QROWS = PAIRS * HD
REL = 512
TAB = 384
C_EYE, C_MA, C_MB = 0, P, 2 * P
C_UT = 3 * P
C_RANK = C_UT + T + P
C_FLIP = C_RANK + E
C_BEFORE = C_FLIP + 128
C_TILES = C_BEFORE + 128
C_ALL = C_TILES + NT + SLOT_TILES


W_LOADS, R_LOADS = 20, 5
PAIR_OF_ONES = float.fromhex("0x1.007f00p+0")


class Step:

    def __init__(self, k, J=0, period=3, count=B):
        self.k, self.J, self.period, self.count = k, J, period, count

    def n(self, d=0):
        return self.k + d + self.period * self.J

    def turn(self, d=0):
        return (self.k + d) // self.period + self.J

    def has(self, d=0):
        return 0 <= self.k + d < self.count

    def buf(self, d=0):
        return (self.k + d) % self.period


class Shared:
    pass


def build(nc, x_in, w_qkv, b_qkv, w_out, b_out, w1_rpe, b1_rpe, w2_rpe, b2_rpe, router_w, router_b,
          gu_w, gu_b, down_w, down_b, qk_w, qk_b, v_w, cproj_w, resid, skip, centre, f_w, f_b, f_v, f_c,
          consts, rel, out):
    with ExitStack() as ctx:
        def sb(name, shape, dt=F32):
            return ctx.enter_context(nc.sbuf_tensor(name, shape, dt))

        def sem(name):
            return ctx.enter_context(nc.semaphore(name))

        v = Shared()
        v.sem = sem
        v.x_in, v.w_qkv, v.b_qkv, v.w_out, v.b_out, v.w1_rpe = x_in, w_qkv, b_qkv, w_out, b_out, w1_rpe
        v.b1_rpe, v.w2_rpe, v.b2_rpe, v.router_w, v.router_b, v.gu_w = b1_rpe, w2_rpe, b2_rpe, router_w, router_b, gu_w
        v.gu_b, v.down_w, v.down_b, v.qk_w, v.qk_b, v.v_w = gu_b, down_w, down_b, qk_w, qk_b, v_w
        v.cproj_w, v.resid, v.skip, v.centre, v.f_w, v.f_b = cproj_w, resid, skip, centre, f_w, f_b
        v.f_v, v.f_c, v.consts, v.rel, v.out = f_v, f_c, consts, rel, out

        v.ps = ctx.enter_context(nc.psum_tensor("ps", [P, 8, 512], F32))

        v.x = sb("x", [P, NT, D])
        v.gate = sb("gate", [P, NT, D])
        v.xnT = sb("xnT", [P, NT * P])
        v.probs = sb("probs", [P, 8, 1024])
        v.qs = sb("qs", [P, 3, H, T], BF16)
        v.ks = sb("ks", [P, 3, H, T], BF16)
        v.tabB = sb("tabB", [P, H, TAB])
        v.tabA = sb("tabA", [P, H, TAB], BF16)
        v.vpad = sb("vpad", [P, 3, 8, 160])
        v.onespad = sb("onespad", [P, 4, 32])
        v.cst = sb("cst", [P, C_ALL])
        v.eyeb = sb("eyeb", [P, P], BF16)
        v.maskA = sb("maskA", [P, P], BF16)
        v.maskB = sb("maskB", [P, P], BF16)
        v.wqk0 = sb("wqk0", [P, 2, P])
        v.wqk1 = sb("wqk1", [P, 2, P])
        v.wv0 = sb("wv0", [P, P])
        v.wv1 = sb("wv1", [P, 2, P])
        v.wvs = sb("wvs", [P, P])
        v.wo0 = sb("wo0", [P, D])
        v.wo1 = sb("wo1", [P, D])
        v.bo = sb("bo", [P, D])
        v.cols = sb("cols", [P, 8])
        v.rwT = sb("rwT", [P, E])
        v.rb = sb("rb", [1, 4 * E])
        v.ones = sb("ones", [1, P])
        v.feff = sb("feff", [P, D])
        v.fb = sb("fb", [1, D])
        v.wt = sb("wt", [P, TOPK, NT])
        v.place = sb("place", [P, TOPK, NT], U32)
        v.owner = sb("owner", [1, SLOT_TILES], I32)
        v.xb = sb("xb", [P, T])
        v.qkf = sb("qkf", [P, 2, T])
        v.qkr = sb("qkr", [P, 2, T])
        v.qk3 = sb("qk3", [P, 2, PARTS, T], BF16)
        v.mx = sb("mx", [P, 3, 2, H])
        v.mres = sb("mres", [P, 2, H])
        v.m3 = sb("m3", [P, PARTS, 2, H], BF16)
        v.mT = sb("mT", [PARTS * 2 * H, P], BF16)
        v.rden = sb("rden", [P, T])
        v.on = sb("on", [P, T])
        v.yt = sb("yt", [P, T])
        v.stat = sb("stat", [P, 4, NT])
        v.zrow = sb("zrow", [PARTS, T], BF16)
        v.eps = sb("eps", [P, 1])

        tabs = v.tabB[:, :, :].rearrange("p h u -> p (h u)")
        v.wgu = tabs[:, 0:E * 2 * I].rearrange("p (e n) -> p e n", e=E)
        v.wdn = tabs[:, E * 2 * I:E * 3 * I].rearrange("p (e c n) -> p e c n", e=E, c=2)
        v.squares = v.probs[:, 6:8, :].rearrange("p a b -> p (a b)").rearrange("p (t d) -> p t d", d=D)
        v.vcen = v.tabA[:, 0:6, 0:256].bitcast(F32).rearrange("p (b c) n -> p b c n", c=2)
        v.scratch = v.probs[:, 0:6, :].rearrange("p a b -> p (a b)")

        v.bias_f = nc.dram_tensor("bias_f", (H, REL), F32, kind="Internal")
        v.bias_r = nc.dram_tensor("bias_r", (H, REL), BF16, kind="Internal")
        v.parts_d = nc.dram_tensor("parts_d", (3, 2, PARTS, P, T), BF16, kind="Internal")
        v.bias3_d = nc.dram_tensor("bias3_d", (PARTS, 5 * E, P), BF16, kind="Internal")
        v.slots_in = nc.dram_tensor("slots_in", (SLOT_TILES * P, D), F32, kind="Internal")
        v.slots_out = nc.dram_tensor("slots_out", (SLOT_TILES * P, D), F32, kind="Internal")
        v.max_d = nc.dram_tensor("max_d", (3, PARTS, 2, H, P), BF16, kind="Internal")

        setup(nc, v)
        attention(nc, v, 0)
        experts(nc, v)
        middle(nc, v)
        attention(nc, v, 1)


def setup(nc, v):
    sem = v.sem
    ps, cst, x, gate, xnT, stat = v.ps, v.cst, v.x, v.gate, v.xnT, v.stat
    at = [0]

    def take(n, rows=P):
        at[0] += n
        assert at[0] <= v.scratch.shape[1]
        return v.scratch[0:rows, at[0] - n:at[0]]

    hid, relb = take(2 * REL, RPE + 1), take(2 * REL, RPE)
    w2, w2p, rpc = take(H, RPE + 1), take(H, RPE + 1), take(2, RPE)
    bfw, brv = take(REL, H), take(REL // 2, H).bitcast(BF16)
    wqkv, wqk = take(3 * P), take(2 * P)
    rows = take(6 * P, 1).rearrange("p (a b) -> p a b", b=P)
    rowsp = take(6 * P, 1).rearrange("p (a b) -> p a b", b=P)
    gains = take(3 * H).rearrange("p (a h) -> p a h", h=H)
    bor, bvb, fw = take(P, 1), take(P), take(P)
    fv, fc, fvT, fcT, rw = take(RANK), take(RANK), take(P, RANK), take(P, RANK), take(P, E)
    flipb = take(P // 2).bitcast(BF16)
    zero = take(D)
    b40 = v.qkf[0:5 * E, 0, 0:P]
    b3 = v.qk3[0:5 * E, 0, :, 0:P]
    ones128 = fw
    rt = v.scratch[:, 0:7 * NT * E].rearrange("p (k t e) -> p k t e", k=7, e=E)
    small = v.scratch[:, 7 * NT * E:7 * NT * E + 4 * NT + 3 * E]
    eye = cst[:, C_EYE:C_EYE + P]
    flip = cst[:, C_FLIP:C_FLIP + P]
    tabs = (v.tabA[:].rearrange("p h u -> p (h u)"), v.tabB[:].rearrange("p h u -> p (h u)"))
    NB = H * TAB // 512

    c_load = sem("su_consts")
    x_load = sem("su_x")
    r_load = sem("su_rpe")
    w_load = sem("su_weights")
    copied = sem("su_copied")
    hidden = sem("su_hidden")
    bias_mm = sem("su_bias_mm")
    bias_cp = sem("su_bias_cp")
    bias_st = sem("su_bias_stored")
    tab_ld = [sem("su_tab_a"), sem("su_tab_b")]
    tab_mm, tab_cp = sem("su_tab_mm"), sem("su_tab_cp")
    small_mm = sem("su_small_mm")
    small_cp = sem("su_small_cp")
    zeroed = sem("su_zeroed")
    cleared = sem("su_cleared")
    zero_tile = sem("su_zero_tile")
    ln, sq, rs = sem("su_ln"), sem("su_sq"), sem("su_rs")
    tr, trc, lg = sem("su_tr"), sem("su_trc"), sem("su_lg")
    ro = sem("su_ro")
    chosen, counted = sem("su_chosen"), sem("su_counted")
    gaps, ex = sem("su_gaps"), sem("su_ex")
    eb_load, eb_parts = sem("su_expert_biases"), sem("su_expert_bias_parts")

    with nc.Block() as block:
        def routing(dve):
            L, cand, one1, L2, one2, both, ew = (rt[:, k] for k in range(7))
            m1, m2, rk, gap = (small[:, NT * k:NT * k + NT] for k in range(4))
            cnt, tiles, ends = (small[:, 4 * NT + E * k:4 * NT + E * k + E] for k in range(3))
            rank = cst[:, C_RANK:C_RANK + E].unsqueeze(1).broadcast_to([P, NT, E])
            steps = [0]

            def step(ins):
                ins.then_inc(ro, 1)
                steps[0] += 1
                dve.wait_ge(ro, steps[0])

            def wide(a):
                return a.unsqueeze(2).broadcast_to([P, NT, E])

            def pick(src, m, hot):
                step(nc.vector.tensor_reduce(m, src, AX.X, ALU.max))
                step(nc.vector.tensor_tensor(cand, src, wide(m), ALU.is_equal))
                step(nc.vector.tensor_tensor(cand, cand, rank, ALU.mult))
                step(nc.vector.tensor_reduce(rk, cand, AX.X, ALU.max))
                step(nc.vector.tensor_tensor(hot, cand, wide(rk), ALU.is_equal))

            dve.wait_ge(lg, G)
            step(nc.vector.tensor_copy(L, ps[:, 7, 0:NT * E].rearrange("p (t e) -> p t e", e=E)))
            pick(L, m1, one1)
            step(nc.vector.scalar_tensor_tensor(L2, one1, -3.0e38, L, ALU.mult, ALU.add))
            pick(L2, m2, one2)
            nc.vector.tensor_tensor(both, one1, one2, ALU.add).then_inc(chosen, 1)
            nc.vector.tensor_tensor(ew, L, wide(m1), ALU.subtract).then_inc(gaps, 1)
            nc.vector.tensor_tensor(gap, m2, m1, ALU.subtract).then_inc(gaps, 1)
            dve.wait_ge(counted, 1)
            run = L2
            for e in range(E):
                step(nc.vector.tensor_tensor_scan(run[:, :, e], ones128[:, 0:NT], ps[:, 1, e:NT * E:E], 0.0, ALU.mult, ALU.add))
            step(nc.vector.tensor_copy(cnt, run[:, NT - 1, :]))
            more = cand.rearrange("p t e -> p (t e)").rearrange("p (e t) -> p e t", e=E)
            step(nc.vector.tensor_tensor(more, cnt.unsqueeze(2).broadcast_to([P, E, NT]),
                                         cst[:, C_TILES:C_TILES + NT].unsqueeze(1).broadcast_to([P, E, NT]), ALU.is_gt))
            step(nc.vector.tensor_reduce(tiles, more, AX.X, ALU.add))
            step(nc.vector.tensor_tensor_scan(ends, ones128[:, 0:E], tiles, 0.0, ALU.mult, ALU.add))
            step(nc.vector.tensor_tensor(tiles, ends, tiles, ALU.subtract))
            step(nc.vector.tensor_tensor(run, run, ps[:, 1, 0:NT * E].rearrange("p (t e) -> p t e", e=E), ALU.subtract))
            step(nc.vector.tensor_tensor(run, run, ps[:, 0, 0:NT * E].rearrange("p (t e) -> p t e", e=E), ALU.add))
            step(nc.vector.scalar_tensor_tensor(run, tiles.unsqueeze(1).broadcast_to([P, NT, E]), float(P), run,
                                                ALU.mult, ALU.add))
            for k, hot in enumerate((one1, one2)):
                step(nc.vector.tensor_tensor(cand, hot, run, ALU.mult))
                step(nc.vector.tensor_reduce(m1, cand, AX.X, ALU.add))
                step(nc.vector.tensor_copy(v.place[:, k, :], m1))
            own = one1.rearrange("p t e -> p (t e)")[0:1, 0:SLOT_TILES]
            step(nc.vector.tensor_scalar(own, cst[0:1, C_TILES + NT:C_ALL], ends[0:1, 0:1], None, ALU.is_ge))
            for e in range(1, E - 1):
                step(nc.vector.scalar_tensor_tensor(own, cst[0:1, C_TILES + NT:C_ALL], ends[0:1, e:e + 1], own,
                                                    ALU.is_ge, ALU.add))
            step(nc.vector.tensor_copy(v.owner[:], own))
            dve.wait_ge(ex, 2)
            step(nc.vector.tensor_reduce(m2, ew, AX.X, ALU.add))
            step(nc.vector.reciprocal(v.wt[:, 0, :], m2))
            step(nc.vector.tensor_tensor(v.wt[:, 1, :], v.wt[:, 0, :], gap, ALU.mult))

        @block.sync
        def _(sp):
            for half in range(2):
                sp.dma_start(x[:, 16 * half:16 * half + 16, :],
                             v.x_in[8 * half:8 * half + 8].rearrange("b (c p) d -> p (b c) d", p=P)).then_inc(x_load, 16)
            sp.dma_start(cst[:, :], v.consts[:, :]).then_inc(c_load, 16)
            rpe = [
                (relb, v.rel[0, :].partition_broadcast(RPE)),
                (w2[0:RPE, :], v.w2_rpe[:, :]),
                (w2[RPE:RPE + 1, :], v.b2_rpe.rearrange("(a n) -> a n", a=1)),
                (rpc[:, 0:1], v.w1_rpe.rearrange("a k -> k a")),
                (rpc[:, 1:2], v.b1_rpe.rearrange("(k a) -> k a", a=1)),
            ]
            for dst, src in rpe:
                sp.dma_start(dst, src).then_inc(r_load, 16)
            loads = [
                (wqkv, v.w_qkv[:, :]),
                (wqk, v.qk_w[:, :]),
                (v.wv1[:, 0, :], v.v_w[:, :]),
                (v.wo0[:, :], v.w_out[:, :]),
                (v.wo1[:, :], v.cproj_w[:, :]),
                (rows[:, 0:3, :], v.b_qkv.rearrange("(o a n) -> o a n", o=1, a=3)),
                (rows[:, 3:5, :], v.qk_b.rearrange("(o a n) -> o a n", o=1, a=2)),
                (gains[:, 0, :], v.resid[0, :, 0, 0].partition_broadcast(P)),
                (gains[:, 1, :], v.skip[0, :, 0, 0].partition_broadcast(P)),
                (gains[:, 2, :], v.centre[0, :, 0, 0].partition_broadcast(P)),
                (bor, v.b_out.rearrange("(a n) -> a n", a=1)),
                (fw, v.f_w[:, :]),
                (fv, v.f_v[:, :]),
                (fc, v.f_c[:, :]),
                (v.fb[:, :], v.f_b.rearrange("(a n) -> a n", a=1)),
                (rw, v.router_w[:, :]),
            ] + [(v.rb[:, E * c:E * c + E], v.router_b.rearrange("(a n) -> a n", a=1)) for c in range(4)]
            for dst, src in loads:
                sp.dma_start(dst, src).then_inc(w_load, 16)
            sp.dma_start(b40[0:4 * E, :], v.gu_b.rearrange("e (j n) -> (e j) n", n=P)).then_inc(eb_load, 16)
            sp.dma_start(b40[4 * E:5 * E, :], v.down_b[:, :]).then_inc(eb_load, 16)
            assert len(loads) == W_LOADS and len(rpe) == R_LOADS
            sp.wait_ge(bias_cp, 2)
            sp.dma_start(v.bias_r[:, :], brv).then_inc(bias_st, 16)
            sp.dma_start(v.bias_f[:, :], bfw).then_inc(bias_st, 16)
            sp.wait_ge(bias_st, 32)
            for i, src in enumerate((v.bias_r, v.bias_f)):
                sp.dma_start((v.tabA, v.tabB)[i][:], bass.AP(src, 1, [[1, P], [REL, H], [1, TAB]])).then_inc(tab_ld[i], 16)
            sp.wait_ge(eb_parts, 5)
            sp.dma_start(v.bias3_d[:].rearrange("c r n -> r c n"), b3[:]).then_inc(eb_load, 16)
            sp.wait_ge(eb_load, 48)
            sp.wait_ge(zero_tile, 1)
            sp.dma_start(v.slots_in[:, :].rearrange("(t p) d -> p t d", p=P),
                         zero.unsqueeze(1).broadcast_to([P, SLOT_TILES, D])).then_inc(cleared, 16)
            sp.wait_ge(cleared, 16)

        @block.gpsimd
        def _(pool):
            nc.gpsimd.memset(v.zrow[:], 0.0).then_inc(zeroed, 1)
            for buf in range(3):
                nc.gpsimd.memset(v.qs[:, buf].bitcast(F32), 0.0).then_inc(zeroed, 1)
                nc.gpsimd.memset(v.ks[:, buf].bitcast(F32), 0.0).then_inc(zeroed, 1)
            nc.gpsimd.memset(v.vpad[:], 0.0).then_inc(zeroed, 1)
            nc.gpsimd.memset(v.onespad[:], 0.0).then_inc(zeroed, 1)
            pool.wait_ge(zeroed, 9)
            for i in range(4):
                nc.gpsimd.memset(v.onespad[:, i, 8 * i:8 * i + 8], 1.0).then_inc(zeroed, 1)
            pool.wait_ge(zeroed, 13)
            nc.gpsimd.memset(v.ks[32:64].rearrange("p b h t -> p (b h t)").bitcast(F32), PAIR_OF_ONES).then_inc(zeroed, 1)

        @block.vector
        def _(dve):
            nc.vector.memset(v.eps[:], EPS).then_inc(ln, 1)
            nc.vector.memset(zero, 0.0).then_inc(zero_tile, 1)
            nc.vector.memset(v.ones[:], 1.0).then_inc(copied, 1)
            nc.vector.memset(hid[RPE:RPE + 1, :], 1.0).then_inc(copied, 1)
            dve.wait_ge(r_load, 16 * R_LOADS)
            nc.vector.tensor_scalar(hid[0:RPE, :], relb, rpc[:, 0:1], rpc[:, 1:2], ALU.mult, ALU.add).then_inc(hidden, 1)
            dve.wait_ge(hidden, 1)
            nc.vector.tensor_scalar(hid[0:RPE, :], hid[0:RPE, :], 0.0, None, ALU.max).then_inc(hidden, 1)
            for i in range(4):
                nc.vector.tensor_copy(w2p[:, 4 * i:4 * i + 4], w2[:, i:H:4]).then_inc(hidden, 1)
            dve.wait_ge(c_load, 16)
            nc.vector.tensor_copy(v.eyeb[:], eye).then_inc(copied, 1)
            nc.vector.tensor_copy(v.maskA[:], cst[:, C_MA:C_MA + P]).then_inc(copied, 1)
            nc.vector.tensor_copy(v.maskB[:], cst[:, C_MB:C_MB + P]).then_inc(copied, 1)
            nc.vector.tensor_copy(flipb, flip).then_inc(copied, 1)
            dve.wait_ge(bias_mm, 2)
            nc.vector.tensor_copy(brv, ps[0:H, 1, :]).then_inc(bias_cp, 1)
            nc.vector.tensor_copy(bfw, ps[0:H, 0, :]).then_inc(bias_cp, 1)
            layernorm_vector(nc, dve, v, ln, sq, rs, x_load)
            dve.wait_ge(w_load, 16 * W_LOADS)
            for src, dst in ((wqkv, v.wqk0), (wqk, v.wqk1)):
                for a in range(2):
                    nc.vector.tensor_copy(dst[:, a, :].rearrange("p (d i q) -> p d i q", d=HD, i=4),
                                          src[:, P * a:P * a + P].rearrange("p (q i d) -> p d i q", q=4, i=4)
                                          ).then_inc(copied, 1)
            for a in (0, 1, 3, 4):
                nc.vector.tensor_copy(rowsp[:, a, :].rearrange("p (d i q) -> p d i q", d=HD, i=4),
                                      rows[:, a, :].rearrange("p (q i d) -> p d i q", q=4, i=4)).then_inc(copied, 1)
            nc.vector.tensor_copy(rowsp[:, 2, :], rows[:, 2, :]).then_inc(copied, 1)
            nc.vector.tensor_copy(rowsp[:, 5, :].rearrange("p (h d) -> p h d", d=HD),
                                  gains[0:1, 0, :].unsqueeze(2).broadcast_to([1, H, HD])).then_inc(copied, 1)
            nc.vector.tensor_copy(v.wv0[:], wqkv[:, 2 * P:3 * P]).then_inc(copied, 1)
            vw = v.wv1[:, 0, :].rearrange("p (h d) -> p h d", d=HD)
            nc.vector.tensor_tensor(v.wvs[:].rearrange("p (h d) -> p h d", d=HD), vw,
                                    gains[:, 1, :].unsqueeze(2).broadcast_to([P, H, HD]), ALU.mult).then_inc(copied, 1)
            nc.vector.scalar_tensor_tensor(v.wv1[:, 1, :].rearrange("p (h d) -> p h d", d=HD), vw, -1.0,
                                           gains[:, 2, :].unsqueeze(2).broadcast_to([P, H, HD]),
                                           ALU.mult, ALU.mult).then_inc(copied, 1)
            dve.wait_ge(eb_load, 32)
            for c in range(PARTS):
                nc.vector.tensor_copy(b3[:, c, :], b40[:]).then_inc(eb_parts, 1)
                if c < PARTS - 1:
                    dve.wait_ge(eb_parts, 2 * c + 1)
                    nc.vector.tensor_tensor(b40[:], b40[:], b3[:, c, :], ALU.subtract).then_inc(eb_parts, 1)
                    dve.wait_ge(eb_parts, 2 * c + 2)
            dve.wait_ge(small_mm, 1)
            nc.vector.tensor_copy(v.rwT[:], ps[:, 2, 8:8 + E]).then_inc(small_cp, 1)
            nc.vector.tensor_scalar(v.cols[:, 0:1], ps[:, 2, 0:1], QSCALE, None, ALU.mult).then_inc(small_cp, 1)
            nc.vector.tensor_copy(v.cols[:, 1:3], ps[:, 2, 1:3]).then_inc(small_cp, 1)
            nc.vector.tensor_scalar(v.cols[:, 3:4], ps[:, 2, 3:4], QSCALE, None, ALU.mult).then_inc(small_cp, 1)
            nc.vector.tensor_copy(v.cols[:, 4:6], ps[:, 2, 4:6]).then_inc(small_cp, 1)
            nc.vector.tensor_copy(fvT, ps[0:RANK, 2, 128:256]).then_inc(small_cp, 1)
            nc.vector.tensor_copy(fcT, ps[0:RANK, 2, 256:384]).then_inc(small_cp, 1)
            dve.wait_ge(small_cp, 7)
            nc.vector.tensor_copy(bvb, v.cols[:, 2:3].broadcast_to([P, P])).then_inc(small_cp, 1)
            dve.wait_ge(small_mm, 2)
            nc.vector.tensor_copy(v.bo[:], ps[:, 3, 0:P]).then_inc(small_cp, 1)
            nc.vector.tensor_copy(v.feff[:], ps[:, 3, P:2 * P]).then_inc(small_cp, 1)
            nc.vector.memset(ones128, 1.0).then_inc(small_cp, 1)
            routing(dve)

        @block.scalar
        def _(act):
            layernorm_scalar(nc, act, v, ln, sq, rs)
            for g in range(G):
                act.wait_ge(tr, g + 1)
                nc.scalar.activation(xnT[:, 512 * g:512 * g + 512], ps[:, 4 + g % 2, :], ACT.Copy).then_inc(trc, 1)
            for k in range(2 * NB):
                act.wait_ge(tab_mm, k + 1)
                n = k % NB
                nc.scalar.activation(tabs[k // NB][:, 512 * n:512 * n + 512], ps[:, 4 + k % 3, :], ACT.Copy).then_inc(tab_cp, 1)
                if k == 2 * NB - 8:
                    act.wait_ge(gaps, 2)
                    ew, gap = rt[:, 6], small[:, 3 * NT:4 * NT]
                    nc.scalar.activation(ew, ew, ACT.Exp).then_inc(ex, 1)
                    nc.scalar.activation(gap, gap, ACT.Exp).then_inc(ex, 1)

        @block.tensor
        def _(pe):
            pe.wait_ge(copied, 2)
            pe.wait_ge(hidden, 6)
            for k in range(2):
                nc.tensor.matmul(ps[0:H, k, :], w2p, hid[:, REL * k:REL * k + REL], start=True, stop=True).then_inc(bias_mm, 1)
            pe.wait_ge(c_load, 16)
            for g in range(G):
                if g >= 2:
                    pe.wait_ge(trc, g - 1)
                pe.wait_ge(ln, layernorm_ready(g))
                for c in range(4):
                    mm = nc.tensor.transpose(ps[:, 4 + g % 2, P * c:P * c + P], gate[:, 4 * g + c, :], eye)
                mm.then_inc(tr, 1)
            pe.wait_ge(copied, 2 + 4 + 13)
            for k in range(6):
                nc.tensor.matmul(ps[:, 2, k:k + 1], rowsp[:, k, :], v.ones[0:1, 0:1], start=True, stop=True)
            nc.tensor.transpose(ps[:, 2, 8:8 + E], rw, eye[0:E, 0:E])
            nc.tensor.matmul(ps[0:RANK, 2, 128:256], fv, eye, start=True, stop=True)
            nc.tensor.matmul(ps[0:RANK, 2, 256:384], fc, eye, start=True, stop=True).then_inc(small_mm, 1)
            pe.wait_ge(small_cp, 1)
            for g in range(G):
                pe.wait_ge(trc, g + 1)
                nc.tensor.matmul(ps[:, 7, 32 * g:32 * g + 32], v.ones[0:1, 0:P], v.rb[:], start=(g == 0), stop=False,
                                 skip_group_check=True)
                for c in range(4):
                    t = 4 * g + c
                    mm = nc.tensor.matmul(ps[:, 7, E * t:E * t + E], xnT[:, P * t:P * t + P], v.rwT[:],
                                          start=False, stop=True, skip_group_check=True)
                mm.then_inc(lg, 1)
            pe.wait_ge(small_cp, 8)
            nc.tensor.matmul(ps[:, 3, 0:P], bvb, v.wo0[:], start=True, stop=False)
            nc.tensor.matmul(ps[:, 3, 0:P], v.ones[0:1, 0:P], bor, start=False, stop=True)
            nc.tensor.matmul(ps[:, 3, P:2 * P], fw, eye, start=True, stop=False)
            nc.tensor.matmul(ps[:, 3, P:2 * P], fvT, fcT, start=False, stop=True).then_inc(small_mm, 1)
            for k in range(2 * NB):
                if k % NB == 0:
                    pe.wait_ge(tab_ld[k // NB], 16)
                if k >= 3:
                    pe.wait_ge(tab_cp, k - 2)
                n = k % NB
                nc.tensor.matmul(ps[:, 4 + k % 3, :], flipb if k < NB else flip, tabs[k // NB][:, 512 * n:512 * n + 512],
                                 start=True, stop=True).then_inc(tab_mm, 1)
                if k == NB:
                    pe.wait_ge(chosen, 1)
                    both = rt[:, 5].rearrange("p t e -> p (t e)")
                    nc.tensor.matmul(ps[:, 0, 0:NT * E], cst[:, C_BEFORE:C_BEFORE + P], both, start=True, stop=True)
                    nc.tensor.matmul(ps[:, 1, 0:NT * E], ones128, both, start=True, stop=True).then_inc(counted, 1)


def layernorm_ready(g):
    return 7 if g < G // 2 else 13


def layernorm_vector(nc, dve, v, ln, sq, rs, x_load=None):
    for half in range(2):
        a = slice(16 * half, 16 * half + 16)
        xh, gh = v.x[:, a, :], v.gate[:, a, :]
        s, var, r, m = (v.stat[:, k, a] for k in range(4))
        n = 6 * half + 1
        if x_load is not None:
            dve.wait_ge(x_load, 16 * (half + 1))
        nc.vector.tensor_reduce(s, xh, AX.X, ALU.add).then_inc(ln, 1)
        dve.wait_ge(ln, n + 1)
        nc.vector.tensor_scalar(m, s, 1.0 / D, None, ALU.mult).then_inc(ln, 1)
        dve.wait_ge(ln, n + 2)
        nc.vector.tensor_tensor(gh, xh, m.unsqueeze(2).broadcast_to([P, 16, D]), ALU.subtract).then_inc(ln, 1)
        dve.wait_ge(sq, half + 1)
        nc.vector.tensor_reduce(var, v.squares, AX.X, ALU.add).then_inc(ln, 1)
        dve.wait_ge(rs, half + 1)
        nc.vector.reciprocal(r, r).then_inc(ln, 1)
        dve.wait_ge(ln, n + 5)
        nc.vector.tensor_tensor(gh, gh, r.unsqueeze(2).broadcast_to([P, 16, D]), ALU.mult).then_inc(ln, 1)


def layernorm_scalar(nc, act, v, ln, sq, rs):
    for half in range(2):
        a = slice(16 * half, 16 * half + 16)
        act.wait_ge(ln, 6 * half + 4)
        nc.scalar.activation(v.squares, v.gate[:, a, :], ACT.Square).then_inc(sq, 1)
        act.wait_ge(ln, 6 * half + 5)
        nc.scalar.activation(v.stat[:, 2, a], v.stat[:, 1, a], ACT.Sqrt, bias=v.eps[:, 0:1], scale=1.0 / D).then_inc(rs, 1)


def pipeline(eng, body, first, loop, rounds, last, period, count):
    for k in range(first, loop):
        body(Step(k, 0, period, count))
    with eng.Fori(0, rounds) as J:
        for r in range(period):
            body(Step(loop + r, J, period, count))
    for k in range(loop + period * rounds, last + 1):
        body(Step(k, 0, period, count))


def experts(nc, v):
    sem = v.sem
    ps, cst, wgu, wdn = v.ps, v.cst, v.wgu, v.wdn
    eye = cst[:, C_EYE:C_EYE + P]
    at = [0]

    def take(n):
        at[0] += n
        return v.probs[:].rearrange("p a b -> p (a b)")[:, at[0] - n:at[0]]

    xg = take(4 * P).rearrange("p (b n) -> p b n", b=4)
    xgT = take(2 * P).rearrange("p (b n) -> p b n", b=2)
    gt, up, sg, gl, ac, acT = (take(2 * I).rearrange("p (b n) -> p b n", b=2) for _ in range(6))
    yo = take(4 * D).rearrange("p (b n) -> p b n", b=4)
    onesb = take(P // 2).bitcast(BF16)
    biases = v.tabA[:].rearrange("p h u -> p (h u)")[:, 0:5 * E * P]
    gub = biases[:, 0:4 * E * P].rearrange("p (e n) -> p e n", e=E)
    dnb = biases[:, 4 * E * P:5 * E * P].rearrange("p (e n) -> p e n", e=E)

    w_load, b_zero, b_load = sem("ex_weights"), sem("ex_bias_zero"), sem("ex_biases")
    x_load = [sem(f"ex_x{i}") for i in range(4)]
    y_store = [sem(f"ex_y{i}") for i in range(4)]
    x_full, x_evac = sem("ex_x_full"), sem("ex_x_evac")
    gu_full = sem("ex_gu_full")
    clipped = sem("ex_clipped")
    sig = sem("ex_sig")
    glu = sem("ex_glu")
    a_done = sem("ex_a_done")
    a_full, a_evac = sem("ex_a_full"), sem("ex_a_evac")
    dn_full, y_evac = sem("ex_dn_full"), sem("ex_y_evac")

    def run(eng, body):
        pipeline(eng, body, -1, 7, 16, SLOT_TILES + 2, 4, SLOT_TILES)

    with nc.Block() as block:
        @block.sync
        def _(sp):
            sp.dma_start(wgu, v.gu_w.rearrange("e h n -> h e n")).then_inc(w_load, 16)
            sp.dma_start(wdn, v.down_w.rearrange("e (c i) h -> i e c h", c=2)).then_inc(w_load, 16)
            sp.wait_ge(b_zero, 2)
            sp.dma_start(biases[0:PARTS, :], v.bias3_d[:].rearrange("c r n -> c (r n)")).then_inc(b_load, 16)

            def body(s):
                if s.has(1):
                    b = s.buf(1)
                    if s.has(-3):
                        read = s.n(-3) + 1
                        sp.wait_ge(x_full, read if isinstance(read, int) else sp.snap(sp.to_reg(read)))
                    sp.dma_start(xg[:, b, :], v.slots_in[bass.ds(s.n(1) * P, P), :]).then_inc(x_load[b], 16)

            run(sp, body)

        @block.tensor
        def _(pe):
            def expert(s, d):
                return nc.tensor.value_load(v.owner[0:1, bass.ds(s.n(d), 1)], min_val=0, max_val=E - 1)

            def body(s):
                if s.has(1):
                    b = s.buf(1)
                    pe.wait_ge(x_load[b], 16 * (s.turn(1) + 1))
                    if s.has(-1):
                        pe.wait_ge(x_evac, s.n(-1) + 1)
                    nc.tensor.transpose(ps[:, 2 + b % 2, 0:P], xg[:, b, :], eye).then_inc(x_full, 1)
                if s.has(-2):
                    b = s.buf(-2) % 2
                    pe.wait_ge(a_done, s.n(-2) + 1)
                    if s.has(-4):
                        pe.wait_ge(a_evac, s.n(-4) + 1)
                    for c in range(2):
                        mm = nc.tensor.transpose(ps[:, 4 + b, P * c:P * c + P], ac[:, b, P * c:P * c + P], eye)
                    mm.then_inc(a_full, 1)
                if s.has():
                    b = s.buf() % 2
                    e = expert(s, 0)
                    if s.k == 0:
                        pe.wait_ge(w_load, 32)
                        pe.wait_ge(b_load, 16)
                    pe.wait_ge(x_evac, s.n() + 1)
                    if s.has(-2):
                        pe.wait_ge(clipped, 2 * (s.n(-2) + 1))
                    nc.tensor.matmul(ps[:, b, :], xgT[:, b, :], wgu[:, bass.ds(e, 1), :].rearrange("p a n -> p (a n)"),
                                     start=True, stop=False)
                    nc.tensor.matmul(ps[:, b, :], onesb, gub[:, bass.ds(e, 1), :].rearrange("p a n -> p (a n)"),
                                     start=False, stop=True).then_inc(gu_full, 1)
                if s.has(-3):
                    b = s.buf(-3) % 2
                    e = expert(s, -3)
                    pe.wait_ge(a_evac, s.n(-3) + 1)
                    if s.has(-5):
                        pe.wait_ge(y_evac, s.n(-5) + 1)
                    o = ps[:, 6 + b, 0:D]
                    for c in range(2):
                        nc.tensor.matmul(o, acT[:, b, P * c:P * c + P],
                                         wdn[:, bass.ds(e, 1), c, :].rearrange("p a n -> p (a n)"), start=(c == 0), stop=False)
                    nc.tensor.matmul(o, onesb, dnb[:, bass.ds(e, 1), :].rearrange("p a n -> p (a n)"),
                                     start=False, stop=True).then_inc(dn_full, 1)

            run(pe, body)

        @block.scalar
        def _(act):
            def body(s):
                if s.has(1):
                    b = s.buf(1) % 2
                    act.wait_ge(x_full, s.n(1) + 1)
                    if s.has(-1):
                        act.wait_ge(gu_full, s.n(-1) + 1)
                    nc.scalar.activation(xgT[:, b, :], ps[:, 2 + b, 0:P], ACT.Copy).then_inc(x_evac, 1)
                if s.has(-2):
                    b = s.buf(-2) % 2
                    act.wait_ge(a_full, s.n(-2) + 1)
                    if s.has(-4):
                        act.wait_ge(dn_full, s.n(-4) + 1)
                    nc.scalar.activation(acT[:, b, :], ps[:, 4 + b, 0:I], ACT.Copy).then_inc(a_evac, 1)
                if s.has():
                    b = s.buf() % 2
                    act.wait_ge(clipped, 2 * s.n() + 1)
                    if s.has(-2):
                        act.wait_ge(glu, s.n(-2) + 1)
                    nc.scalar.activation(sg[:, b, :], gt[:, b, :], ACT.Sigmoid, scale=ALPHA).then_inc(sig, 1)
                if s.has(-3):
                    act.wait_ge(y_evac, s.n(-3) + 1)
                    act.dma_start(v.slots_out[bass.ds(s.n(-3) * P, P), :], yo[:, s.buf(-3), :]).then_inc(y_store[s.buf(-3)], 16)

            run(act, body)
            for b in range(4):
                act.wait_ge(y_store[b], 16 * (SLOT_TILES // 4))

        @block.vector
        def _(dve):
            nc.vector.memset(biases.bitcast(F32), 0.0).then_inc(b_zero, 1)
            nc.vector.memset(onesb, 1.0).then_inc(b_zero, 1)

            def body(s):
                if s.has(-1):
                    b = s.buf(-1) % 2
                    dve.wait_ge(glu, s.n(-1) + 1)
                    dve.wait_ge(clipped, 2 * (s.n(-1) + 1))
                    if s.has(-3):
                        dve.wait_ge(a_full, s.n(-3) + 1)
                    nc.vector.scalar_tensor_tensor(ac[:, b, :], up[:, b, :], 1.0, gl[:, b, :], ALU.add, ALU.mult
                                                   ).then_inc(a_done, 1)
                if s.has():
                    b = s.buf() % 2
                    dve.wait_ge(gu_full, s.n() + 1)
                    if s.has(-2):
                        dve.wait_ge(glu, s.n(-2) + 1)
                        dve.wait_ge(a_done, s.n(-2) + 1)
                    nc.vector.tensor_scalar(gt[:, b, :], ps[:, b, 0:I], LIMIT, None, ALU.min).then_inc(clipped, 1)
                    nc.vector.tensor_scalar(up[:, b, :], ps[:, b, I:2 * I], LIMIT, -LIMIT, ALU.min, ALU.max
                                            ).then_inc(clipped, 1)
                if s.has(-3):
                    dve.wait_ge(dn_full, s.n(-3) + 1)
                    if s.has(-7):
                        dve.wait_ge(y_store[s.buf(-7)], 16 * (s.turn(-7) + 1))
                    nc.vector.tensor_copy(yo[:, s.buf(-3), :], ps[:, 6 + s.buf(-3) % 2, 0:D]).then_inc(y_evac, 1)

            run(dve, body)

        @block.gpsimd
        def _(pool):
            def body(s):
                if s.has():
                    b = s.buf() % 2
                    pool.wait_ge(sig, s.n() + 1)
                    if s.has(-2):
                        pool.wait_ge(a_done, s.n(-2) + 1)
                    nc.gpsimd.tensor_tensor(gl[:, b, :], gt[:, b, :], sg[:, b, :], ALU.mult).then_inc(glu, 1)

            run(pool, body)


def middle(nc, v):
    sem = v.sem
    ps, gate, x, xnT, cst, stat = v.ps, v.gate, v.x, v.xnT, v.cst, v.stat
    eye = cst[:, C_EYE:C_EYE + P]
    flat = v.probs[:].rearrange("p a b -> p (a b)")
    ys = flat[:, 0:2048].rearrange("p (g k n) -> p g k n", g=2, k=TOPK)
    sgm = flat[:, 2048:3072].rearrange("p (g n) -> p g n", g=2)
    sqr = flat[:, 3072:4096].rearrange("p (g n) -> p g n", g=2)
    got = [sem("mi_gathered0"), sem("mi_gathered1")]
    mix, s1 = sem("mi_mix"), sem("mi_sigmoid")
    res, sqd, sqt, nrm = sem("mi_residual"), sem("mi_squares"), sem("mi_sqrt"), sem("mi_normalise")
    tr, trc, fm, s2, gd = sem("mi_tr"), sem("mi_trc"), sem("mi_ffn"), sem("mi_ffn_sigmoid"), sem("mi_gate")
    eps_set = sem("mi_eps")

    def tiles(a, g):
        return a[:, 4 * g:4 * g + 4, :]

    def four(a):
        return a.rearrange("p (t d) -> p t d", d=D)

    with nc.Block() as block:
        @block.gpsimd
        def _(pool):
            for g in range(G):
                if g >= 2:
                    pool.wait_ge(res, 6 * (g - 1))
                for k in range(TOPK):
                    for c in range(4):
                        nc.gpsimd.indirect_dma_start(ys[:, g % 2, k, D * c:D * c + D], None, v.slots_out[:, :],
                                                     bass.IndirectOffsetOnAxis(ap=v.place[:, k, 4 * g + c:4 * g + c + 1], axis=0)
                                                     ).then_inc(got[g % 2], 16)

        @block.vector
        def _(dve):
            nc.vector.memset(v.eps[:], EPS).then_inc(eps_set, 1)

            def weigh(g):
                dve.wait_ge(got[g % 2], 16 * 8 * (g // 2 + 1))
                n = 3 * g
                for k in range(TOPK):
                    y = four(ys[:, g % 2, k])
                    nc.vector.tensor_tensor(y, y, v.wt[:, k, 4 * g:4 * g + 4].unsqueeze(2).broadcast_to([P, 4, D]), ALU.mult
                                            ).then_inc(mix, 1)
                dve.wait_ge(mix, n + 2)
                nc.vector.tensor_tensor(ys[:, g % 2, 0], ys[:, g % 2, 0], ys[:, g % 2, 1], ALU.add).then_inc(mix, 1)

            def residual(g):
                y, n = ys[:, g % 2, 0], 6 * g
                dve.wait_ge(s1, g + 1)
                nc.vector.tensor_tensor(y, y, sgm[:, g % 2], ALU.mult).then_inc(res, 1)
                dve.wait_ge(res, n + 1)
                nc.vector.tensor_tensor(four(y), four(y), tiles(gate, g), ALU.mult).then_inc(res, 1)
                dve.wait_ge(res, n + 2)
                nc.vector.tensor_tensor(tiles(x, g), tiles(x, g), four(y), ALU.add).then_inc(res, 1)
                dve.wait_ge(res, n + 3)
                nc.vector.tensor_reduce(stat[:, 0, 4 * g:4 * g + 4], tiles(x, g), AX.X, ALU.add).then_inc(res, 1)
                dve.wait_ge(res, n + 4)
                nc.vector.tensor_scalar(stat[:, 3, 4 * g:4 * g + 4], stat[:, 0, 4 * g:4 * g + 4], 1.0 / D, None, ALU.mult
                                        ).then_inc(res, 1)
                dve.wait_ge(res, n + 5)
                nc.vector.tensor_tensor(tiles(gate, g), tiles(x, g),
                                        stat[:, 3, 4 * g:4 * g + 4].unsqueeze(2).broadcast_to([P, 4, D]), ALU.subtract
                                        ).then_inc(res, 1)

            def variance(g):
                dve.wait_ge(sqd, g + 1)
                nc.vector.tensor_reduce(stat[:, 1, 4 * g:4 * g + 4], four(sqr[:, g % 2]), AX.X, ALU.add).then_inc(nrm, 1)

            def normalise(g):
                r = stat[:, 2, 4 * g:4 * g + 4]
                dve.wait_ge(sqt, g + 1)
                nc.vector.reciprocal(r, r).then_inc(nrm, 1)
                dve.wait_ge(nrm, 3 * g + 2)
                nc.vector.tensor_tensor(tiles(gate, g), tiles(gate, g), r.unsqueeze(2).broadcast_to([P, 4, D]), ALU.mult
                                        ).then_inc(nrm, 1)

            def silu(g):
                dve.wait_ge(s2, g + 1)
                nc.vector.tensor_tensor(tiles(gate, g), four(ps[:, 4 + g % 4, :]), tiles(gate, g), ALU.mult).then_inc(gd, 1)

            for g in range(G + 3):
                if g < G:
                    weigh(g)
                if g < G:
                    residual(g)
                    variance(g)
                if g >= 3:
                    silu(g - 3)
                if g < G:
                    normalise(g)

        @block.scalar
        def _(act):
            act.wait_ge(eps_set, 1)
            for g in range(G + 3):
                if g < G:
                    act.wait_ge(mix, 3 * g + 3)
                    nc.scalar.activation(sgm[:, g % 2], ys[:, g % 2, 0], ACT.Sigmoid).then_inc(s1, 1)
                if g >= 3:
                    act.wait_ge(fm, g - 2)
                    nc.scalar.activation(tiles(gate, g - 3), four(ps[:, 4 + (g - 3) % 4, :]), ACT.Sigmoid).then_inc(s2, 1)
                if g < G:
                    act.wait_ge(res, 6 * g + 6)
                    nc.scalar.activation(four(sqr[:, g % 2]), tiles(gate, g), ACT.Square).then_inc(sqd, 1)
                    act.wait_ge(nrm, 3 * g + 1)
                    nc.scalar.activation(stat[:, 2, 4 * g:4 * g + 4], stat[:, 1, 4 * g:4 * g + 4], ACT.Sqrt,
                                         bias=v.eps[:, 0:1], scale=1.0 / D).then_inc(sqt, 1)
                if 1 <= g <= G:
                    act.wait_ge(tr, g)
                    nc.scalar.activation(xnT[:, 512 * g - 512:512 * g], ps[:, (g - 1) % 4, :], ACT.Copy).then_inc(trc, 1)

        @block.tensor
        def _(pe):
            def ffn(g):
                pe.wait_ge(trc, g + 1)
                if g >= 4:
                    pe.wait_ge(gd, g - 3)
                for c in range(4):
                    t = 4 * g + c
                    o = ps[:, 4 + g % 4, D * c:D * c + D]
                    nc.tensor.matmul(o, v.ones[0:1, 0:P], v.fb[:], start=(c == 0), stop=False, skip_group_check=True)
                    mm = nc.tensor.matmul(o, xnT[:, P * t:P * t + P], v.feff[:], start=False, stop=True,
                                          skip_group_check=True)
                mm.then_inc(fm, 1)

            for g in range(G):
                pe.wait_ge(nrm, 3 * g + 3)
                if g >= 4:
                    pe.wait_ge(trc, g - 3)
                for c in range(4):
                    mm = nc.tensor.transpose(ps[:, g % 4, P * c:P * c + P], gate[:, 4 * g + c, :], eye)
                mm.then_inc(tr, 1)
                if g >= 1:
                    ffn(g - 1)
            ffn(G - 1)

class Units:

    def __init__(self, count):
        self.count = count
        self.order = [("A", 0), ("A", 1), ("A", 2)]
        for j in range(count - 3):
            self.order += [("B", j), ("A", j + 3)]
        self.order += [("B", j) for j in range(count - 3, count)]

    def exists(self, k, kind):
        return 0 <= (k if kind == "A" else k - 1) < B

    def slot(self, k, pos):
        return (len(self.order) * k + pos) % 3

    def before(self, k, pos):
        n = len(self.order) * k + pos - 3
        while n >= 0:
            kk, p = divmod(n, len(self.order))
            kind, j = self.order[p]
            if self.exists(kk, kind):
                return kind, j, kk - k
            n -= 3
        return None


def attention(nc, v, layer):
    U = Units(8 if layer == 0 else 6)
    NU = U.count
    ps, x, gate, xnT, probs, qs, ks = v.ps, v.x, v.gate, v.xnT, v.probs, v.qs, v.ks
    cst, vpad, onespad, cols, xb, vcen = v.cst, v.vpad, v.onespad, v.cols, v.xb, v.vcen
    qkf, qkr, qk3, mx, mres, m3, mT = v.qkf, v.qkr, v.qk3, v.mx, v.mres, v.m3, v.mT
    rden, on, yt, eyeb, maskA, maskB = v.rden, v.on, v.yt, v.eyeb, v.maskA, v.maskB
    wqk, wo = (v.wqk0, v.wo0) if layer == 0 else (v.wqk1, v.wo1)
    bq, bk = (0, 1) if layer == 0 else (3, 4)
    ring = ps[:, 0:6, :].rearrange("p (s b) n -> p s (b n)", s=3)
    od = ps[:, 6, :]
    misc = ps[:, 7, :]

    def sem(name):
        return v.sem(f"l{layer}_{name}")

    full = {"A": sem("a_full"), "B": sem("b_full")}
    used = {"A": sem("a_used"), "B": sem("b_used")}
    exp_done = sem("exp_done") if layer == 0 else used["B"]
    pv_done = sem("pv_done")
    qk_full, v_full, e_full = sem("qk_full"), sem("v_full"), sem("e_full")
    y_full, mt_full = sem("y_full"), sem("mt_full")
    qk_evac, v_evac, e_evac = sem("qk_evac"), sem("v_evac"), sem("e_evac")
    y_evac, mt_evac = sem("y_evac"), sem("mt_evac")
    s1_done, r1_done, s2_done, s3_done = sem("s1"), sem("r1"), sem("s2"), sem("s3")
    xb_done = sem("xb")
    max_parts = sem("max_parts")
    rd_done, on_done = sem("rd"), sem("on")
    y_done, fin_done = sem("y"), sem("fin")
    part_st = [sem(f"part_st{i}") for i in range(3)]
    stack_ld = [sem(f"stack_ld{i}") for i in range(3)]
    max_st = [sem(f"max_st{i}") for i in range(3)]
    max_ld = [sem(f"max_ld{i}") for i in range(3)]
    out_st = [sem(f"out_st{i}") for i in range(3)]
    sorted_in = sem("sorted_in")
    STACK_DMAS = 10

    MISC = ["QK", "V", "E", "Y", "M"] if layer else ["QK", "V", "Y", "M"]
    LAG = {"QK": 1, "V": 0, "E": -2, "Y": -2, "M": 0}
    EVAC = {"QK": qk_evac, "V": v_evac, "E": e_evac, "Y": y_evac, "M": mt_evac}

    COUNT = {"QK": 2, "V": 3 if layer else 2, "E": 1, "Y": 1, "M": 1}

    def misc_free(eng, s, use):
        at = MISC.index(use)
        for back in range(0, -3, -1):
            for m in reversed(MISC[:at] if back == 0 else MISC):
                if s.has(back + LAG[m]):
                    eng.wait_ge(EVAC[m], COUNT[m] * (s.n(back + LAG[m]) + 1))
                    return

    def heads_of(kind, j):
        if layer == 0:
            return range(4 * (j // 2), 4 * (j // 2) + 4), j % 2, T
        if j < 4:
            return range(4 * j, 4 * j + 4), (1 if kind == "A" else 0), T
        return range(8 * (j - 4), 8 * (j - 4) + 8), (0 if kind == "A" else 1), P

    def emit(eng, body):
        pipeline(eng, body, -1, 3, 4, B + 1, 3, B)

    with nc.Block() as block:
        @block.sync
        def _(sp):
            def ahead(*counts):
                return [c if isinstance(c, int) else sp.snap(sp.to_reg(c)) for c in counts]

            def stacks(s):
                b = s.buf(1)
                made, stored, scored = ahead(s.n(1) + 1, 16 * (s.turn(1) + 1), NU * (s.n(-2) + 1))
                sp.wait_ge(s3_done, made)
                sp.dma_start(v.parts_d[b].rearrange("a c p t -> p a c t"), qk3[:]).then_inc(part_st[b], 16)
                sp.wait_ge(part_st[b], stored)
                if s.has(-2):
                    sp.wait_ge(full["B"], scored)
                part = v.parts_d[b].rearrange("a c (d h) t -> a (c d) h t", d=HD)
                for row, n in ((0, 3), (3, 2), (5, 1)):
                    sp.dma_start(qs[8 * row:8 * (row + n), b], part[0, 0:8 * n]).then_inc(stack_ld[b], 16)
                for row, c in enumerate((0, 0, 0, 1, 1, 2)):
                    sp.dma_start(ks[8 * row:8 * row + 8, b], part[1, 8 * c:8 * c + 8]).then_inc(stack_ld[b], 16)
                sp.dma_start(qs[QROWS:QROWS + PARTS, b], v.zrow[:].unsqueeze(1).broadcast_to([PARTS, H, T])
                             ).then_inc(stack_ld[b], 16)

            def maxima(s):
                b = s.buf()
                turned, stored, scored = ahead(s.n() + 1, 16 * (s.turn() + 1), NU * (s.n() + 1))
                sp.wait_ge(mt_evac, turned)
                sp.dma_start(v.max_d[b].rearrange("c t h p -> (c t h) p"), mT[:]).then_inc(max_st[b], 16)
                sp.wait_ge(max_st[b], stored)
                sp.wait_ge(full["A"], scored)
                for t in range(2):
                    sp.dma_start(qs[QROWS:QROWS + PARTS, b, :, P * t:P * t + P], v.max_d[b, :, t]
                                 ).then_inc(max_ld[b], 16)

            def body(s):
                if s.has(1):
                    stacks(s)
                if s.has():
                    maxima(s)

            emit(sp, body)
            for b in range(3):
                uses = len(range(b, B, 3))
                sp.wait_ge(max_ld[b], 32 * uses)
                if layer:
                    sp.wait_ge(out_st[b], 16 * uses)

        def rest_one(eng, ops, s):
            eng.wait_ge(s1_done, s.n(1) + 1)
            ops.tensor_tensor(qkr[:], qkf[:], qk3[:, :, 0, :], ALU.subtract).then_inc(r1_done, 1)

        def rest_two(eng, ops, s):
            eng.wait_ge(s2_done, s.n(1) + 1)
            ops.tensor_tensor(qk3[:, :, 2, :], qkr[:], qk3[:, :, 1, :], ALU.subtract).then_inc(s3_done, 1)

        @block.gpsimd
        def _(pool):
            if layer == 0:
                for t in range(NT):
                    for k in range(TOPK):
                        nc.gpsimd.indirect_dma_start(v.slots_in[:, :],
                                                     bass.IndirectOffsetOnAxis(ap=v.place[:, k, t:t + 1], axis=0),
                                                     gate[:, t, :], None).then_inc(sorted_in, 16)
                pool.wait_ge(sorted_in, 16 * TOPK * NT)
            else:
                def body(s):
                    if s.has(1):
                        rest_one(pool, nc.gpsimd, s)
                        rest_two(pool, nc.gpsimd, s)

                emit(pool, body)

        @block.vector
        def _(dve):
            def maximum(s, j, slot):
                heads, t, w = heads_of("A", j)
                dve.wait_ge(full["A"], NU * s.n() + j + 1)
                nc.vector.tensor_reduce(mx[:, s.buf(), t, heads[0]:heads[-1] + 1],
                                        ring[:, slot].rearrange("p (h n) -> p h n", n=w), AX.X, ALU.max
                                        ).then_inc(used["A"], 1)

            def add_bias(s, j, slot):
                heads, c, _ = heads_of("B", j)
                off = P * (1 - c)
                dve.wait_ge(full["B"], NU * s.n(-1) + j + 1)
                if s.has(-2):
                    dve.wait_ge(pv_done, NU * s.n(-2) + j + 1)
                nc.vector.tensor_tensor(probs[:, j, :].rearrange("p (h n) -> p h n", n=T),
                                        ring[:, slot].rearrange("p (h n) -> p h n", n=T),
                                        v.tabB[:, heads[0]:heads[0] + 4, off:off + T], ALU.add).then_inc(used["B"], 1)

            def divide(s):
                b = s.buf(-2)
                dve.wait_ge(pv_done, NU * (s.n(-2) + 1))
                nc.vector.reciprocal(rden[:], od[:, T:2 * T]).then_inc(rd_done, 1)
                dve.wait_ge(rd_done, s.n(-2) + 1)
                if s.has(-3):
                    dve.wait_ge(y_full, s.n(-3) + 1)
                if layer == 0:
                    nc.vector.tensor_tensor(on[:], od[:, 0:T], rden[:], ALU.mult).then_inc(on_done, 1)
                else:
                    nc.vector.scalar_tensor_tensor(on[:], od[:, 0:T], cols[:, 5:6], rden[:], ALU.mult, ALU.mult
                                                   ).then_inc(on_done, 1)

            def add_shape(s):
                b = s.buf(-2)
                dve.wait_ge(e_full, s.n(-2) + 1)
                dve.wait_ge(on_done, s.n(-2) + 1)
                nc.vector.tensor_tensor(on[:], misc[:, 0:T], on[:], ALU.add).then_inc(e_evac, 1)

            def maximum_parts(s):
                m = mx[:, s.buf()]
                n = 4 * s.n()
                dve.wait_ge(used["A"], NU * (s.n() + 1))
                if s.has(-1):
                    dve.wait_ge(mt_full, s.n(-1) + 1)
                nc.vector.tensor_scalar(m3[:, 0], m, -1.0, None, ALU.mult).then_inc(max_parts, 1)
                dve.wait_ge(max_parts, n + 1)
                nc.vector.scalar_tensor_tensor(mres[:], m, -1.0, m3[:, 0], ALU.mult, ALU.subtract).then_inc(max_parts, 1)
                dve.wait_ge(max_parts, n + 2)
                nc.vector.tensor_copy(m3[:, 1], mres[:]).then_inc(max_parts, 1)
                dve.wait_ge(max_parts, n + 3)
                nc.vector.tensor_tensor(m3[:, 2], mres[:], m3[:, 1], ALU.subtract).then_inc(max_parts, 1)

            def project(s):
                y = yt[:].rearrange("p (c d) -> p c d", c=2)
                o = misc[:, 0:T].rearrange("p (c d) -> p c d", c=2)
                dve.wait_ge(y_full, s.n(-2) + 1)
                g = gate[:, bass.ds(s.n(-2) * 2, 2), :]
                if layer == 0:
                    if s.k == 2:
                        dve.wait_ge(sorted_in, 16 * TOPK * NT)
                    nc.vector.tensor_tensor(g, o, v.bo[:].unsqueeze(1).broadcast_to([P, 2, D]), ALU.add).then_inc(y_evac, 1)
                else:
                    xt = x[:, bass.ds(s.n(-2) * 2, 2), :]
                    if s.has(-3):
                        dve.wait_ge(out_st[s.buf(-3)], 16 * (s.turn(-3) + 1))
                    nc.vector.tensor_tensor(y, o, g, ALU.mult).then_inc(y_evac, 1)
                    dve.wait_ge(y_evac, s.n(-2) + 1)
                    nc.vector.tensor_tensor(y, xt, y, ALU.add).then_inc(fin_done, 1)

            def body(s):
                if s.has(-2):
                    divide(s)
                for pos, (kind, j) in enumerate(U.order):
                    if U.exists(s.k, kind):
                        (maximum if kind == "A" else add_bias if layer == 0 else lambda *a: None)(s, j, U.slot(s.k, pos))
                    if kind == "A" and j == NU - 1 and s.has():
                        maximum_parts(s)
                    if layer and pos == 4 and s.has(-2):
                        add_shape(s)
                    if layer == 0 and s.has(1):
                        if pos == 1:
                            rest_one(dve, nc.vector, s)
                        if pos == 4:
                            rest_two(dve, nc.vector, s)
                    if pos == 7 and s.has(-2):
                        project(s)

            emit(dve, body)

        @block.scalar
        def _(act):
            def parts_one(s):
                b = s.buf(1)
                act.wait_ge(qk_full, s.n(1) + 1)
                if s.has():
                    act.wait_ge(s3_done, s.n() + 1)
                nc.scalar.activation(qkf[:, 0], misc[:, 0:T], ACT.Identity, bias=cols[:, bq:bq + 1], scale=QSCALE
                                     ).then_inc(qk_evac, 1)
                nc.scalar.activation(qkf[:, 1], misc[:, T:2 * T], ACT.Identity, bias=cols[:, bk:bk + 1]
                                     ).then_inc(qk_evac, 1)
                act.wait_ge(qk_evac, 2 * (s.n(1) + 1))
                if s.has():
                    act.wait_ge(part_st[s.buf()], 16 * (s.turn() + 1))
                nc.scalar.activation(qk3[:, :, 0, :], qkf[:], ACT.Copy).then_inc(s1_done, 1)

            def parts_two(s):
                act.wait_ge(r1_done, s.n(1) + 1)
                nc.scalar.activation(qk3[:, :, 1, :], qkr[:], ACT.Copy).then_inc(s2_done, 1)

            def values(s):
                b = s.buf()
                act.wait_ge(v_full, s.n() + 1)
                if s.has(-3):
                    act.wait_ge(pv_done, NU * (s.n(-3) + 1))
                w = P if layer == 0 else 2 * P
                pv = misc[:, 0:2 * w].rearrange("p (c a n) -> p c a n", c=2, n=P)
                dst = vpad[:, b].rearrange("p c (i w) -> p c i w", w=40)
                for c in range(2):
                    nc.scalar.activation(dst[:, 4 * c:4 * c + 4, :, 0:HD],
                                               pv[:, c, 0, :].rearrange("p (q i d) -> p q i d", q=4, i=4), ACT.Copy
                                         ).then_inc(v_evac, 1)
                if layer:
                    if s.has(-3):
                        act.wait_ge(e_full, s.n(-3) + 1)
                    nc.scalar.activation(vcen[:, b], pv[:, :, 1, :], ACT.Copy).then_inc(v_evac, 1)

            def max_rows(s):
                b = s.buf()
                act.wait_ge(mt_full, s.n() + 1)
                if s.has(-1):
                    act.wait_ge(max_st[s.buf(-1)], 16 * (s.turn(-1) + 1))
                nc.scalar.activation(mT[:], misc[0:PARTS * 2 * H, 0:P // 2].bitcast(BF16), ACT.Copy).then_inc(mt_evac, 1)

            def exponential(s, j, slot):
                if layer == 0:
                    act.wait_ge(used["B"], NU * s.n(-1) + j + 1)
                    nc.scalar.activation(probs[:, j, :], probs[:, j, :], ACT.Exp).then_inc(exp_done, 1)
                else:
                    act.wait_ge(full["B"], NU * s.n(-1) + j + 1)
                    if s.has(-2):
                        act.wait_ge(pv_done, NU * s.n(-2) + j + 1)
                    nc.scalar.activation(probs[:, j, :], ring[:, slot], ACT.Exp).then_inc(exp_done, 1)

            def store(s):
                b = s.buf(-2)
                act.wait_ge(fin_done, s.n(-2) + 1)
                act.dma_start(v.out[bass.ds(s.n(-2), 1)].rearrange("b (c p) d -> p (b c) d", p=P),
                             yt[:].rearrange("p (c d) -> p c d", c=2)).then_inc(out_st[b], 16)

            def body(s):
                if s.has():
                    if s.has(-1):
                        act.wait_ge(v_full, s.n(-1) + 1)
                    nc.scalar.activation(xb[:], xnT[:, bass.ds(s.n() * T, T)], ACT.Copy).then_inc(xb_done, 1)
                for pos, (kind, j) in enumerate(U.order):
                    if kind == "B" and U.exists(s.k, kind):
                        exponential(s, j, U.slot(s.k, pos))
                    if pos == 1 and s.has(1):
                        parts_one(s)
                    if pos == 4 and s.has(1):
                        parts_two(s)
                    if pos == 4 and s.has():
                        values(s)
                if layer and s.has(-2):
                    store(s)
                if s.has():
                    max_rows(s)

            emit(act, body)

        @block.tensor
        def _(pe):
            def batch_tokens(s, d):
                return xnT[:, bass.ds(s.n(d) * T, T)]

            def slot_free(s, pos):
                former = U.before(s.k, pos)
                if former:
                    kind, j, back = former
                    pe.wait_ge(used[kind], NU * s.n(back - (kind == "B")) + j + 1)

            def first_pass(s, pos, j):
                b, o = s.buf(), ring[:, U.slot(s.k, pos)]
                heads, t, w = heads_of("A", j)
                if j == 0:
                    pe.wait_ge(stack_ld[b], 16 * STACK_DMAS * (s.turn() + 1))
                slot_free(s, pos)
                for n, h in enumerate(heads):
                    last = n == len(heads) - 1
                    q = qs[:, b, h, P * t:P * t + P]
                    at = o[:, w * n:w * n + w]
                    if layer == 0:
                        if n % 2 == 0:
                            off = P * (1 - t)
                            nc.tensor.matmul(o[:, T * n:T * n + 2 * T], eyeb[:], v.tabA[:, h:h + 2, off:off + T],
                                             start=True, stop=False, skip_group_check=True)
                        mm = nc.tensor.matmul(at, q, ks[:, b, h, :], start=False, stop=True, skip_group_check=True)
                    elif w == T:
                        nc.tensor.matmul(at, q, ks[:, b, h, :], start=(n % 2 == 0), stop=False, skip_group_check=True)
                        mm = nc.tensor.matmul(at[:, P:T], eyeb[:], maskA[:], start=False, stop=True, skip_group_check=True)
                    else:
                        if n % 4 == 0:
                            nc.tensor.matmul(o[:, P * n:P * n + 4 * P], eyeb[:], maskA[:].unsqueeze(1).broadcast_to([P, 4, P]),
                                             start=True, stop=False, skip_group_check=True)
                        mm = nc.tensor.matmul(at, q, ks[:, b, h, 0:P], start=False, stop=True, skip_group_check=True)
                    if last:
                        mm.then_inc(full["A"], 1)

            def second_pass(s, pos, j):
                b, o = s.buf(-1), ring[:, U.slot(s.k, pos)]
                heads, c, w = heads_of("B", j)
                if j == 0:
                    pe.wait_ge(max_ld[b], 32 * (s.turn(-1) + 1))
                slot_free(s, pos)
                for n, h in enumerate(heads):
                    k = ks[:, b, h, P * c:P * c + P]
                    at = o[:, w * n:w * n + w]
                    if layer == 0:
                        mm = nc.tensor.matmul(at, k, qs[:, b, h, :], start=(n % 2 == 0), stop=True, skip_group_check=True)
                    elif w == T:
                        nc.tensor.matmul(at, k, qs[:, b, h, :], start=(n % 2 == 0), stop=False, skip_group_check=True)
                        mm = nc.tensor.matmul(at[:, 0:P], eyeb[:], maskB[:], start=False, stop=True, skip_group_check=True)
                    else:
                        if n % 4 == 0:
                            nc.tensor.matmul(o[:, P * n:P * n + 4 * P], eyeb[:], maskB[:].unsqueeze(1).broadcast_to([P, 4, P]),
                                             start=True, stop=False, skip_group_check=True)
                        mm = nc.tensor.matmul(at, k, qs[:, b, h, P:T], start=False, stop=True, skip_group_check=True)
                    if n == len(heads) - 1:
                        mm.then_inc(full["B"], 1)

            def values(s, d, j):
                b = s.buf(d)
                heads, c, w = heads_of("B", j)
                if j == 0:
                    pe.wait_ge(v_evac, COUNT["V"] * (s.n(d) + 1))
                    if s.has(d - 1):
                        pe.wait_ge(on_done, s.n(d - 1) + 1)
                pe.wait_ge(exp_done, NU * s.n(d) + j + 1)
                t0 = 0 if w == T else P
                for what in range(2):
                    for n, h in enumerate(heads):
                        i, q = h // 4, h % 4
                        lhs = vpad[:, b, 4 * c + q, 32 * i:32 * i + 32] if what == 0 else onespad[:, i, :]
                        mm = nc.tensor.matmul(od[32 * q:32 * q + 32, T * what + t0:T * what + T], lhs,
                                              probs[:, j, w * n:w * n + w], start=(j == 0 and what == 0 and i == 0),
                                              stop=(j == NU - 1), skip_group_check=True)
                mm.then_inc(pv_done, 1)

            def body(s):
                if s.has(-2):
                    values(s, -2, NU - 2)
                    values(s, -2, NU - 1)
                for pos, (kind, j) in enumerate(U.order):
                    if pos == 1 and s.has(1):
                        misc_free(pe, s, "QK")
                        for a in range(2):
                            mm = nc.tensor.matmul(misc[:, T * a:T * a + T], wqk[:, a, :], batch_tokens(s, 1),
                                                  start=True, stop=True)
                        mm.then_inc(qk_full, 1)
                    if pos == 4 and s.has():
                        misc_free(pe, s, "V")
                        pe.wait_ge(xb_done, s.n() + 1)
                        n = P if layer == 0 else 2 * P
                        w = v.wv0[:] if layer == 0 else v.wv1[:].rearrange("p a n -> p (a n)")
                        for c in range(2):
                            mm = nc.tensor.matmul(misc[:, n * c:n * c + n], xb[:, P * c:P * c + P], w,
                                                  start=True, stop=True)
                        mm.then_inc(v_full, 1)
                    if layer and pos == 5 and s.has(-2):
                        misc_free(pe, s, "E")
                        nc.tensor.matmul(misc[:, 0:T], v.wvs[:], batch_tokens(s, -2), start=True, stop=False,
                                         skip_group_check=True)
                        vc = vcen[:, s.buf(-2)]
                        nc.tensor.matmul(misc[:, 0:T], vc[:, 0], cst[:, C_UT:C_UT + T], start=False, stop=False,
                                         skip_group_check=True)
                        nc.tensor.matmul(misc[:, P:T], vc[:, 1], cst[:, C_UT + T:C_UT + T + P], start=False, stop=True,
                                         skip_group_check=True).then_inc(e_full, 1)
                    if pos == 7 and s.has(-2):
                        misc_free(pe, s, "Y")
                        pe.wait_ge(on_done, s.n(-2) + 1)
                        for c in range(2):
                            mm = nc.tensor.matmul(misc[:, D * c:D * c + D], on[:, P * c:P * c + P], wo[:],
                                                  start=True, stop=True)
                        mm.then_inc(y_full, 1)
                    if U.exists(s.k, kind):
                        (first_pass if kind == "A" else second_pass)(s, pos, j)
                    if kind == "B" and j >= 2 and s.has(-1):
                        values(s, -1, j - 2)
                if s.has():
                    misc_free(pe, s, "M")
                    pe.wait_ge(max_parts, 4 * (s.n() + 1))
                    nc.tensor.transpose(misc[0:PARTS * 2 * H, 0:P // 2].bitcast(BF16),
                                        m3[:].rearrange("p c t h -> p (c t h)"), eyeb[:]).then_inc(mt_full, 1)

            emit(pe, body)


_INS = ['L0_attn_x', 'L0_attn_w_qkv', 'L0_attn_b_qkv', 'L0_attn_w_out', 'L0_attn_b_out', 'L0_attn_w1_rpe',
        'L0_attn_b1_rpe', 'L0_attn_w2_rpe', 'L0_attn_b2_rpe', 'L0_ffn_router_weight', 'L0_ffn_router_bias',
        'L0_ffn_gate_up_proj', 'L0_ffn_gate_up_bias', 'L0_ffn_down_proj', 'L0_ffn_down_bias', 'L1_attn_qk_w',
        'L1_attn_qk_b', 'L1_attn_v_w', 'L1_attn_cproj_w', 'L1_attn_resid_gain', 'L1_attn_skip_gain',
        'L1_attn_centre_gain', 'L1_ffn_W', 'L1_ffn_b', 'L1_ffn_V_r', 'L1_ffn_C']


def _constants():
    import numpy as np
    c = np.zeros((P, C_ALL), np.float32)
    p = np.arange(P)[:, None]
    n = np.arange(P)[None, :]
    t = np.arange(T)[None, :]
    c[:, C_EYE:C_EYE + P] = p == n
    c[:, C_MA:C_MA + P] = np.where(n <= p, 0.0, NEG)
    c[:, C_MB:C_MB + P] = np.where(n >= p, 0.0, NEG)
    share = np.float32(1.0) / (t + 1).astype(np.float32)
    c[:, C_UT:C_UT + T] = np.where(p <= t, share, 0.0)
    c[:, C_UT + T:C_UT + T + P] = np.where(P + p <= t, share, 0.0)[:, P:T]
    c[:, C_BEFORE:C_BEFORE + P] = p < n
    c[:, C_TILES:C_TILES + NT] = P * np.arange(NT)[None, :]
    c[:, C_TILES + NT:C_ALL] = np.arange(SLOT_TILES)[None, :]
    c[:, C_FLIP:C_FLIP + P] = p == P - 1 - n
    c[:, C_RANK:C_RANK + E] = E - np.arange(E)[None, :]
    r = np.arange(-T, T).astype(np.float32)
    f = (np.sign(r) * np.log1p(np.abs(r))).astype(np.float32)
    return c, np.concatenate([f, -f])[None, :].astype(np.float32)


def kernel(**inputs):
    import numpy as _np
    import concourse.bacc as _bacc
    from concourse import mybir as _mybir
    from concourse.bass_utils import run_bass_kernel_spmd as _run

    nc = _bacc.Bacc("TRN2", target_bir_lowering=False, num_devices=1)
    arrays, args = {}, []
    given = {name: inputs[name] for name in _INS}
    given["consts"], given["rel"] = _constants()
    for name, a in given.items():
        a = _np.ascontiguousarray(a)
        arrays[f"in_{name}_dram"] = a
        args.append(nc.dram_tensor(f"in_{name}_dram", a.shape, _mybir.dt.from_np(a.dtype), kind="ExternalInput").ap())
    shape = inputs["L0_attn_x"].shape
    args.append(nc.dram_tensor("out_0_dram", shape, _mybir.dt.float32, kind="ExternalOutput").ap())
    build(nc, *args)
    r = _run(nc, [arrays], core_ids=[0])
    return r.results[0]["out_0_dram"]
```

```python
from contextlib import ExitStack

import concourse.bass as bass
from concourse import mybir

ALU = mybir.AluOpType
ACT = mybir.ActivationFunctionType
F32 = mybir.dt.float32
BF16 = mybir.dt.bfloat16
U32 = mybir.dt.uint32
I32 = mybir.dt.int32
AX = mybir.AxisListType

P = 128
B, T, D = 16, 256, 128
H, HD = 16, 8
Q4 = 4
NT = B * T // P
E, I = 8, 256
TOPK = 2
G = 8
SLOT_TILES = NT * TOPK + E
FLIGHT = 8
SPARE = FLIGHT * P
RPE = 32
RANK = 32
ALPHA, LIMIT = 1.702, 7.0
EPS = 1e-5
QSCALE = float(HD) ** -0.5
NEG = -1.0e30
PARTS = 3
PAIRS = 6
QROWS = PAIRS * HD
REL = 512
TAB = 384
C_EYE, C_MA, C_MB = 0, P, 2 * P
C_UT = 3 * P
C_RANK = C_UT + T + P
C_FLIP = C_RANK + E
C_BEFORE = C_FLIP + 128
C_TILES = C_BEFORE + 128
C_ROWS = C_TILES + NT + SLOT_TILES
C_SPARE = C_ROWS + NT
C_ALL = C_SPARE + FLIGHT


W_LOADS, R_LOADS = 15, 5
PAIR_OF_ONES = float.fromhex("0x1.007f00p+0")


class Step:

    def __init__(self, k, J=0, period=3, count=B):
        self.k, self.J, self.period, self.count = k, J, period, count

    def n(self, d=0):
        return self.k + d + self.period * self.J

    def turn(self, d=0):
        return (self.k + d) // self.period + self.J

    def has(self, d=0):
        return 0 <= self.k + d < self.count

    def buf(self, d=0):
        return (self.k + d) % self.period


class Shared:
    pass


def build(nc, x_in, w_qkv, b_qkv, w_out, b_out, w1_rpe, b1_rpe, w2_rpe, b2_rpe, router_w, router_b,
          gu_w, gu_b, down_w, down_b, qk_w, qk_b, v_w, cproj_w, resid, skip, centre, f_w, f_b, f_v, f_c,
          consts, rel, out):
    with ExitStack() as ctx:
        def sb(name, shape, dt=F32):
            return ctx.enter_context(nc.sbuf_tensor(name, shape, dt))

        def sem(name):
            return ctx.enter_context(nc.semaphore(name))

        v = Shared()
        v.sem = sem
        v.x_in, v.w_qkv, v.b_qkv, v.w_out, v.b_out, v.w1_rpe = x_in, w_qkv, b_qkv, w_out, b_out, w1_rpe
        v.b1_rpe, v.w2_rpe, v.b2_rpe, v.router_w, v.router_b, v.gu_w = b1_rpe, w2_rpe, b2_rpe, router_w, router_b, gu_w
        v.gu_b, v.down_w, v.down_b, v.qk_w, v.qk_b, v.v_w = gu_b, down_w, down_b, qk_w, qk_b, v_w
        v.cproj_w, v.resid, v.skip, v.centre, v.f_w, v.f_b = cproj_w, resid, skip, centre, f_w, f_b
        v.f_v, v.f_c, v.consts, v.rel, v.out = f_v, f_c, consts, rel, out

        v.ps = ctx.enter_context(nc.psum_tensor("ps", [P, 8, 512], F32))

        v.x = sb("x", [P, NT, D])
        v.rows = sb("rows", [P, NT, D + 2])
        v.gate = v.rows[:, :, 0:D]
        v.xnT = sb("xnT", [P, NT * P])
        v.probs = sb("probs", [P, 8, 1024])
        v.qs = sb("qs", [P, 3, H, T], BF16)
        v.ks = sb("ks", [P, 3, H, T], BF16)
        v.tabB = sb("tabB", [P, H, TAB])
        v.tabA = sb("tabA", [P, H, TAB], BF16)
        v.vpad = sb("vpad", [P, 3, 8, 160])
        v.onespad = sb("onespad", [P, 4, 32])
        v.cst = sb("cst", [P, C_ALL])
        v.eyeb = sb("eyeb", [P, P], BF16)
        v.maskA = sb("maskA", [P, P], BF16)
        v.maskB = sb("maskB", [P, P], BF16)
        v.wqk0 = sb("wqk0", [P, 2, P])
        v.wqk1 = sb("wqk1", [P, 2, P])
        v.wv0 = sb("wv0", [P, P])
        v.wv1 = sb("wv1", [P, 2, P])
        v.wvs = sb("wvs", [P, P])
        v.wo0 = sb("wo0", [P, D])
        v.wo1 = sb("wo1", [P, D])
        v.bo = sb("bo", [P, D])
        v.cols = sb("cols", [P, 8])
        v.rwT = sb("rwT", [P, E])
        v.rb = sb("rb", [P, E])
        v.ones = sb("ones", [1, P])
        v.feff = sb("feff", [P, D])
        v.fb = sb("fb", [1, D])
        v.wt = sb("wt", [P, TOPK, NT])
        v.place = sb("place", [P, TOPK, NT], U32)
        v.rowid = sb("rowid", [P, TOPK, NT])
        v.owner = sb("owner", [1, SLOT_TILES], I32)
        v.xb = sb("xb", [P, T])
        v.qkf = sb("qkf", [P, 2, T])
        v.qkr = sb("qkr", [P, 2, T])
        v.qk3 = sb("qk3", [P, 2, PARTS, T], BF16)
        v.mx = sb("mx", [P, 3, 2, H])
        v.mres = sb("mres", [P, 2, H])
        v.m3 = sb("m3", [P, PARTS, 2, H], BF16)
        v.mT = sb("mT", [PARTS * 2 * H, P], BF16)
        v.rden = sb("rden", [P, T])
        v.on = sb("on", [P, T])
        v.yt = sb("yt", [P, T])
        v.stat = sb("stat", [P, 4, NT])
        v.zrow = sb("zrow", [PARTS, T], BF16)
        v.eps = sb("eps", [P, 1])

        v.wgu = v.qs[:, 1:3].rearrange("p b h t -> p (b h t)").bitcast(F32).rearrange("p (e n) -> p e n", e=E)
        v.wdn = v.ks[:, 1].rearrange("p h t -> p (h t)").bitcast(F32).rearrange("p (e c n) -> p e c n", e=E, c=2)
        v.biases = v.tabA[:].rearrange("p h u -> p (h u)")[:, 0:5 * E * P]
        v.w_load, v.b_zero, v.b_load = sem("ex_weights"), sem("ex_bias_zero"), sem("ex_biases")
        v.squares = v.probs[:, 6:8, :].rearrange("p a b -> p (a b)").rearrange("p (t d) -> p t d", d=D)
        v.vcen = v.tabA[:, 0:6, 0:256].bitcast(F32).rearrange("p (b c) n -> p b c n", c=2)
        v.scratch = v.probs[:, 0:6, :].rearrange("p a b -> p (a b)")

        v.bias_f = nc.dram_tensor("bias_f", (H, REL), F32, kind="Internal")
        v.bias_r = nc.dram_tensor("bias_r", (H, REL), BF16, kind="Internal")
        v.parts_d = nc.dram_tensor("parts_d", (3, 2, PARTS, P, T), BF16, kind="Internal")
        v.bias3_d = nc.dram_tensor("bias3_d", (PARTS, 5 * E, P), BF16, kind="Internal")
        v.slots_in = nc.dram_tensor("slots_in", (SLOT_TILES * P, D + 2), F32, kind="Internal")
        v.mixed = nc.dram_tensor("mixed", (SPARE + TOPK * B * T, D), F32, kind="Internal")
        v.max_d = nc.dram_tensor("max_d", (3, PARTS, 2, H, P), BF16, kind="Internal")

        setup(nc, v)
        attention(nc, v, 0)
        experts(nc, v)
        middle(nc, v)
        attention(nc, v, 1)


def setup(nc, v):
    sem = v.sem
    ps, cst, x, gate, xnT, stat = v.ps, v.cst, v.x, v.gate, v.xnT, v.stat
    at = [0]

    def take(n, rows=P):
        at[0] += n
        assert at[0] <= v.scratch.shape[1]
        return v.scratch[0:rows, at[0] - n:at[0]]

    hid, relb = take(2 * REL, RPE + 1), take(2 * REL, RPE)
    w2, w2p, rpc = take(H, RPE + 1), take(H, RPE + 1), take(2, RPE)
    bfw, brv = take(REL, H), take(REL // 2, H).bitcast(BF16)
    wqkv, wqk = take(3 * P), take(2 * P)
    rows = take(6 * P, 1).rearrange("p (a b) -> p a b", b=P)
    rowsp = take(6 * P, 1).rearrange("p (a b) -> p a b", b=P)
    gains = take(3 * H).rearrange("p (a h) -> p a h", h=H)
    bor, bvb, fw = take(P, 1), take(P), take(P)
    fv, fc, fvT, fcT, rw = take(RANK), take(RANK), take(P, RANK), take(P, RANK), take(P, E)
    flipb = take(P // 2).bitcast(BF16)
    zero = take(D + 2)
    b40 = v.qkf[0:5 * E, 0, 0:P]
    b3 = v.qk3[0:5 * E, 0, :, 0:P]
    ones128 = fw
    rt = v.scratch[:, 0:7 * NT * E].rearrange("p (k t e) -> p k t e", k=7, e=E)
    small = v.scratch[:, 7 * NT * E:7 * NT * E + 4 * NT + 3 * E]
    eye = cst[:, C_EYE:C_EYE + P]
    flip = cst[:, C_FLIP:C_FLIP + P]
    tabs = (v.tabA[:].rearrange("p h u -> p (h u)"), v.tabB[:].rearrange("p h u -> p (h u)"))
    NB = H * TAB // 512

    c_load = sem("su_consts")
    x_load = [sem("su_x0"), sem("su_x1")]
    r_load = sem("su_rpe")
    w_load = sem("su_weights")
    copied = sem("su_copied")
    hidden = sem("su_hidden")
    bias_mm = sem("su_bias_mm")
    bias_cp = sem("su_bias_cp")
    bias_st = sem("su_bias_stored")
    tab_ld = [sem("su_tab_a"), sem("su_tab_b")]
    tab_mm, tab_cp = sem("su_tab_mm"), sem("su_tab_cp")
    router_mm, router_cp = sem("su_router_mm"), sem("su_router_cp")
    small_mm = sem("su_small_mm")
    small_cp = sem("su_small_cp")
    zeroed = sem("su_zeroed")
    ln, sq, rs = sem("su_ln"), sem("su_sq"), sem("su_rs")
    tr, trc, lg = sem("su_tr"), sem("su_trc"), sem("su_lg")
    ro = sem("su_ro")
    chosen, counted = sem("su_chosen"), sem("su_counted")
    ex = sem("su_ex")
    eb_load = sem("su_expert_biases")
    eb_parts = sem("su_expert_parts")

    with nc.Block() as block:
        def small_weights(dve):
            dve.wait_ge(small_mm, 1)
            nc.vector.tensor_scalar(v.cols[:, 0:1], ps[:, 2, 0:1], QSCALE, None, ALU.mult).then_inc(small_cp, 1)
            nc.vector.tensor_copy(v.cols[:, 1:3], ps[:, 2, 1:3]).then_inc(small_cp, 1)
            nc.vector.tensor_scalar(v.cols[:, 3:4], ps[:, 2, 3:4], QSCALE, None, ALU.mult).then_inc(small_cp, 1)
            nc.vector.tensor_copy(v.cols[:, 4:6], ps[:, 2, 4:6]).then_inc(small_cp, 1)
            nc.vector.tensor_copy(fvT, ps[0:RANK, 2, 128:256]).then_inc(small_cp, 1)
            nc.vector.tensor_copy(fcT, ps[0:RANK, 2, 256:384]).then_inc(small_cp, 1)
            dve.wait_ge(small_cp, 6)
            nc.vector.tensor_copy(bvb, v.cols[:, 2:3].broadcast_to([P, P])).then_inc(small_cp, 1)
            dve.wait_ge(small_mm, 2)
            nc.vector.tensor_copy(v.bo[:], ps[:, 3, 0:P]).then_inc(small_cp, 1)
            nc.vector.tensor_copy(v.feff[:], ps[:, 3, P:2 * P]).then_inc(small_cp, 1)
            nc.vector.memset(ones128, 1.0).then_inc(small_cp, 1)

        def routing(dve, meanwhile):
            L, cand, one1, L2, one2, both, ew = (rt[:, k] for k in range(7))
            m1, m2, rk, gap = (small[:, NT * k:NT * k + NT] for k in range(4))
            cnt, tiles, ends = (small[:, 4 * NT + E * k:4 * NT + E * k + E] for k in range(3))
            rank = cst[:, C_RANK:C_RANK + E].unsqueeze(1).broadcast_to([P, NT, E])
            steps = [0]

            def step(ins):
                ins.then_inc(ro, 1)
                steps[0] += 1
                dve.wait_ge(ro, steps[0])

            def wide(a):
                return a.unsqueeze(2).broadcast_to([P, NT, E])

            def pick(src, m, hot):
                step(nc.vector.tensor_reduce(m, src, AX.X, ALU.max))
                step(nc.vector.tensor_tensor(cand, src, wide(m), ALU.is_equal))
                step(nc.vector.tensor_tensor(cand, cand, rank, ALU.mult))
                step(nc.vector.tensor_reduce(rk, cand, AX.X, ALU.max))
                step(nc.vector.tensor_tensor(hot, cand, wide(rk), ALU.is_equal))

            dve.wait_ge(lg, G)
            step(nc.vector.tensor_tensor(L, ps[:, 7, 0:NT * E].rearrange("p (t e) -> p t e", e=E),
                                         v.rb[:].unsqueeze(1).broadcast_to([P, NT, E]), ALU.add))
            pick(L, m1, one1)
            step(nc.vector.scalar_tensor_tensor(L2, one1, -3.0e38, L, ALU.mult, ALU.add))
            pick(L2, m2, one2)
            nc.vector.tensor_tensor(both, one1, one2, ALU.add).then_inc(chosen, 1)
            nc.vector.tensor_tensor(ew, L, wide(m1), ALU.subtract).then_inc(chosen, 1)
            nc.vector.tensor_tensor(gap, m2, m1, ALU.subtract).then_inc(chosen, 1)
            meanwhile(dve)
            dve.wait_ge(counted, 1)
            run = L2
            for e in range(E):
                step(nc.vector.tensor_tensor_scan(run[:, :, e], ones128[:, 0:NT], ps[:, 1, e:NT * E:E], 0.0, ALU.mult, ALU.add))
            step(nc.vector.tensor_copy(cnt, run[:, NT - 1, :]))
            more = cand.rearrange("p t e -> p (t e)").rearrange("p (e t) -> p e t", e=E)
            step(nc.vector.tensor_tensor(more, cnt.unsqueeze(2).broadcast_to([P, E, NT]),
                                         cst[:, C_TILES:C_TILES + NT].unsqueeze(1).broadcast_to([P, E, NT]), ALU.is_gt))
            step(nc.vector.tensor_reduce(tiles, more, AX.X, ALU.add))
            step(nc.vector.tensor_tensor_scan(ends, ones128[:, 0:E], tiles, 0.0, ALU.mult, ALU.add))
            step(nc.vector.tensor_tensor(tiles, ends, tiles, ALU.subtract))
            step(nc.vector.tensor_tensor(run, run, ps[:, 1, 0:NT * E].rearrange("p (t e) -> p t e", e=E), ALU.subtract))
            step(nc.vector.tensor_tensor(run, run, ps[:, 0, 0:NT * E].rearrange("p (t e) -> p t e", e=E), ALU.add))
            step(nc.vector.scalar_tensor_tensor(run, tiles.unsqueeze(1).broadcast_to([P, NT, E]), float(P), run,
                                                ALU.mult, ALU.add))
            for k, hot in enumerate((one1, one2)):
                step(nc.vector.tensor_tensor(cand, hot, run, ALU.mult))
                step(nc.vector.tensor_reduce(m1, cand, AX.X, ALU.add))
                step(nc.vector.tensor_copy(v.place[:, k, :], m1))
                step(nc.vector.tensor_scalar(v.rowid[:, k, :], cst[:, C_ROWS:C_SPARE], float(k * B * T), None, ALU.add))
            own = one1.rearrange("p t e -> p (t e)")[0:1, 0:SLOT_TILES]
            step(nc.vector.tensor_scalar(own, cst[0:1, C_TILES + NT:C_ROWS], ends[0:1, 0:1], None, ALU.is_ge))
            for e in range(1, E - 1):
                step(nc.vector.scalar_tensor_tensor(own, cst[0:1, C_TILES + NT:C_ROWS], ends[0:1, e:e + 1], own,
                                                    ALU.is_ge, ALU.add))
            step(nc.vector.tensor_copy(v.owner[:], own))
            dve.wait_ge(ex, 2)
            step(nc.vector.tensor_reduce(m2, ew, AX.X, ALU.add))
            step(nc.vector.reciprocal(v.wt[:, 0, :], m2))
            step(nc.vector.tensor_tensor(v.wt[:, 1, :], v.wt[:, 0, :], gap, ALU.mult))

        @block.sync
        def _(sp):
            for half in range(2):
                sp.dma_start(x[:, 16 * half:16 * half + 16, :],
                             v.x_in[8 * half:8 * half + 8].rearrange("b (c p) d -> p (b c) d", p=P)).then_inc(x_load[half], 16)
            sp.dma_start(cst[:, :], v.consts[:, :]).then_inc(c_load, 16)
            sp.dma_start(rw, v.router_w[:, :]).then_inc(c_load, 16)
            sp.dma_start(v.rb[:], v.router_b.partition_broadcast(P)).then_inc(c_load, 16)
            rpe = [
                (relb, v.rel[0, :].partition_broadcast(RPE)),
                (w2[0:RPE, :], v.w2_rpe[:, :]),
                (w2[RPE:RPE + 1, :], v.b2_rpe.rearrange("(a n) -> a n", a=1)),
                (rpc[:, 0:1], v.w1_rpe.rearrange("a k -> k a")),
                (rpc[:, 1:2], v.b1_rpe.rearrange("(k a) -> k a", a=1)),
            ]
            for dst, src in rpe:
                sp.dma_start(dst, src).then_inc(r_load, 16)
            loads = [
                (wqkv, v.w_qkv[:, :]),
                (wqk, v.qk_w[:, :]),
                (v.wv1[:, 0, :], v.v_w[:, :]),
                (v.wo0[:, :], v.w_out[:, :]),
                (v.wo1[:, :], v.cproj_w[:, :]),
                (rows[:, 0:3, :], v.b_qkv.rearrange("(o a n) -> o a n", o=1, a=3)),
                (rows[:, 3:5, :], v.qk_b.rearrange("(o a n) -> o a n", o=1, a=2)),
                (gains[:, 0, :], v.resid[0, :, 0, 0].partition_broadcast(P)),
                (gains[:, 1, :], v.skip[0, :, 0, 0].partition_broadcast(P)),
                (gains[:, 2, :], v.centre[0, :, 0, 0].partition_broadcast(P)),
                (bor, v.b_out.rearrange("(a n) -> a n", a=1)),
                (fw, v.f_w[:, :]),
                (fv, v.f_v[:, :]),
                (fc, v.f_c[:, :]),
                (v.fb[:, :], v.f_b.rearrange("(a n) -> a n", a=1)),
            ]
            for dst, src in loads:
                sp.dma_start(dst, src).then_inc(w_load, 16)
            sp.dma_start(b40[0:4 * E, :], v.gu_b.rearrange("e (j n) -> (e j) n", n=P)).then_inc(eb_load, 16)
            sp.dma_start(b40[4 * E:5 * E, :], v.down_b[:, :]).then_inc(eb_load, 16)
            assert len(loads) == W_LOADS and len(rpe) == R_LOADS
            sp.wait_ge(bias_cp, 2)
            sp.dma_start(v.bias_r[:, :], brv).then_inc(bias_st, 16)
            sp.dma_start(v.bias_f[:, :], bfw).then_inc(bias_st, 16)
            sp.wait_ge(bias_st, 32)
            for i, src in enumerate((v.bias_r, v.bias_f)):
                sp.dma_start((v.tabA, v.tabB)[i][:], bass.AP(src, 1, [[1, P], [REL, H], [1, TAB]])).then_inc(tab_ld[i], 16)
            sp.wait_ge(eb_parts, 6)
            sp.dma_start(v.bias3_d[:].rearrange("c r n -> r c n"), b3[:]).then_inc(eb_load, 16)
            sp.wait_ge(eb_load, 48)
            sp.dma_start(v.slots_in[:, :].rearrange("(t p) d -> p t d", p=P),
                         zero.unsqueeze(1).broadcast_to([P, SLOT_TILES, D + 2])).then_inc(eb_load, 16)
            sp.wait_ge(eb_load, 64)

        @block.gpsimd
        def _(pool):
            nc.gpsimd.memset(v.zrow[:], 0.0).then_inc(zeroed, 1)
            for buf in range(3):
                nc.gpsimd.memset(v.qs[:, buf].bitcast(F32), 0.0).then_inc(zeroed, 1)
                nc.gpsimd.memset(v.ks[:, buf].bitcast(F32), 0.0).then_inc(zeroed, 1)
            nc.gpsimd.memset(v.vpad[:], 0.0).then_inc(zeroed, 1)
            nc.gpsimd.memset(v.onespad[:], 0.0).then_inc(zeroed, 1)
            pool.wait_ge(zeroed, 9)
            for i in range(4):
                nc.gpsimd.memset(v.onespad[:, i, 8 * i:8 * i + 8], 1.0).then_inc(zeroed, 1)
            pool.wait_ge(zeroed, 13)
            nc.gpsimd.memset(v.ks[32:64].rearrange("p b h t -> p (b h t)").bitcast(F32), PAIR_OF_ONES).then_inc(zeroed, 1)

        @block.vector
        def _(dve):
            nc.vector.memset(v.eps[:], EPS).then_inc(ln, 1)
            nc.vector.memset(zero, 0.0).then_inc(eb_parts, 1)
            nc.vector.memset(v.ones[:], 1.0).then_inc(copied, 1)
            nc.vector.memset(hid[RPE:RPE + 1, :], 1.0).then_inc(copied, 1)
            layernorm_vector(nc, dve, v, ln, sq, rs, x_load, 0)
            dve.wait_ge(r_load, 16 * R_LOADS)
            nc.vector.tensor_scalar(hid[0:RPE, :], relb, rpc[:, 0:1], rpc[:, 1:2], ALU.mult, ALU.add).then_inc(hidden, 1)
            dve.wait_ge(hidden, 1)
            nc.vector.tensor_scalar(hid[0:RPE, :], hid[0:RPE, :], 0.0, None, ALU.max).then_inc(hidden, 1)
            for i in range(4):
                nc.vector.tensor_copy(w2p[:, 4 * i:4 * i + 4], w2[:, i:H:4]).then_inc(hidden, 1)
            dve.wait_ge(c_load, 16 * 3)
            nc.vector.tensor_copy(v.eyeb[:], eye).then_inc(copied, 1)
            nc.vector.tensor_copy(v.maskA[:], cst[:, C_MA:C_MA + P]).then_inc(copied, 1)
            nc.vector.tensor_copy(v.maskB[:], cst[:, C_MB:C_MB + P]).then_inc(copied, 1)
            nc.vector.tensor_copy(flipb, flip).then_inc(copied, 1)
            dve.wait_ge(bias_mm, 2)
            nc.vector.tensor_copy(brv, ps[0:H, 1, :]).then_inc(bias_cp, 1)
            nc.vector.tensor_copy(bfw, ps[0:H, 0, :]).then_inc(bias_cp, 1)
            layernorm_vector(nc, dve, v, ln, sq, rs, x_load, 1)
            dve.wait_ge(w_load, 16 * W_LOADS)
            for src, dst in ((wqkv, v.wqk0), (wqk, v.wqk1)):
                for a in range(2):
                    nc.vector.tensor_copy(dst[:, a, :].rearrange("p (d i q) -> p d i q", d=HD, i=4),
                                          src[:, P * a:P * a + P].rearrange("p (q i d) -> p d i q", q=4, i=4)
                                          ).then_inc(copied, 1)
            for a in (0, 1, 3, 4):
                nc.vector.tensor_copy(rowsp[:, a, :].rearrange("p (d i q) -> p d i q", d=HD, i=4),
                                      rows[:, a, :].rearrange("p (q i d) -> p d i q", q=4, i=4)).then_inc(copied, 1)
            nc.vector.tensor_copy(rowsp[:, 2, :], rows[:, 2, :]).then_inc(copied, 1)
            nc.vector.tensor_copy(rowsp[:, 5, :].rearrange("p (h d) -> p h d", d=HD),
                                  gains[0:1, 0, :].unsqueeze(2).broadcast_to([1, H, HD])).then_inc(copied, 1)
            nc.vector.tensor_copy(v.wv0[:], wqkv[:, 2 * P:3 * P]).then_inc(copied, 1)
            vw = v.wv1[:, 0, :].rearrange("p (h d) -> p h d", d=HD)
            nc.vector.tensor_tensor(v.wvs[:].rearrange("p (h d) -> p h d", d=HD), vw,
                                    gains[:, 1, :].unsqueeze(2).broadcast_to([P, H, HD]), ALU.mult).then_inc(copied, 1)
            nc.vector.scalar_tensor_tensor(v.wv1[:, 1, :].rearrange("p (h d) -> p h d", d=HD), vw, -1.0,
                                           gains[:, 2, :].unsqueeze(2).broadcast_to([P, H, HD]),
                                           ALU.mult, ALU.mult).then_inc(copied, 1)
            dve.wait_ge(eb_load, 32)
            for c in range(PARTS):
                nc.vector.tensor_copy(b3[:, c, :], b40[:]).then_inc(eb_parts, 1)
                if c < PARTS - 1:
                    dve.wait_ge(eb_parts, 2 * c + 2)
                    nc.vector.tensor_tensor(b40[:], b40[:], b3[:, c, :], ALU.subtract).then_inc(eb_parts, 1)
                    dve.wait_ge(eb_parts, 2 * c + 3)
            routing(dve, small_weights)

        @block.scalar
        def _(act):
            act.wait_ge(router_mm, 1)
            nc.scalar.activation(v.rwT[:], ps[:, 3, 0:E], ACT.Copy).then_inc(router_cp, 1)
            def transposed(groups):
                for g in groups:
                    act.wait_ge(tr, g + 1)
                    nc.scalar.activation(xnT[:, 512 * g:512 * g + 512], ps[:, 4 + g % 2, :], ACT.Copy).then_inc(trc, 1)

            layernorm_square(nc, act, v, ln, sq, 0)
            layernorm_root(nc, act, v, ln, rs, 0)
            transposed(range(0, 2))
            layernorm_square(nc, act, v, ln, sq, 1)
            transposed(range(2, 3))
            layernorm_root(nc, act, v, ln, rs, 1)
            transposed(range(3, G))
            for k in range(2 * NB):
                act.wait_ge(tab_mm, k + 1)
                n = k % NB
                nc.scalar.activation(tabs[k // NB][:, 512 * n:512 * n + 512], ps[:, 4 + k % 3, :], ACT.Copy).then_inc(tab_cp, 1)
                if k == 2 * NB - 8:
                    act.wait_ge(chosen, 3)
                    ew, gap = rt[:, 6], small[:, 3 * NT:4 * NT]
                    nc.scalar.activation(ew, ew, ACT.Exp).then_inc(ex, 1)
                    nc.scalar.activation(gap, gap, ACT.Exp).then_inc(ex, 1)

        @block.tensor
        def _(pe):
            def small_products():
                pe.wait_ge(small_cp, 7)
                nc.tensor.matmul(ps[:, 3, 0:P], bvb, v.wo0[:], start=True, stop=False)
                nc.tensor.matmul(ps[:, 3, 0:P], v.ones[0:1, 0:P], bor, start=False, stop=True)
                nc.tensor.matmul(ps[:, 3, P:2 * P], fw, eye, start=True, stop=False)
                nc.tensor.matmul(ps[:, 3, P:2 * P], fvT, fcT, start=False, stop=True).then_inc(small_mm, 1)

            pe.wait_ge(c_load, 16 * 3)
            nc.tensor.transpose(ps[:, 3, 0:E], rw, eye[0:E, 0:E]).then_inc(router_mm, 1)
            pe.wait_ge(copied, 2)
            pe.wait_ge(hidden, 6)
            for k in range(2):
                nc.tensor.matmul(ps[0:H, k, :], w2p, hid[:, REL * k:REL * k + REL], start=True, stop=True).then_inc(bias_mm, 1)
            pe.wait_ge(router_cp, 1)
            for g in range(G + 1):
                if g < G:
                    if g >= 2:
                        pe.wait_ge(trc, g - 1)
                    pe.wait_ge(ln, layernorm_ready(g))
                    for c in range(4):
                        mm = nc.tensor.transpose(ps[:, 4 + g % 2, P * c:P * c + P], gate[:, 4 * g + c, :], eye)
                    mm.then_inc(tr, 1)
                if g >= 1:
                    pe.wait_ge(trc, g)
                    for t in range(4 * g - 4, 4 * g):
                        mm = nc.tensor.matmul(ps[:, 7, E * t:E * t + E], xnT[:, P * t:P * t + P], v.rwT[:],
                                              start=(t == 0), stop=True, skip_group_check=True)
                    mm.then_inc(lg, 1)
            pe.wait_ge(copied, 2 + 4 + 13)
            for k in range(6):
                nc.tensor.matmul(ps[:, 2, k:k + 1], rowsp[:, k, :], v.ones[0:1, 0:1], start=True, stop=True)
            nc.tensor.matmul(ps[0:RANK, 2, 128:256], fv, eye, start=True, stop=True)
            nc.tensor.matmul(ps[0:RANK, 2, 256:384], fc, eye, start=True, stop=True).then_inc(small_mm, 1)
            for k in range(2 * NB):
                if k % NB == 0:
                    pe.wait_ge(tab_ld[k // NB], 16)
                if k >= 3:
                    pe.wait_ge(tab_cp, k - 2)
                n = k % NB
                nc.tensor.matmul(ps[:, 4 + k % 3, :], flipb if k < NB else flip, tabs[k // NB][:, 512 * n:512 * n + 512],
                                 start=True, stop=True).then_inc(tab_mm, 1)
                if k == NB - 1:
                    small_products()
                    pe.wait_ge(chosen, 1)
                    pe.wait_ge(small_cp, 10)
                    both = rt[:, 5].rearrange("p t e -> p (t e)")
                    nc.tensor.matmul(ps[:, 0, 0:NT * E], cst[:, C_BEFORE:C_BEFORE + P], both, start=True, stop=True)
                    nc.tensor.matmul(ps[:, 1, 0:NT * E], ones128, both, start=True, stop=True).then_inc(counted, 1)


def layernorm_ready(g):
    return 7 if g < G // 2 else 13


def layernorm_vector(nc, dve, v, ln, sq, rs, x_load, half):
    a = slice(16 * half, 16 * half + 16)
    xh, gh = v.x[:, a, :], v.gate[:, a, :]
    s, var, r, m = (v.stat[:, k, a] for k in range(4))
    n = 6 * half + 1
    dve.wait_ge(x_load[half], 16)
    nc.vector.tensor_reduce(s, xh, AX.X, ALU.add).then_inc(ln, 1)
    dve.wait_ge(ln, n + 1)
    nc.vector.tensor_scalar(m, s, 1.0 / D, None, ALU.mult).then_inc(ln, 1)
    dve.wait_ge(ln, n + 2)
    nc.vector.tensor_tensor(gh, xh, m.unsqueeze(2).broadcast_to([P, 16, D]), ALU.subtract).then_inc(ln, 1)
    dve.wait_ge(sq, half + 1)
    nc.vector.tensor_reduce(var, v.squares, AX.X, ALU.add).then_inc(ln, 1)
    dve.wait_ge(rs, half + 1)
    nc.vector.reciprocal(r, r).then_inc(ln, 1)
    dve.wait_ge(ln, n + 5)
    nc.vector.tensor_tensor(gh, gh, r.unsqueeze(2).broadcast_to([P, 16, D]), ALU.mult).then_inc(ln, 1)


def layernorm_square(nc, act, v, ln, sq, half):
    act.wait_ge(ln, 6 * half + 4)
    nc.scalar.activation(v.squares, v.gate[:, 16 * half:16 * half + 16, :], ACT.Square).then_inc(sq, 1)


def layernorm_root(nc, act, v, ln, rs, half):
    a = slice(16 * half, 16 * half + 16)
    act.wait_ge(ln, 6 * half + 5)
    nc.scalar.activation(v.stat[:, 2, a], v.stat[:, 1, a], ACT.Sqrt, bias=v.eps[:, 0:1], scale=1.0 / D).then_inc(rs, 1)


def pipeline(eng, body, first, loop, rounds, last, period, count):
    for k in range(first, loop):
        body(Step(k, 0, period, count))
    with eng.Fori(0, rounds) as J:
        for r in range(period):
            body(Step(loop + r, J, period, count))
    for k in range(loop + period * rounds, last + 1):
        body(Step(k, 0, period, count))


def experts(nc, v):
    sem = v.sem
    ps, cst, wgu, wdn, biases = v.ps, v.cst, v.wgu, v.wdn, v.biases
    eye = cst[:, C_EYE:C_EYE + P]
    at = [0]

    def take(n):
        at[0] += n
        return v.probs[:].rearrange("p a b -> p (a b)")[:, at[0] - n:at[0]]

    xg = take(FLIGHT * (D + 2)).rearrange("p (b n) -> p b n", b=FLIGHT)
    rows = take(FLIGHT).bitcast(U32)
    xgT = take(2 * P).rearrange("p (b n) -> p b n", b=2)
    gt, up, sg, gl, ac, acT = (take(2 * I).rearrange("p (b n) -> p b n", b=2) for _ in range(6))
    yo = take(4 * D).rearrange("p (b n) -> p b n", b=4)
    onesb = take(P // 2).bitcast(BF16)
    gub = biases[:, 0:4 * E * P].rearrange("p (e n) -> p e n", e=E)
    dnb = biases[:, 4 * E * P:5 * E * P].rearrange("p (e n) -> p e n", e=E)

    ones_set = sem("ex_ones")
    x_load = [sem(f"ex_x{i}") for i in range(FLIGHT)]
    y_store = [sem(f"ex_y{i}") for i in range(4)]
    x_full, x_evac = sem("ex_x_full"), sem("ex_x_evac")
    gu_full = sem("ex_gu_full")
    clipped = sem("ex_clipped")
    sig = sem("ex_sig")
    glu = sem("ex_glu")
    a_done = sem("ex_a_done")
    a_full, a_evac = sem("ex_a_full"), sem("ex_a_evac")
    dn_full, y_evac = sem("ex_dn_full"), sem("ex_y_evac")

    def run(eng, body):
        pipeline(eng, body, -1, 7, 8, SLOT_TILES + 3, FLIGHT, SLOT_TILES)

    with nc.Block() as block:
        @block.sync
        def _(sp):
            def body(s):
                if s.has(1):
                    b = s.buf(1)
                    if s.has(-7):
                        done = 2 * (s.n(-7) + 1)
                        sp.wait_ge(y_evac, done if isinstance(done, int) else sp.snap(sp.to_reg(done)))
                    sp.dma_start(xg[:, b, :], v.slots_in[bass.ds(s.n(1) * P, P), :]).then_inc(x_load[b], 16)

            run(sp, body)

        @block.tensor
        def _(pe):
            held = {}

            def expert(s, d):
                key = (s.k + d, id(s.J))
                if key not in held:
                    held[key] = nc.tensor.value_load(v.owner[0:1, bass.ds(s.n(d), 1)], min_val=0, max_val=E - 1)
                return held[key]

            def body(s):
                if s.has():
                    e = expert(s, 0)
                if s.has(1):
                    b = s.buf(1)
                    pe.wait_ge(x_load[b], 16 * (s.turn(1) + 1))
                    if s.has(-1):
                        pe.wait_ge(x_evac, s.n(-1) + 1)
                    nc.tensor.transpose(ps[:, 2 + b % 2, 0:P], xg[:, b, 0:D], eye).then_inc(x_full, 1)
                if s.has():
                    b = s.buf() % 2
                    if s.k == 0:
                        pe.wait_ge(ones_set, 1)
                    pe.wait_ge(x_evac, s.n() + 1)
                    if s.has(-2):
                        pe.wait_ge(clipped, 2 * (s.n(-2) + 1))
                    nc.tensor.matmul(ps[:, b, :], xgT[:, b, :], wgu[:, bass.ds(e, 1), :].rearrange("p a n -> p (a n)"),
                                     start=True, stop=False)
                    nc.tensor.matmul(ps[:, b, :], onesb, gub[:, bass.ds(e, 1), :].rearrange("p a n -> p (a n)"),
                                     start=False, stop=True).then_inc(gu_full, 1)
                if s.has(-3):
                    e3 = expert(s, -3)
                if s.has(-2):
                    b = s.buf(-2) % 2
                    pe.wait_ge(a_done, s.n(-2) + 1)
                    if s.has(-4):
                        pe.wait_ge(a_evac, s.n(-4) + 1)
                    for c in range(2):
                        mm = nc.tensor.transpose(ps[:, 4 + b, P * c:P * c + P], ac[:, b, P * c:P * c + P], eye)
                    mm.then_inc(a_full, 1)
                if s.has(-3):
                    b = s.buf(-3) % 2
                    pe.wait_ge(a_evac, s.n(-3) + 1)
                    if s.has(-5):
                        pe.wait_ge(y_evac, 2 * (s.n(-5) + 1))
                    o = ps[:, 6 + b, 0:D]
                    for c in range(2):
                        nc.tensor.matmul(o, acT[:, b, P * c:P * c + P],
                                         wdn[:, bass.ds(e3, 1), c, :].rearrange("p a n -> p (a n)"), start=(c == 0), stop=False)
                    nc.tensor.matmul(o, onesb, dnb[:, bass.ds(e3, 1), :].rearrange("p a n -> p (a n)"),
                                     start=False, stop=True).then_inc(dn_full, 1)

            run(pe, body)

        @block.scalar
        def _(act):
            def body(s):
                if s.has(1):
                    b = s.buf(1) % 2
                    act.wait_ge(x_full, s.n(1) + 1)
                    if s.has(-1):
                        act.wait_ge(gu_full, s.n(-1) + 1)
                    nc.scalar.activation(xgT[:, b, :], ps[:, 2 + b, 0:P], ACT.Copy).then_inc(x_evac, 1)
                if s.has(-2):
                    b = s.buf(-2) % 2
                    act.wait_ge(a_full, s.n(-2) + 1)
                    if s.has(-4):
                        act.wait_ge(dn_full, s.n(-4) + 1)
                    nc.scalar.activation(acT[:, b, :], ps[:, 4 + b, 0:I], ACT.Copy).then_inc(a_evac, 1)
                if s.has():
                    b = s.buf() % 2
                    act.wait_ge(clipped, 2 * s.n() + 1)
                    if s.has(-2):
                        act.wait_ge(glu, s.n(-2) + 1)
                    nc.scalar.activation(sg[:, b, :], gt[:, b, :], ACT.Sigmoid, scale=ALPHA).then_inc(sig, 1)

            run(act, body)

        @block.vector
        def _(dve):
            nc.vector.memset(onesb, 1.0).then_inc(ones_set, 1)

            def body(s):
                if s.has():
                    b = s.buf() % 2
                    dve.wait_ge(gu_full, s.n() + 1)
                    if s.has(-2):
                        dve.wait_ge(glu, s.n(-2) + 1)
                        dve.wait_ge(a_done, s.n(-2) + 1)
                    nc.vector.tensor_scalar(gt[:, b, :], ps[:, b, 0:I], LIMIT, None, ALU.min).then_inc(clipped, 1)
                    nc.vector.tensor_scalar(up[:, b, :], ps[:, b, I:2 * I], LIMIT, -LIMIT, ALU.min, ALU.max
                                            ).then_inc(clipped, 1)
                if s.has(-1):
                    b = s.buf(-1) % 2
                    dve.wait_ge(glu, s.n(-1) + 1)
                    dve.wait_ge(clipped, 2 * (s.n(-1) + 1))
                    if s.has(-3):
                        dve.wait_ge(a_full, s.n(-3) + 1)
                    nc.vector.scalar_tensor_tensor(ac[:, b, :], up[:, b, :], 1.0, gl[:, b, :], ALU.add, ALU.mult
                                                   ).then_inc(a_done, 1)
                if s.has(-3):
                    dve.wait_ge(dn_full, s.n(-3) + 1)
                    if s.has(-7):
                        dve.wait_ge(y_store[s.buf(-7) % 4], 16 * (2 * s.turn(-7) + s.buf(-7) // 4 + 1))
                    b = s.buf(-3)
                    nc.vector.tensor_tensor(rows[:, b:b + 1], xg[:, b, D:D + 1], cst[:, C_SPARE + b:C_SPARE + b + 1], ALU.max
                                            ).then_inc(y_evac, 1)
                    nc.vector.tensor_scalar(yo[:, b % 4, :], ps[:, 6 + b % 2, 0:D], xg[:, b, D + 1:D + 2], None, ALU.mult
                                            ).then_inc(y_evac, 1)

            run(dve, body)

        @block.gpsimd
        def _(pool):
            def body(s):
                if s.has(-4):
                    pool.wait_ge(y_evac, 2 * (s.n(-4) + 1))
                if s.has():
                    b = s.buf() % 2
                    pool.wait_ge(sig, s.n() + 1)
                    if s.has(-2):
                        pool.wait_ge(a_done, s.n(-2) + 1)
                    nc.gpsimd.tensor_tensor(gl[:, b, :], gt[:, b, :], sg[:, b, :], ALU.mult).then_inc(glu, 1)
                if s.has(-4):
                    b = s.buf(-4)
                    nc.gpsimd.indirect_dma_start(v.mixed[:, :], bass.IndirectOffsetOnAxis(ap=rows[:, b:b + 1], axis=0),
                                                 yo[:, b % 4, :], None).then_inc(y_store[b % 4], 16)

            run(pool, body)
            for b in range(4):
                pool.wait_ge(y_store[b], 16 * (SLOT_TILES // 4))


def middle(nc, v):
    sem = v.sem
    ps, gate, x, xnT, cst, stat = v.ps, v.gate, v.x, v.xnT, v.cst, v.stat
    eye = cst[:, C_EYE:C_EYE + P]
    flat = v.probs[:].rearrange("p a b -> p (a b)")
    ys = flat[:, 0:4096].rearrange("p (g k n) -> p g k n", g=4, k=TOPK)
    sgm = flat[:, 4096:5120].rearrange("p (g n) -> p g n", g=2)
    sqr = flat[:, 5120:6144].rearrange("p (g n) -> p g n", g=2)
    got = [sem(f"mi_loaded{i}") for i in range(4)]
    cleared = sem("mi_stacks_cleared")
    mix, s1 = sem("mi_mix"), sem("mi_sigmoid")
    scaled = sem("mi_scaled")
    res, var, nrm = sem("mi_residual"), sem("mi_variance"), sem("mi_normalise")
    sqd, sqt = sem("mi_squares"), sem("mi_sqrt")
    tr, trc, fm, s2, gd = sem("mi_tr"), sem("mi_trc"), sem("mi_ffn"), sem("mi_ffn_sigmoid"), sem("mi_gate")

    def tiles(a, g):
        return a[:, 4 * g:4 * g + 4, :]

    def four(a):
        return a.rearrange("p (t d) -> p t d", d=D)

    with nc.Block() as block:
        @block.sync
        def _(sp):
            for g in range(G):
                if g >= 4:
                    sp.wait_ge(res, 4 * (g - 4) + 1)
                for k in range(TOPK):
                    first = SPARE + B * T * k + 4 * P * g
                    sp.dma_start(four(ys[:, g % 4, k]),
                                 v.mixed[first:first + 4 * P, :].rearrange("(c p) d -> p c d", p=P)).then_inc(got[g % 4], 16)

        @block.gpsimd
        def _(pool):
            for g in range(G + 1):
                if g in (2, 3):
                    nc.gpsimd.memset(v.qs[:, g - 1].bitcast(F32), 0.0).then_inc(cleared, 1)
                if g == 4:
                    nc.gpsimd.memset(v.ks[:, 1].bitcast(F32), 0.0).then_inc(cleared, 1)
                if g < G:
                    y, z = ys[:, g % 4, 0], ys[:, g % 4, 1]
                    pool.wait_ge(got[g % 4], 32 * (g // 4 + 1))
                    nc.gpsimd.tensor_tensor(y, y, z, ALU.add).then_inc(mix, 1)
                    pool.wait_ge(mix, 2 * g + 1)
                    nc.gpsimd.tensor_tensor(four(z), four(y), tiles(gate, g), ALU.mult).then_inc(mix, 1)
                if g >= 1:
                    z = ys[:, (g - 1) % 4, 1]
                    pool.wait_ge(s1, g)
                    pool.wait_ge(mix, 2 * g)
                    nc.gpsimd.tensor_tensor(z, z, sgm[:, (g - 1) % 2], ALU.mult).then_inc(scaled, 1)
            pool.wait_ge(cleared, 3)
            pool.wait_ge(scaled, G)
            nc.gpsimd.memset(v.ks[32:64, 1].bitcast(F32), PAIR_OF_ONES).then_inc(cleared, 1)
        @block.vector
        def _(dve):
            def residual(g):
                n = 4 * g
                dve.wait_ge(scaled, g + 1)
                nc.vector.tensor_tensor(tiles(x, g), tiles(x, g), four(ys[:, g % 4, 1]), ALU.add).then_inc(res, 1)
                dve.wait_ge(res, n + 1)
                nc.vector.tensor_reduce(stat[:, 0, 4 * g:4 * g + 4], tiles(x, g), AX.X, ALU.add).then_inc(res, 1)
                dve.wait_ge(res, n + 2)
                nc.vector.tensor_scalar(stat[:, 3, 4 * g:4 * g + 4], stat[:, 0, 4 * g:4 * g + 4], 1.0 / D, None, ALU.mult
                                        ).then_inc(res, 1)
                dve.wait_ge(res, n + 3)
                nc.vector.tensor_tensor(tiles(gate, g), tiles(x, g),
                                        stat[:, 3, 4 * g:4 * g + 4].unsqueeze(2).broadcast_to([P, 4, D]), ALU.subtract
                                        ).then_inc(res, 1)

            def variance(g):
                dve.wait_ge(sqd, g + 1)
                nc.vector.tensor_reduce(stat[:, 1, 4 * g:4 * g + 4], four(sqr[:, g % 2]), AX.X, ALU.add).then_inc(var, 1)

            def normalise(g):
                r = stat[:, 2, 4 * g:4 * g + 4]
                dve.wait_ge(sqt, g + 1)
                nc.vector.reciprocal(r, r).then_inc(nrm, 1)
                dve.wait_ge(nrm, 2 * g + 1)
                nc.vector.tensor_tensor(tiles(gate, g), tiles(gate, g), r.unsqueeze(2).broadcast_to([P, 4, D]), ALU.mult
                                        ).then_inc(nrm, 1)

            def silu(g):
                dve.wait_ge(s2, g + 1)
                nc.vector.tensor_tensor(tiles(gate, g), four(ps[:, 4 + g % 4, :]), tiles(gate, g), ALU.mult).then_inc(gd, 1)

            for g in range(G + 3):
                for stage, lag in ((residual, 0), (normalise, 2), (variance, 1), (silu, 3)):
                    if 0 <= g - lag < G:
                        stage(g - lag)

        @block.scalar
        def _(act):
            def mixture_sigmoid(g):
                act.wait_ge(mix, 2 * g + 1)
                if g >= 2:
                    act.wait_ge(scaled, g - 1)
                nc.scalar.activation(sgm[:, g % 2], ys[:, g % 4, 0], ACT.Sigmoid).then_inc(s1, 1)

            def square(g):
                act.wait_ge(res, 4 * g + 4)
                if g >= 2:
                    act.wait_ge(var, g - 1)
                nc.scalar.activation(four(sqr[:, g % 2]), tiles(gate, g), ACT.Square).then_inc(sqd, 1)

            def root(g):
                act.wait_ge(var, g + 1)
                nc.scalar.activation(stat[:, 2, 4 * g:4 * g + 4], stat[:, 1, 4 * g:4 * g + 4], ACT.Sqrt,
                                     bias=v.eps[:, 0:1], scale=1.0 / D).then_inc(sqt, 1)

            def transposed(g):
                act.wait_ge(tr, g + 1)
                nc.scalar.activation(xnT[:, 512 * g:512 * g + 512], ps[:, g % 4, :], ACT.Copy).then_inc(trc, 1)

            def ffn_sigmoid(g):
                act.wait_ge(fm, g + 1)
                nc.scalar.activation(tiles(gate, g), four(ps[:, 4 + g % 4, :]), ACT.Sigmoid).then_inc(s2, 1)

            for g in range(-1, G + 3):
                for stage, lag in ((mixture_sigmoid, -1), (ffn_sigmoid, 3), (square, 0), (root, 1), (transposed, 2)):
                    if 0 <= g - lag < G:
                        stage(g - lag)

        @block.tensor
        def _(pe):
            for g in range(G):
                pe.wait_ge(nrm, 2 * g + 2)
                if g >= 4:
                    pe.wait_ge(trc, g - 3)
                for c in range(4):
                    mm = nc.tensor.transpose(ps[:, g % 4, P * c:P * c + P], gate[:, 4 * g + c, :], eye)
                mm.then_inc(tr, 1)
                pe.wait_ge(trc, g + 1)
                if g >= 4:
                    pe.wait_ge(gd, g - 3)
                for c in range(4):
                    t = 4 * g + c
                    o = ps[:, 4 + g % 4, D * c:D * c + D]
                    nc.tensor.matmul(o, v.ones[0:1, 0:P], v.fb[:], start=(c == 0), stop=False, skip_group_check=True)
                    mm = nc.tensor.matmul(o, xnT[:, P * t:P * t + P], v.feff[:], start=False, stop=True,
                                          skip_group_check=True)
                mm.then_inc(fm, 1)


class Units:

    def __init__(self, count):
        self.count = count
        self.order = [("A", 0), ("A", 1), ("A", 2)]
        for j in range(count - 3):
            self.order += [("B", j), ("A", j + 3)]
        self.order += [("B", j) for j in range(count - 3, count)]

    def exists(self, k, kind):
        return 0 <= (k if kind == "A" else k - 1) < B

    def slot(self, k, pos):
        return (len(self.order) * k + pos) % 3

    def before(self, k, pos):
        n = len(self.order) * k + pos - 3
        while n >= 0:
            kk, p = divmod(n, len(self.order))
            kind, j = self.order[p]
            if self.exists(kk, kind):
                return kind, j, kk - k
            n -= 3
        return None


def attention(nc, v, layer):
    U = Units(8 if layer == 0 else 6)
    NU = U.count
    ps, x, gate, xnT, probs, qs, ks = v.ps, v.x, v.gate, v.xnT, v.probs, v.qs, v.ks
    cst, vpad, onespad, cols, xb, vcen = v.cst, v.vpad, v.onespad, v.cols, v.xb, v.vcen
    qkf, qkr, qk3, mx, mres, m3, mT = v.qkf, v.qkr, v.qk3, v.mx, v.mres, v.m3, v.mT
    rden, on, yt, eyeb, maskA, maskB = v.rden, v.on, v.yt, v.eyeb, v.maskA, v.maskB
    wqk, wo = (v.wqk0, v.wo0) if layer == 0 else (v.wqk1, v.wo1)
    bq, bk = (0, 1) if layer == 0 else (3, 4)
    ring = ps[:, 0:6, :].rearrange("p (s b) n -> p s (b n)", s=3)
    od = ps[:, 6, :]
    misc = ps[:, 7, :]

    def sem(name):
        return v.sem(f"l{layer}_{name}")

    full = {"A": sem("a_full"), "B": sem("b_full")}
    used = {"A": sem("a_used"), "B": sem("b_used")}
    exp_done = sem("exp_done") if layer == 0 else used["B"]
    pv_done = sem("pv_done")
    if layer:
        added = sem("added")
        sum_done = sem("sum_done")
    qk_full, v_full = sem("qk_full"), sem("v_full")
    y_full, mt_full = sem("y_full"), sem("mt_full")
    qk_evac, v_evac = sem("qk_evac"), sem("v_evac")
    y_evac, mt_evac = sem("y_evac"), sem("mt_evac")
    s1_done, r1_done, s2_done, s3_done = sem("s1"), sem("r1"), sem("s2"), sem("s3")
    xb_done = sem("xb")
    max_parts = sem("max_parts")
    rd_done, on_done = sem("rd"), sem("on")
    part_st = [sem(f"part_st{i}") for i in range(3)]
    stack_ld = [sem(f"stack_ld{i}") for i in range(3)]
    max_st = [sem(f"max_st{i}") for i in range(3)]
    max_ld = [sem(f"max_ld{i}") for i in range(3)]
    if layer == 0:
        sorted_in = sem("sorted_in")
        labelled = sem("labelled")
    else:
        e_full, e_evac = sem("e_full"), sem("e_evac")
        fin_done = sem("fin")
        out_st = [sem(f"out_st{i}") for i in range(3)]
    STACK_DMAS = 10
    GROUPS = 4
    LOOP = 3

    MISC = ["QK", "V", "E", "Y", "M"] if layer else ["QK", "V", "Y", "M"]
    LAG = {"QK": 1, "V": 0, "E": -2, "Y": -2, "M": 0}
    EVAC = {"QK": qk_evac, "V": v_evac, "Y": y_evac, "M": mt_evac}
    if layer:
        EVAC["E"] = e_evac

    COUNT = {"QK": 2, "V": 3 if layer else 2, "E": 1, "Y": 1, "M": 1}

    def misc_free(eng, s, use):
        at = MISC.index(use)
        for back in range(0, -3, -1):
            for m in reversed(MISC[:at] if back == 0 else MISC):
                if s.has(back + LAG[m]):
                    eng.wait_ge(EVAC[m], COUNT[m] * (s.n(back + LAG[m]) + 1))
                    return

    def heads_of(kind, j):
        if layer == 0:
            return range(4 * (j // 2), 4 * (j // 2) + 4), j % 2, T
        if j < 4:
            return range(4 * j, 4 * j + 4), (1 if kind == "A" else 0), T
        return range(8 * (j - 4), 8 * (j - 4) + 8), (0 if kind == "A" else 1), P

    def emit(eng, body):
        pipeline(eng, body, -1, LOOP, 4, B + 1, 3, B)

    with nc.Block() as block:
        @block.sync
        def _(sp):
            def ahead(*counts):
                return [c if isinstance(c, int) else sp.snap(sp.to_reg(c)) for c in counts]

            def stacks(s):
                b = s.buf(1)
                made, stored, scored = ahead(s.n(1) + 1, 16 * (s.turn(1) + 1), NU * (s.n(-2) + 1))
                sp.wait_ge(s3_done, made)
                sp.dma_start(v.parts_d[b].rearrange("a c p t -> p a c t"), qk3[:]).then_inc(part_st[b], 16)
                sp.wait_ge(part_st[b], stored)
                if s.has(-2):
                    sp.wait_ge(full["B"], scored)
                part = v.parts_d[b].rearrange("a c (d h) t -> a (c d) h t", d=HD)
                for row, n in ((0, 3), (3, 2), (5, 1)):
                    sp.dma_start(qs[8 * row:8 * (row + n), b], part[0, 0:8 * n]).then_inc(stack_ld[b], 16)
                for row, c in enumerate((0, 0, 0, 1, 1, 2)):
                    sp.dma_start(ks[8 * row:8 * row + 8, b], part[1, 8 * c:8 * c + 8]).then_inc(stack_ld[b], 16)
                sp.dma_start(qs[QROWS:QROWS + PARTS, b], v.zrow[:].unsqueeze(1).broadcast_to([PARTS, H, T])
                             ).then_inc(stack_ld[b], 16)

            def maxima(s):
                b = s.buf()
                turned, stored, scored = ahead(s.n() + 1, 16 * (s.turn() + 1), NU * (s.n() + 1))
                sp.wait_ge(mt_evac, turned)
                sp.dma_start(v.max_d[b].rearrange("c t h p -> (c t h) p"), mT[:]).then_inc(max_st[b], 16)
                sp.wait_ge(max_st[b], stored)
                sp.wait_ge(full["A"], scored)
                for t in range(2):
                    sp.dma_start(qs[QROWS:QROWS + PARTS, b, :, P * t:P * t + P], v.max_d[b, :, t]
                                 ).then_inc(max_ld[b], 16)

            def body(s):
                if s.has(1):
                    stacks(s)
                if s.has():
                    maxima(s)

            emit(sp, body)
            if layer == 0:
                sp.wait_ge(full["B"], NU * (B - 1))
                sp.dma_start(v.wgu, v.gu_w.rearrange("e h n -> h e n")).then_inc(v.w_load, 16)
                sp.dma_start(v.wdn, v.down_w.rearrange("e (c i) h -> i e c h", c=2)).then_inc(v.w_load, 16)
                sp.wait_ge(v.b_zero, 1)
                sp.dma_start(v.biases[0:PARTS, :], v.bias3_d[:].rearrange("c r n -> c (r n)")).then_inc(v.b_load, 16)
                sp.wait_ge(v.w_load, 32)
                sp.wait_ge(v.b_load, 16)
            for b in range(3):
                uses = len(range(b, B, 3))
                sp.wait_ge(max_ld[b], 32 * uses)
                if layer:
                    sp.wait_ge(out_st[b], 16 * uses)

        def rest_one(eng, ops, s):
            eng.wait_ge(s1_done, s.n(1) + 1)
            ops.tensor_tensor(qkr[:], qkf[:], qk3[:, :, 0, :], ALU.subtract).then_inc(r1_done, 1)

        def rest_two(eng, ops, s):
            eng.wait_ge(s2_done, s.n(1) + 1)
            ops.tensor_tensor(qk3[:, :, 2, :], qkr[:], qk3[:, :, 1, :], ALU.subtract).then_inc(s3_done, 1)

        def add_tiles(pool, s, g):
            pool.wait_ge(pv_done, NU * s.n(-2) + 4 + g // 2 + 1)
            later = probs[:, g, :].rearrange("p (h t) -> p h t", t=T)[:, :, P:T]
            second = probs[:, 4 + g // 2, :].rearrange("p (h t) -> p h t", t=P)[:, 4 * (g % 2):4 * (g % 2) + 4, :]
            nc.gpsimd.tensor_tensor(later, later, second, ALU.add).then_inc(added, 1)

        @block.gpsimd
        def _(pool):
            if layer == 0:
                for k in range(TOPK):
                    if k:
                        pool.wait_ge(sorted_in, 16 * NT)
                    nc.gpsimd.tensor_copy(v.rows[:, :, D:D + 1], v.rowid[:, k].unsqueeze(2)).then_inc(labelled, 1)
                    nc.gpsimd.tensor_copy(v.rows[:, :, D + 1:D + 2], v.wt[:, k].unsqueeze(2)).then_inc(labelled, 1)
                    pool.wait_ge(labelled, 2 * (k + 1))
                    for t in range(NT):
                        nc.gpsimd.indirect_dma_start(v.slots_in[:, :],
                                                     bass.IndirectOffsetOnAxis(ap=v.place[:, k, t:t + 1], axis=0),
                                                     v.rows[:, t, :], None).then_inc(sorted_in, 16)
                pool.wait_ge(sorted_in, 16 * TOPK * NT)

            def body(s):
                if layer and s.has(-2):
                    for g in range(GROUPS):
                        add_tiles(pool, s, g)
                if s.has(1) and (layer or s.k >= LOOP):
                    rest_one(pool, nc.gpsimd, s)
                    rest_two(pool, nc.gpsimd, s)

            emit(pool, body)

        @block.vector
        def _(dve):
            def maximum(s, j, slot):
                heads, t, w = heads_of("A", j)
                dve.wait_ge(full["A"], NU * s.n() + j + 1)
                nc.vector.tensor_reduce(mx[:, s.buf(), t, heads[0]:heads[-1] + 1],
                                        ring[:, slot].rearrange("p (h n) -> p h n", n=w), AX.X, ALU.max
                                        ).then_inc(used["A"], 1)

            def add_bias(s, j, slot):
                heads, c, _ = heads_of("B", j)
                off = P * (1 - c)
                dve.wait_ge(full["B"], NU * s.n(-1) + j + 1)
                if s.has(-2):
                    dve.wait_ge(pv_done, NU * s.n(-2) + j + 1)
                nc.vector.tensor_tensor(probs[:, j, :].rearrange("p (h n) -> p h n", n=T),
                                        ring[:, slot].rearrange("p (h n) -> p h n", n=T),
                                        v.tabB[:, heads[0]:heads[0] + 4, off:off + T], ALU.add).then_inc(used["B"], 1)

            def divide(s):
                b = s.buf(-2)
                if layer == 0:
                    dve.wait_ge(pv_done, NU * (s.n(-2) + 1))
                else:
                    dve.wait_ge(sum_done, GROUPS * (s.n(-2) + 1))
                nc.vector.reciprocal(rden[:], od[:, T:2 * T]).then_inc(rd_done, 1)
                dve.wait_ge(rd_done, s.n(-2) + 1)
                if s.has(-3):
                    dve.wait_ge(y_full, s.n(-3) + 1)
                if layer == 0:
                    nc.vector.tensor_tensor(on[:], od[:, 0:T], rden[:], ALU.mult).then_inc(on_done, 1)
                else:
                    nc.vector.scalar_tensor_tensor(on[:], od[:, 0:T], cols[:, 5:6], rden[:], ALU.mult, ALU.mult
                                                   ).then_inc(on_done, 1)

            def add_shape(s):
                b = s.buf(-2)
                dve.wait_ge(e_full, s.n(-2) + 1)
                dve.wait_ge(on_done, s.n(-2) + 1)
                nc.vector.tensor_tensor(on[:], misc[:, 0:T], on[:], ALU.add).then_inc(e_evac, 1)

            def maximum_parts(s):
                m = mx[:, s.buf()]
                n = 4 * s.n()
                dve.wait_ge(used["A"], NU * (s.n() + 1))
                if s.has(-1):
                    dve.wait_ge(mt_full, s.n(-1) + 1)
                nc.vector.tensor_scalar(m3[:, 0], m, -1.0, None, ALU.mult).then_inc(max_parts, 1)
                dve.wait_ge(max_parts, n + 1)
                nc.vector.scalar_tensor_tensor(mres[:], m, -1.0, m3[:, 0], ALU.mult, ALU.subtract).then_inc(max_parts, 1)
                dve.wait_ge(max_parts, n + 2)
                nc.vector.tensor_copy(m3[:, 1], mres[:]).then_inc(max_parts, 1)
                dve.wait_ge(max_parts, n + 3)
                nc.vector.tensor_tensor(m3[:, 2], mres[:], m3[:, 1], ALU.subtract).then_inc(max_parts, 1)

            def project(s):
                y = yt[:].rearrange("p (c d) -> p c d", c=2)
                o = misc[:, 0:T].rearrange("p (c d) -> p c d", c=2)
                dve.wait_ge(y_full, s.n(-2) + 1)
                g = gate[:, bass.ds(s.n(-2) * 2, 2), :]
                if layer == 0:
                    if s.k == 2:
                        dve.wait_ge(sorted_in, 16 * TOPK * NT)
                    nc.vector.tensor_tensor(g, o, v.bo[:].unsqueeze(1).broadcast_to([P, 2, D]), ALU.add).then_inc(y_evac, 1)
                else:
                    xt = x[:, bass.ds(s.n(-2) * 2, 2), :]
                    if s.has(-3):
                        dve.wait_ge(out_st[s.buf(-3)], 16 * (s.turn(-3) + 1))
                    nc.vector.tensor_tensor(y, o, g, ALU.mult).then_inc(y_evac, 1)
                    dve.wait_ge(y_evac, s.n(-2) + 1)
                    nc.vector.tensor_tensor(y, xt, y, ALU.add).then_inc(fin_done, 1)

            def body(s):
                if layer == 0 and s.has(-2):
                    divide(s)
                for pos, (kind, j) in enumerate(U.order):
                    if U.exists(s.k, kind):
                        (maximum if kind == "A" else add_bias if layer == 0 else lambda *a: None)(s, j, U.slot(s.k, pos))
                    if kind == "A" and j == NU - 1 and s.has():
                        maximum_parts(s)
                    if layer and pos == 3 and s.has(-2):
                        divide(s)
                    if layer and pos == 5 and s.has(-2):
                        add_shape(s)
                    if layer == 0 and s.has(1):
                        if pos == 1 and s.k < LOOP:
                            rest_one(dve, nc.vector, s)
                        if pos == 4 and s.k < LOOP:
                            rest_two(dve, nc.vector, s)
                    if pos == 7 and s.has(-2):
                        project(s)
                if layer == 0 and s.k == B:
                    dve.wait_ge(full["A"], NU * B)
                    nc.vector.memset(v.biases.bitcast(F32), 0.0).then_inc(v.b_zero, 1)

            emit(dve, body)

        @block.scalar
        def _(act):
            def parts_one(s):
                b = s.buf(1)
                act.wait_ge(qk_full, s.n(1) + 1)
                if s.has():
                    act.wait_ge(s3_done, s.n() + 1)
                nc.scalar.activation(qkf[:, 0], misc[:, 0:T], ACT.Identity, bias=cols[:, bq:bq + 1], scale=QSCALE
                                     ).then_inc(qk_evac, 1)
                nc.scalar.activation(qkf[:, 1], misc[:, T:2 * T], ACT.Identity, bias=cols[:, bk:bk + 1]
                                     ).then_inc(qk_evac, 1)
                act.wait_ge(qk_evac, 2 * (s.n(1) + 1))
                if s.has():
                    act.wait_ge(part_st[s.buf()], 16 * (s.turn() + 1))
                nc.scalar.activation(qk3[:, :, 0, :], qkf[:], ACT.Copy).then_inc(s1_done, 1)

            def parts_two(s):
                act.wait_ge(r1_done, s.n(1) + 1)
                nc.scalar.activation(qk3[:, :, 1, :], qkr[:], ACT.Copy).then_inc(s2_done, 1)

            def values(s):
                b = s.buf()
                act.wait_ge(v_full, s.n() + 1)
                if s.has(-3):
                    act.wait_ge(pv_done, NU * (s.n(-3) + 1))
                w = P if layer == 0 else 2 * P
                pv = misc[:, 0:2 * w].rearrange("p (c a n) -> p c a n", c=2, n=P)
                dst = vpad[:, b].rearrange("p c (i w) -> p c i w", w=40)
                for c in range(2):
                    nc.scalar.activation(dst[:, 4 * c:4 * c + 4, :, 0:HD],
                                               pv[:, c, 0, :].rearrange("p (q i d) -> p q i d", q=4, i=4), ACT.Copy
                                         ).then_inc(v_evac, 1)
                if layer:
                    if s.has(-3):
                        act.wait_ge(e_full, s.n(-3) + 1)
                    nc.scalar.activation(vcen[:, b], pv[:, :, 1, :], ACT.Copy).then_inc(v_evac, 1)

            def max_rows(s):
                b = s.buf()
                act.wait_ge(mt_full, s.n() + 1)
                if s.has(-1):
                    act.wait_ge(max_st[s.buf(-1)], 16 * (s.turn(-1) + 1))
                nc.scalar.activation(mT[:], misc[0:PARTS * 2 * H, 0:P // 2].bitcast(BF16), ACT.Copy).then_inc(mt_evac, 1)

            def exponential(s, j, slot):
                if layer == 0:
                    act.wait_ge(used["B"], NU * s.n(-1) + j + 1)
                    nc.scalar.activation(probs[:, j, :], probs[:, j, :], ACT.Exp).then_inc(exp_done, 1)
                else:
                    act.wait_ge(full["B"], NU * s.n(-1) + j + 1)
                    if s.has(-2):
                        act.wait_ge(sum_done, GROUPS * s.n(-2) + (j + 1 if j < 4 else 2 * (j - 4) + 2))
                    nc.scalar.activation(probs[:, j, :], ring[:, slot], ACT.Exp).then_inc(exp_done, 1)

            def store(s):
                b = s.buf(-2)
                act.wait_ge(fin_done, s.n(-2) + 1)
                act.dma_start(v.out[bass.ds(s.n(-2), 1)].rearrange("b (c p) d -> p (b c) d", p=P),
                             yt[:].rearrange("p (c d) -> p c d", c=2)).then_inc(out_st[b], 16)

            def body(s):
                if s.has():
                    if s.has(-1):
                        act.wait_ge(v_full, s.n(-1) + 1)
                    nc.scalar.activation(xb[:], xnT[:, bass.ds(s.n() * T, T)], ACT.Copy).then_inc(xb_done, 1)
                for pos, (kind, j) in enumerate(U.order):
                    if kind == "B" and U.exists(s.k, kind):
                        exponential(s, j, U.slot(s.k, pos))
                    if pos == 1 and s.has(1):
                        parts_one(s)
                    if pos == 4 and s.has(1):
                        parts_two(s)
                    if pos == 4 and s.has():
                        values(s)
                if layer and s.has(-2):
                    store(s)
                if s.has():
                    max_rows(s)

            emit(act, body)

        @block.tensor
        def _(pe):
            def batch_tokens(s, d):
                return xnT[:, bass.ds(s.n(d) * T, T)]

            def slot_free(s, pos):
                former = U.before(s.k, pos)
                if former:
                    kind, j, back = former
                    pe.wait_ge(used[kind], NU * s.n(back - (kind == "B")) + j + 1)

            def first_pass(s, pos, j):
                b, o = s.buf(), ring[:, U.slot(s.k, pos)]
                heads, t, w = heads_of("A", j)
                if j == 0:
                    pe.wait_ge(stack_ld[b], 16 * STACK_DMAS * (s.turn() + 1))
                slot_free(s, pos)
                for n, h in enumerate(heads):
                    last = n == len(heads) - 1
                    q = qs[:, b, h, P * t:P * t + P]
                    at = o[:, w * n:w * n + w]
                    if layer == 0:
                        if n % 2 == 0:
                            off = P * (1 - t)
                            nc.tensor.matmul(o[:, T * n:T * n + 2 * T], eyeb[:], v.tabA[:, h:h + 2, off:off + T],
                                             start=True, stop=False, skip_group_check=True)
                        mm = nc.tensor.matmul(at, q, ks[:, b, h, :], start=False, stop=True, skip_group_check=True)
                    elif w == T:
                        nc.tensor.matmul(at, q, ks[:, b, h, :], start=(n % 2 == 0), stop=False, skip_group_check=True)
                        mm = nc.tensor.matmul(at[:, P:T], eyeb[:], maskA[:], start=False, stop=True, skip_group_check=True)
                    else:
                        if n % 4 == 0:
                            nc.tensor.matmul(o[:, P * n:P * n + 4 * P], eyeb[:], maskA[:].unsqueeze(1).broadcast_to([P, 4, P]),
                                             start=True, stop=False, skip_group_check=True)
                        mm = nc.tensor.matmul(at, q, ks[:, b, h, 0:P], start=False, stop=True, skip_group_check=True)
                    if last:
                        mm.then_inc(full["A"], 1)

            def second_pass(s, pos, j):
                b, o = s.buf(-1), ring[:, U.slot(s.k, pos)]
                heads, c, w = heads_of("B", j)
                if j == 0:
                    pe.wait_ge(max_ld[b], 32 * (s.turn(-1) + 1))
                slot_free(s, pos)
                for n, h in enumerate(heads):
                    k = ks[:, b, h, P * c:P * c + P]
                    at = o[:, w * n:w * n + w]
                    if layer == 0:
                        mm = nc.tensor.matmul(at, k, qs[:, b, h, :], start=(n % 2 == 0), stop=True, skip_group_check=True)
                    elif w == T:
                        nc.tensor.matmul(at, k, qs[:, b, h, :], start=(n % 2 == 0), stop=False, skip_group_check=True)
                        mm = nc.tensor.matmul(at[:, 0:P], eyeb[:], maskB[:], start=False, stop=True, skip_group_check=True)
                    else:
                        if n % 4 == 0:
                            nc.tensor.matmul(o[:, P * n:P * n + 4 * P], eyeb[:], maskB[:].unsqueeze(1).broadcast_to([P, 4, P]),
                                             start=True, stop=False, skip_group_check=True)
                        mm = nc.tensor.matmul(at, k, qs[:, b, h, P:T], start=False, stop=True, skip_group_check=True)
                    if n == len(heads) - 1:
                        mm.then_inc(full["B"], 1)

            def values(s, d, j):
                b = s.buf(d)
                heads, c, w = heads_of("B", j)
                if j == 0:
                    pe.wait_ge(v_evac, COUNT["V"] * (s.n(d) + 1))
                    if s.has(d - 1):
                        pe.wait_ge(on_done, s.n(d - 1) + 1)
                pe.wait_ge(exp_done, NU * s.n(d) + j + 1)
                t0 = 0 if w == T else P
                for what in range(2 if layer == 0 else 1):
                    for n, h in enumerate(heads):
                        i, q = h // 4, h % 4
                        lhs = vpad[:, b, 4 * c + q, 32 * i:32 * i + 32] if what == 0 else onespad[:, i, :]
                        mm = nc.tensor.matmul(od[32 * q:32 * q + 32, T * what + t0:T * what + T], lhs,
                                              probs[:, j, w * n:w * n + w], start=(j == 0 and what == 0 and i == 0),
                                              stop=(j == NU - 1), skip_group_check=True)
                mm.then_inc(pv_done, 1)

            def sums(s, g):
                pe.wait_ge(added, GROUPS * s.n(-2) + g + 1)
                for q in range(4):
                    mm = nc.tensor.matmul(od[32 * q:32 * q + 32, T:2 * T], onespad[:, g, :], probs[:, g, T * q:T * q + T],
                                          start=False, stop=(g == GROUPS - 1), skip_group_check=True)
                mm.then_inc(sum_done, 1)

            def body(s):
                if s.has(-2):
                    values(s, -2, NU - 2)
                    values(s, -2, NU - 1)
                for pos, (kind, j) in enumerate(U.order):
                    if pos == 1 and s.has(1):
                        misc_free(pe, s, "QK")
                        for a in range(2):
                            mm = nc.tensor.matmul(misc[:, T * a:T * a + T], wqk[:, a, :], batch_tokens(s, 1),
                                                  start=True, stop=True)
                        mm.then_inc(qk_full, 1)
                    if pos == 4 and s.has():
                        misc_free(pe, s, "V")
                        pe.wait_ge(xb_done, s.n() + 1)
                        n = P if layer == 0 else 2 * P
                        w = v.wv0[:] if layer == 0 else v.wv1[:].rearrange("p a n -> p (a n)")
                        for c in range(2):
                            mm = nc.tensor.matmul(misc[:, n * c:n * c + n], xb[:, P * c:P * c + P], w,
                                                  start=True, stop=True)
                        mm.then_inc(v_full, 1)
                    if layer and pos == 5 and s.has(-2):
                        misc_free(pe, s, "E")
                        nc.tensor.matmul(misc[:, 0:T], v.wvs[:], batch_tokens(s, -2), start=True, stop=False,
                                         skip_group_check=True)
                        vc = vcen[:, s.buf(-2)]
                        nc.tensor.matmul(misc[:, 0:T], vc[:, 0], cst[:, C_UT:C_UT + T], start=False, stop=False,
                                         skip_group_check=True)
                        nc.tensor.matmul(misc[:, P:T], vc[:, 1], cst[:, C_UT + T:C_UT + T + P], start=False, stop=True,
                                         skip_group_check=True).then_inc(e_full, 1)
                    if pos == 7 and s.has(-2):
                        misc_free(pe, s, "Y")
                        pe.wait_ge(on_done, s.n(-2) + 1)
                        for c in range(2):
                            mm = nc.tensor.matmul(misc[:, D * c:D * c + D], on[:, P * c:P * c + P], wo[:],
                                                  start=True, stop=True)
                        mm.then_inc(y_full, 1)
                    if U.exists(s.k, kind):
                        (first_pass if kind == "A" else second_pass)(s, pos, j)
                    if kind == "B" and j >= 2 and s.has(-1):
                        values(s, -1, j - 2)
                    if layer and pos in (1, 2) and s.has(-2):
                        sums(s, 2 * pos - 2)
                        sums(s, 2 * pos - 1)
                if s.has():
                    misc_free(pe, s, "M")
                    pe.wait_ge(max_parts, 4 * (s.n() + 1))
                    nc.tensor.transpose(misc[0:PARTS * 2 * H, 0:P // 2].bitcast(BF16),
                                        m3[:].rearrange("p c t h -> p (c t h)"), eyeb[:]).then_inc(mt_full, 1)

            emit(pe, body)


_INS = ['L0_attn_x', 'L0_attn_w_qkv', 'L0_attn_b_qkv', 'L0_attn_w_out', 'L0_attn_b_out', 'L0_attn_w1_rpe',
        'L0_attn_b1_rpe', 'L0_attn_w2_rpe', 'L0_attn_b2_rpe', 'L0_ffn_router_weight', 'L0_ffn_router_bias',
        'L0_ffn_gate_up_proj', 'L0_ffn_gate_up_bias', 'L0_ffn_down_proj', 'L0_ffn_down_bias', 'L1_attn_qk_w',
        'L1_attn_qk_b', 'L1_attn_v_w', 'L1_attn_cproj_w', 'L1_attn_resid_gain', 'L1_attn_skip_gain',
        'L1_attn_centre_gain', 'L1_ffn_W', 'L1_ffn_b', 'L1_ffn_V_r', 'L1_ffn_C']


def _constants():
    import numpy as np
    c = np.zeros((P, C_ALL), np.float32)
    p = np.arange(P)[:, None]
    n = np.arange(P)[None, :]
    t = np.arange(T)[None, :]
    c[:, C_EYE:C_EYE + P] = p == n
    c[:, C_MA:C_MA + P] = np.where(n <= p, 0.0, NEG)
    c[:, C_MB:C_MB + P] = np.where(n >= p, 0.0, NEG)
    share = np.float32(1.0) / (t + 1).astype(np.float32)
    c[:, C_UT:C_UT + T] = np.where(p <= t, share, 0.0)
    c[:, C_UT + T:C_UT + T + P] = np.where(P + p <= t, share, 0.0)[:, P:T]
    c[:, C_BEFORE:C_BEFORE + P] = p < n
    c[:, C_TILES:C_TILES + NT] = P * np.arange(NT)[None, :]
    c[:, C_TILES + NT:C_ROWS] = np.arange(SLOT_TILES)[None, :]
    c[:, C_ROWS:C_SPARE] = SPARE + P * np.arange(NT)[None, :] + p
    c[:, C_SPARE:C_ALL] = P * np.arange(FLIGHT)[None, :] + p
    c[:, C_FLIP:C_FLIP + P] = p == P - 1 - n
    c[:, C_RANK:C_RANK + E] = E - np.arange(E)[None, :]
    r = np.arange(-T, T).astype(np.float32)
    f = (np.sign(r) * np.log1p(np.abs(r))).astype(np.float32)
    return c, np.concatenate([f, -f])[None, :].astype(np.float32)


def kernel(**inputs):
    import numpy as _np
    import concourse.bacc as _bacc
    from concourse import mybir as _mybir
    from concourse.bass_utils import run_bass_kernel_spmd as _run

    nc = _bacc.Bacc("TRN2", target_bir_lowering=False, num_devices=1)
    arrays, args = {}, []
    given = {name: inputs[name] for name in _INS}
    given["consts"], given["rel"] = _constants()
    for name, a in given.items():
        a = _np.ascontiguousarray(a)
        arrays[f"in_{name}_dram"] = a
        args.append(nc.dram_tensor(f"in_{name}_dram", a.shape, _mybir.dt.from_np(a.dtype), kind="ExternalInput").ap())
    shape = inputs["L0_attn_x"].shape
    args.append(nc.dram_tensor("out_0_dram", shape, _mybir.dt.float32, kind="ExternalOutput").ap())
    build(nc, *args)
    r = _run(nc, [arrays], core_ids=[0])
    return r.results[0]["out_0_dram"]
```
